# Optimizing a Trainium2 kernel written in Bass

```python
import numpy as np
import jax
import jax.numpy as jnp

def _softmax(x, axis=-1):
    return jax.nn.softmax(x, axis=axis)

def _gelu(x):
    return jax.nn.gelu(x, approximate=True)

def _silu(x):
    return jax.nn.silu(x)

def _sigmoid(x):
    return jax.nn.sigmoid(x)

def _layernorm(x, axis=-1, eps=1e-05):
    m = jnp.mean(x, axis=axis, keepdims=True)
    v = jnp.var(x, axis=axis, keepdims=True)
    return (x - m) / jnp.sqrt(v + eps)

def _scatter_add(tgt, idx, src, axis=0):
    return tgt.at[idx].add(src)

def _segment_sum(src, seg, n):
    return jax.ops.segment_sum(src, seg, n)
kernel_name = 'mk_gnn_resnorm_d2_gnn_r32_190757'

def setup_inputs(seed: int=0):
    np.random.seed(seed)
    _w = jnp.asarray

    def _rec_inputs():
        import jax
        import jax.numpy as jnp
        _gk = jax.random.key(seed)
        x = -0.0005121 + 1.001 * jax.random.normal(jax.random.fold_in(_gk, 1), (50000, 64), jnp.float32)
        src = jax.random.randint(jax.random.fold_in(_gk, 2), (50000,), 0, 50000, jnp.int32)
        dst = jnp.minimum((50000 * jax.random.uniform(jax.random.fold_in(_gk, 3), (50000,)) ** 2.0).astype(jnp.int32), 49999)
        _o = jnp.argsort(dst, stable=True)
        src = src[_o]
        dst = dst[_o]
        edge_attr_64 = -9.77346e-05 + 0.999888 * jax.random.normal(jax.random.fold_in(_gk, 12), (50000, 64), jnp.float32)
        return (x, src, dst, edge_attr_64)
    x, src, dst, edge_attr_64 = _rec_inputs()

    def _L0_gnn_setup():
        import jax, jax.numpy as jnp
        import numpy as np
        N, E, D, H, L = (50000, 25000, 64, 4, 2)
        DH = D // H

        def layer_norm(h, g, b, eps=1e-05):
            mu = h.mean(-1, keepdims=True)
            var = ((h - mu) ** 2).mean(-1, keepdims=True)
            return (h - mu) / jnp.sqrt(var + eps) * g + b

        def exphormer_layer(h, edge_attr, src, dst, p):
            wq, wk, we, wv, wo, bo, g1, be1, w1, b1, w2, b2, g2, be2 = p
            n = h.shape[0]
            Qh = (h @ wq).reshape(n, H, DH)
            Kh = (h @ wk).reshape(n, H, DH)
            Vh = (h @ wv).reshape(n, H, DH)
            Eh = (edge_attr @ we).reshape(-1, H, DH)
            s = jnp.sum(Kh[src] * Qh[dst] * Eh, axis=-1, keepdims=True) / np.sqrt(DH)
            score = jnp.exp(jnp.clip(s, -5.0, 5.0))
            msg = Vh[src] * score
            wV = jax.ops.segment_sum(msg, dst, num_segments=n)
            Z = jax.ops.segment_sum(score, dst, num_segments=n)
            h_attn = (wV / (Z + 1e-06)).reshape(n, D)
            h1 = layer_norm(h + (h_attn @ wo + bo), g1, be1)
            ffn = jax.nn.relu(h1 @ w1 + b1) @ w2 + b2
            return layer_norm(h1 + ffn, g2, be2)
        key = jax.random.key(seed)
        ks = jax.random.split(key, 16)
        s = 1.0 / np.sqrt(D)
        inp = {'x': jax.random.normal(ks[0], (N, D), jnp.float32), 'edge_attr': jax.random.normal(ks[1], (E, D), jnp.float32), 'edge_index': jax.random.randint(ks[2], (2, E), 0, N, jnp.int64), 'WQ': jax.random.normal(ks[3], (L, D, D), jnp.float32) * s, 'WK': jax.random.normal(ks[4], (L, D, D), jnp.float32) * s, 'WE': jax.random.normal(ks[5], (L, D, D), jnp.float32) * s, 'WV': jax.random.normal(ks[6], (L, D, D), jnp.float32) * s, 'WO': jax.random.normal(ks[7], (L, D, D), jnp.float32) * s, 'bO': jnp.zeros((L, D), jnp.float32), 'ln1_g': jnp.ones((L, D), jnp.float32), 'ln1_b': jnp.zeros((L, D), jnp.float32), 'W1': jax.random.normal(ks[8], (L, D, 2 * D), jnp.float32) * s, 'b1': jnp.zeros((L, 2 * D), jnp.float32), 'W2': jax.random.normal(ks[9], (L, 2 * D, D), jnp.float32) * (1.0 / np.sqrt(2 * D)), 'b2': jnp.zeros((L, D), jnp.float32), 'ln2_g': jnp.ones((L, D), jnp.float32), 'ln2_b': jnp.zeros((L, D), jnp.float32)}
        return inp
    _L0_gnn_all = _L0_gnn_setup()
    _L0_gnn_in = {k: v for k, v in _L0_gnn_all.items() if k in ('WQ', 'WK', 'WE', 'WV', 'WO', 'bO', 'ln1_g', 'ln1_b', 'W1', 'b1', 'W2', 'b2', 'ln2_g', 'ln2_b')}
    del _L0_gnn_all

    def _L1_gnn_setup():
        import jax, jax.numpy as jnp
        import numpy as np
        EPS = 1e-05

        def _bn(h, gamma, beta):
            mu = h.mean(axis=0)
            var = ((h - mu) ** 2).mean(axis=0)
            return (h - mu) * jax.lax.rsqrt(var + EPS) * gamma + beta

        def _mlp(h, W1, b1, g1, be1, W2, b2):
            h = h @ W1 + b1
            h = jax.nn.relu(_bn(h, g1, be1))
            return h @ W2 + b2
        key = jax.random.key(seed)
        ks = jax.random.split(key, 12)
        N, E = (50000, 25000)
        node_dim, edge_dim, hidden = (64, 64, 128)
        d_in1 = node_dim + edge_dim
        d_in2 = node_dim + hidden

        def lin(k, fi, fo):
            s = 1.0 / np.sqrt(fi)
            return jax.random.uniform(k, (fi, fo), jnp.float32, -s, s)
        inp = {'x': jax.random.normal(ks[0], (N, node_dim), jnp.float32), 'edge_index': jax.random.randint(ks[1], (2, E), 0, N, jnp.int32), 'edge_attr': jax.random.normal(ks[2], (E, edge_dim), jnp.float32), 'u': jax.random.normal(ks[3], (1, 16), jnp.float32), 'batch': jnp.zeros((N,), jnp.int32), 'W1a': lin(ks[4], d_in1, hidden), 'b1a': jnp.zeros((hidden,), jnp.float32), 'g1a': jnp.ones((hidden,), jnp.float32), 'be1a': jnp.zeros((hidden,), jnp.float32), 'W2a': lin(ks[5], hidden, hidden), 'b2a': jnp.zeros((hidden,), jnp.float32), 'W1b': lin(ks[6], d_in2, hidden), 'b1b': jnp.zeros((hidden,), jnp.float32), 'g1b': jnp.ones((hidden,), jnp.float32), 'be1b': jnp.zeros((hidden,), jnp.float32), 'W2b': lin(ks[7], hidden, node_dim), 'b2b': jnp.zeros((node_dim,), jnp.float32)}
        return inp
    _L1_gnn_all = _L1_gnn_setup()
    _L1_gnn_in = {k: v for k, v in _L1_gnn_all.items() if k in ('u', 'W1a', 'b1a', 'g1a', 'be1a', 'W2a', 'b2a', 'W1b', 'b1b', 'g1b', 'be1b', 'W2b', 'b2b')}
    del _L1_gnn_all
    return {'x': x, 'src': src, 'dst': dst, 'edge_attr_64': edge_attr_64, 'L0_gnn_WQ': _L0_gnn_in['WQ'], 'L0_gnn_WK': _L0_gnn_in['WK'], 'L0_gnn_WE': _L0_gnn_in['WE'], 'L0_gnn_WV': _L0_gnn_in['WV'], 'L0_gnn_WO': _L0_gnn_in['WO'], 'L0_gnn_bO': _L0_gnn_in['bO'], 'L0_gnn_ln1_g': _L0_gnn_in['ln1_g'], 'L0_gnn_ln1_b': _L0_gnn_in['ln1_b'], 'L0_gnn_W1': _L0_gnn_in['W1'], 'L0_gnn_b1': _L0_gnn_in['b1'], 'L0_gnn_W2': _L0_gnn_in['W2'], 'L0_gnn_b2': _L0_gnn_in['b2'], 'L0_gnn_ln2_g': _L0_gnn_in['ln2_g'], 'L0_gnn_ln2_b': _L0_gnn_in['ln2_b'], 'L1_gnn_u': _L1_gnn_in['u'], 'L1_gnn_W1a': _L1_gnn_in['W1a'], 'L1_gnn_b1a': _L1_gnn_in['b1a'], 'L1_gnn_g1a': _L1_gnn_in['g1a'], 'L1_gnn_be1a': _L1_gnn_in['be1a'], 'L1_gnn_W2a': _L1_gnn_in['W2a'], 'L1_gnn_b2a': _L1_gnn_in['b2a'], 'L1_gnn_W1b': _L1_gnn_in['W1b'], 'L1_gnn_b1b': _L1_gnn_in['b1b'], 'L1_gnn_g1b': _L1_gnn_in['g1b'], 'L1_gnn_be1b': _L1_gnn_in['be1b'], 'L1_gnn_W2b': _L1_gnn_in['W2b'], 'L1_gnn_b2b': _L1_gnn_in['b2b']}

def reference(x, src, dst, edge_attr_64, L0_gnn_WQ, L0_gnn_WK, L0_gnn_WE, L0_gnn_WV, L0_gnn_WO, L0_gnn_bO, L0_gnn_ln1_g, L0_gnn_ln1_b, L0_gnn_W1, L0_gnn_b1, L0_gnn_W2, L0_gnn_b2, L0_gnn_ln2_g, L0_gnn_ln2_b, L1_gnn_u, L1_gnn_W1a, L1_gnn_b1a, L1_gnn_g1a, L1_gnn_be1a, L1_gnn_W2a, L1_gnn_b2a, L1_gnn_W1b, L1_gnn_b1b, L1_gnn_g1b, L1_gnn_be1b, L1_gnn_W2b, L1_gnn_b2b):
    import jax
    import jax.numpy as jnp

    def _L0_gnn_ref(x, edge_attr, edge_index, WQ, WK, WE, WV, WO, bO, ln1_g, ln1_b, W1, b1, W2, b2, ln2_g, ln2_b):
        import jax, jax.numpy as jnp
        import numpy as np
        N, E, D, H, L = (50000, 25000, 64, 4, 2)
        DH = D // H

        def layer_norm(h, g, b, eps=1e-05):
            mu = h.mean(-1, keepdims=True)
            var = ((h - mu) ** 2).mean(-1, keepdims=True)
            return (h - mu) / jnp.sqrt(var + eps) * g + b

        def exphormer_layer(h, edge_attr, src, dst, p):
            wq, wk, we, wv, wo, bo, g1, be1, w1, b1, w2, b2, g2, be2 = p
            n = h.shape[0]
            Qh = (h @ wq).reshape(n, H, DH)
            Kh = (h @ wk).reshape(n, H, DH)
            Vh = (h @ wv).reshape(n, H, DH)
            Eh = (edge_attr @ we).reshape(-1, H, DH)
            s = jnp.sum(Kh[src] * Qh[dst] * Eh, axis=-1, keepdims=True) / np.sqrt(DH)
            score = jnp.exp(jnp.clip(s, -5.0, 5.0))
            msg = Vh[src] * score
            wV = jax.ops.segment_sum(msg, dst, num_segments=n)
            Z = jax.ops.segment_sum(score, dst, num_segments=n)
            h_attn = (wV / (Z + 1e-06)).reshape(n, D)
            h1 = layer_norm(h + (h_attn @ wo + bo), g1, be1)
            ffn = jax.nn.relu(h1 @ w1 + b1) @ w2 + b2
            return layer_norm(h1 + ffn, g2, be2)
        src = edge_index[0]
        dst = edge_index[1]
        h = x
        for l in range(L):
            p = (WQ[l], WK[l], WE[l], WV[l], WO[l], bO[l], ln1_g[l], ln1_b[l], W1[l], b1[l], W2[l], b2[l], ln2_g[l], ln2_b[l])
            h = exphormer_layer(h, edge_attr, src, dst, p)
        return h

    def _L1_gnn_ref(x, edge_index, edge_attr, u, batch, W1a, b1a, g1a, be1a, W2a, b2a, W1b, b1b, g1b, be1b, W2b, b2b):
        import jax, jax.numpy as jnp
        import numpy as np
        EPS = 1e-05

        def _bn(h, gamma, beta):
            mu = h.mean(axis=0)
            var = ((h - mu) ** 2).mean(axis=0)
            return (h - mu) * jax.lax.rsqrt(var + EPS) * gamma + beta

        def _mlp(h, W1, b1, g1, be1, W2, b2):
            h = h @ W1 + b1
            h = jax.nn.relu(_bn(h, g1, be1))
            return h @ W2 + b2
        row, col = (edge_index[0], edge_index[1])
        out = jnp.concatenate([x[row], edge_attr], axis=1)
        out = _mlp(out, W1a, b1a, g1a, be1a, W2a, b2a)
        out = jax.ops.segment_sum(out, col, num_segments=x.shape[0])
        out = jnp.concatenate([x, out], axis=1)
        return _mlp(out, W1b, b1b, g1b, be1b, W2b, b2b)
    edge_index = jnp.stack([src, dst])
    batch0 = jnp.zeros((50000,), jnp.int32)
    x = _layernorm(x + _L0_gnn_ref(x, edge_attr_64, edge_index, L0_gnn_WQ, L0_gnn_WK, L0_gnn_WE, L0_gnn_WV, L0_gnn_WO, L0_gnn_bO, L0_gnn_ln1_g, L0_gnn_ln1_b, L0_gnn_W1, L0_gnn_b1, L0_gnn_W2, L0_gnn_b2, L0_gnn_ln2_g, L0_gnn_ln2_b), axis=-1)
    x = _layernorm(x + _L1_gnn_ref(x, edge_index, edge_attr_64, L1_gnn_u, batch0, L1_gnn_W1a, L1_gnn_b1a, L1_gnn_g1a, L1_gnn_be1a, L1_gnn_W2a, L1_gnn_b2a, L1_gnn_W1b, L1_gnn_b1b, L1_gnn_g1b, L1_gnn_be1b, L1_gnn_W2b, L1_gnn_b2b), axis=-1)
    return x

_drawn_inputs = setup_inputs


def setup_inputs(seed=0):
    import zlib

    import numpy as np

    out = dict(_drawn_inputs(seed))
    spreads = {'L0_gnn_bO': (0.0, 0.1),
     'L0_gnn_ln1_g': (1.0, 0.2),
     'L0_gnn_ln1_b': (0.0, 0.1),
     'L0_gnn_b1': (0.0, 0.1),
     'L0_gnn_b2': (0.0, 0.1),
     'L0_gnn_ln2_g': (1.0, 0.2),
     'L0_gnn_ln2_b': (0.0, 0.1),
     'L1_gnn_b1a': (0.0, 0.8),
     'L1_gnn_g1a': (1.0, 0.2),
     'L1_gnn_be1a': (0.0, 0.429),
     'L1_gnn_b2a': (0.0, 0.1),
     'L1_gnn_b1b': (0.0, 0.8),
     'L1_gnn_g1b': (1.0, 0.2),
     'L1_gnn_be1b': (0.0, 0.1),
     'L1_gnn_b2b': (0.0, 0.1)}
    factors = {}
    for name, (base, spread) in spreads.items():
        noise = np.random.default_rng([zlib.crc32(name.encode()), seed]).standard_normal(out[name].shape)
        drawn = base * np.exp(spread * noise) if base else spread * noise
        out[name] = jnp.asarray(drawn.astype(out[name].dtype))
    for name, factor in factors.items():
        out[name] = (out[name] * factor).astype(out[name].dtype)
    return out
```

```python
from contextlib import ExitStack

import numpy as np

import concourse.bass as bass
from concourse import mybir

P = 128
D = 64
HEADS = 4
DH = D // HEADS
HID = 2 * D
LAYERS = 2
MSG = D + HEADS
TPG = 8
TPH = TPG // 2
ROWS = TPG * P
HROWS = TPH * P
TABLES = 2
EPS_LN = 1e-5
EPS_BN = 1e-5
EPS_Z = 1e-6
CLIP = 5.0 * DH ** 0.5

ALU = mybir.AluOpType
ACT = mybir.ActivationFunctionType
AX = mybir.AxisListType
F32 = mybir.dt.float32
I32 = mybir.dt.int32

CONSTS = dict(ident=(0, P), center=(P, P), average=(2 * P, P), earlier=(3 * P, P), spare=(4 * P, 1))
N_CONSTS = 4 * P + 1
LAYER_W = dict(kvq=(0, 3 * D), e=(3 * D, D), wo_t=(256, P), w1_lo=(384, P), w1_hi=(512, P),
               w2_t_lo=(640, P), w2_t_hi=(768, P))
N_LAYER_W = 896
LAYER_B = ("bo", "g1", "be1", "b1", "b2", "g2", "be2")
MLP_W = dict(w1a=(0, P), w2a=(P, P), w1b_x_lo=(2 * P, P), w1b_x_hi=(3 * P, P), w1b_agg=(4 * P, P), w2b=(5 * P, D))
N_MLP_W = 5 * P + D
MLP_B = ("b1a", "g1a", "be1a", "b1b", "g1b", "be1b")


def row_of(ap, p=P):
    return ap.partition_broadcast(p)


def build(nc, n_nodes, n_edges, x, ea_t, gather_idx, dst_row, dst_col, consts, layer_w, layer_b, mlp_w, mlp_b,
          mlp_rows, out):
    groups_n = x.shape[0] // ROWS
    groups_e = ea_t.shape[1] // ROWS
    n_pad = groups_n * ROWS
    table_rows = n_pad + P
    pairs = groups_n // 2
    odd = groups_n % 2

    h_mid = nc.dram_tensor("h_mid", [n_pad, D], F32, kind="Internal").ap()
    x_mid = nc.dram_tensor("x_mid", [n_pad, D], F32, kind="Internal").ap()
    attn_sums = [nc.dram_tensor(f"attn_sums{l}", [table_rows, MSG], F32, kind="Internal").ap() for l in range(LAYERS)]
    mlp_sums = [nc.dram_tensor(f"mlp_sums{t}", [table_rows, HID], F32, kind="Internal").ap() for t in range(TABLES)]
    edge_hid = nc.dram_tensor("edge_hid", [2 * groups_e, P, HROWS], F32, kind="Internal").ap()
    node_hid = nc.dram_tensor("node_hid", [groups_n, P, ROWS], F32, kind="Internal").ap()

    x_g = x.rearrange("(g p j) d -> g p (j d)", p=P, j=TPG)
    h_mid_g = h_mid.rearrange("(g p j) d -> g p (j d)", p=P, j=TPG)
    x_mid_g = x_mid.rearrange("(g p j) d -> g p (j d)", p=P, j=TPG)
    out_g = out.rearrange("(g p j) d -> g p (j d)", p=P, j=TPG)
    attn_sums_g = [t[0:n_pad, :].rearrange("(g p j) d -> g p (j d)", p=P, j=TPG) for t in attn_sums]
    mlp_sums_g = [t[0:n_pad, :].rearrange("(g p j) d -> g p (j d)", p=P, j=TPG) for t in mlp_sums]
    ea_t_h = ea_t.rearrange("d (h c) -> h d c", c=HROWS)

    with ExitStack() as top:
        def sb(name, shape, dt=F32, ctx=top):
            return ctx.enter_context(nc.sbuf_tensor(name, shape, dt))

        def sem(name):
            return top.enter_context(nc.semaphore(name))

        def sems(name):
            return [sem(f"{name}{q}") for q in range(2)]

        cst = sb("cst", [P, N_CONSTS])
        lw = sb("lw", [P, LAYERS, N_LAYER_W])
        lb = sb("lb", [P, LAYERS, len(LAYER_B)])
        mw = sb("mw", [P, N_MLP_W])
        mb = sb("mb", [P, len(MLP_B)])
        b2a_rows = sb("b2a_rows", [P, HID])
        b2b_rows = sb("b2b_rows", [P, D])
        eps_col = sb("eps_col", [P, 1])
        centered = sb("centered", [P, LAYERS, 3, P])
        centered_b = sb("centered_b", [P, LAYERS, 2])
        scatter_all = sb("scatter_all", [P, groups_e * TPG], I32)
        edge_affine = sb("edge_affine", [P, 8])
        node_affine = sb("node_affine", [P, 8])

        def const(name):
            a, n = CONSTS[name]
            return cst[:, a:a + n]

        def layer(l, name):
            a, n = LAYER_W[name]
            return lw[:, l, a:a + n]

        def layer_bias(l, name):
            k = LAYER_B.index(name)
            return lb[:, l, k:k + 1]

        def mlp(name):
            a, n = MLP_W[name]
            return mw[:, a:a + n]

        def mlp_bias(name):
            k = MLP_B.index(name)
            return mb[:, k:k + 1]

        ident = const("ident")
        center = const("center")
        average = const("average")

        setup_loaded, zeros_set = sem("setup_loaded"), sem("zeros_set")
        tables_zero = sem("tables_zero")
        weights_centered, weights_copied = sem("weights_centered"), sem("weights_copied")
        n_setup = 7
        with ExitStack() as ctx:
            z_cols = table_rows // P * 4
            zeros = sb("zeros", [P, z_cols], ctx=ctx)
            ps_w = [ctx.enter_context(nc.psum_tensor(f"ps_w{k}", [P, 512], F32)) for k in range(LAYERS)]
            block = ctx.enter_context(nc.Block())

            @block.sync
            def _(sp):
                for dst, src in ((cst[:], consts), (lw[:], layer_w), (lb[:], layer_b), (mw[:], mlp_w), (mb[:], mlp_b),
                                 (b2a_rows[:], row_of(mlp_rows[0, :])),
                                 (b2b_rows[:], row_of(mlp_rows[1, 0:D]))):
                    sp.dma_start(dst, src).then_inc(setup_loaded, 16)
                sp.wait_ge(zeros_set, 1)
                n = 0
                for table in (*attn_sums, *mlp_sums):
                    flat = table.rearrange("(p r) d -> p (r d)", p=P)
                    for c in range(0, flat.shape[1], z_cols):
                        sp.dma_start(flat[:, c:c + z_cols], zeros[:]).then_inc(tables_zero, 16)
                        n += 1
                sp.wait_ge(tables_zero, 16 * n)

            @block.vector
            def _(dve):
                nc.vector.memset(eps_col[:], EPS_LN)
                nc.vector.memset(zeros[:], 0.0).then_inc(zeros_set, 1)
                dve.wait_ge(weights_centered, 1)
                for l in range(LAYERS):
                    nc.vector.tensor_copy(centered[:, l, :, :], ps_w[l][:, 0:3 * P].rearrange("p (k c) -> p k c", c=P))
                    nc.vector.tensor_copy(centered_b[:, l, :], ps_w[l][:, 3 * P:3 * P + 2]).then_inc(weights_copied, 1)
                dve.wait_ge(weights_copied, LAYERS)

            @block.tensor
            def _(pe):
                pe.wait_ge(setup_loaded, 16 * n_setup)
                for l in range(LAYERS):
                    for k, name in enumerate(("wo_t", "w2_t_lo", "w2_t_hi")):
                        nc.tensor.matmul(ps_w[l][:, k * P:(k + 1) * P], layer(l, name), center, start=True, stop=True)
                    for k, name in enumerate(("bo", "b2")):
                        last = nc.tensor.matmul(ps_w[l][:, 3 * P + k:3 * P + k + 1], center, layer_bias(l, name),
                                                start=True, stop=True)
                last.then_inc(weights_centered, 1)

        idx_loaded, gathered, edge_loaded = sems("idx_loaded"), sems("gathered"), sems("edge_loaded")
        pair_t, pair_t_copied = sems("pair_t"), sems("pair_t_copied")
        kvqe_ready, qe_copied = sems("kvqe_ready"), sem("qe_copied")
        same_ready, writer_step = sems("same_ready"), sem("writer_step")
        scatter_idx_ready = sems("scatter_idx_ready")
        kq_ready, kqe_ready, dot_ready, clipped = sem("kq_ready"), sems("kqe_ready"), sem("dot_ready"), sem("clipped")
        exp_ready, msg_ready = sems("exp_ready"), sems("msg_ready")
        sums_ready, sums_copied, scattered = sems("sums_ready"), sems("sums_copied"), sems("scattered")

        def attention(l):
            nodes = (x, h_mid)[l]
            with ExitStack() as ctx:
                def buf(name, shape, dt=F32):
                    return [sb(f"{name}_{l}{q}", shape, dt, ctx) for q in range(2)]

                idx = buf("idx", [P, 2 * TPH], I32)
                pair = buf("pair", [P, TPH, 2 * D])
                pairT = buf("pairT", [P, HROWS])
                ea = buf("ea", [D, HROWS])
                drow = buf("drow", [P, TPH, P], I32)
                dcol = buf("dcol", [P, TPH], I32)
                same = buf("same", [P, TPH, P])
                earlier = buf("earlier", [P, TPH, P])
                count = buf("count", [P, TPH])
                offset = buf("offset", [P, TPH])
                masked = buf("masked", [P, TPH])
                sidx = buf("sidx", [P, TPH], I32)
                qe = buf("qe", [P, TPH, 2 * D])
                kq = buf("kq", [P, TPH * D])
                kqe = buf("kqe", [P, TPH * D])
                dot = buf("dot", [P, TPH * HEADS])
                dotc = buf("dotc", [P, TPH * HEADS])
                msg = buf("msg", [P, TPH, MSG])
                sums = buf("sums", [P, TPH, MSG])
                ps_t = [ctx.enter_context(nc.psum_tensor(f"ps_t_{l}{q}", [P, HROWS], F32)) for q in range(2)]
                ps_kvqe = [ctx.enter_context(nc.psum_tensor(f"ps_kvqe_{l}{q}", [P, TPH, 4 * D], F32)) for q in range(2)]
                ps_s = [ctx.enter_context(nc.psum_tensor(f"ps_s_{l}{q}", [P, 512], F32)) for q in range(2)]
                base = l * groups_e

                def nth(i, q):
                    return i * 2 + (2 * base + q + 1)

                block = ctx.enter_context(nc.Block())

                @block.sync
                def _(sp):
                    with sp.Fori(0, groups_e) as i:
                        for q in range(2):
                            sp.wait_ge(gathered[q], (i + base) * (2 * TPH * 16))
                            sp.dma_start(idx[q][:], gather_idx[bass.ds(i * 2 + q, 1)].rearrange("a p c -> p (a c)")
                                         ).then_inc(idx_loaded[q], 16)
                            sp.wait_ge(kvqe_ready[q], i + base)
                            sp.dma_start(ea[q][:], ea_t_h[bass.ds(i * 2 + q, 1)].rearrange("a p c -> p (a c)")
                                         ).then_inc(edge_loaded[q], 16)
                            if l == 0:
                                sp.wait_ge(scatter_idx_ready[q], i + base)
                            sp.wait_ge(same_ready[q], i + base)
                            sp.dma_start(dcol[q][:], dst_col[bass.ds(i * 2 + q, 1)].rearrange("a p c -> p (a c)")
                                         ).then_inc(edge_loaded[q], 16)
                            sp.dma_start(drow[q][:], dst_row[bass.ds(i * 2 + q, 1), :].rearrange("a c -> (a c)")
                                         .partition_broadcast(P)).then_inc(edge_loaded[q], 16)

                @block.gpsimd
                def _(pool):
                    def gather(i, q, k):
                        if k == 0:
                            pool.wait_ge(idx_loaded[q], (i + 1) * 16)
                            pool.wait_ge(pair_t[q], i)
                            pool.nop(nofuse=True)
                        for side in range(2):
                            nc.gpsimd.indirect_dma_start(
                                pair[q][:, k, side * D:(side + 1) * D], None, nodes,
                                bass.IndirectOffsetOnAxis(ap=idx[q][:, side * TPH + k:side * TPH + k + 1], axis=0)
                            ).then_inc(gathered[q], 16)

                    def scatter(i, q, k):
                        if k == 0:
                            pool.wait_ge(sums_copied[q], i + 1)
                            pool.wait_ge(scatter_idx_ready[q], i + 1)
                            pool.wait_ge(scattered[1 - q], (i + q) * (TPH * 16))
                        else:
                            pool.wait_ge(scattered[q], i * (TPH * 16) + 16 * k)
                        pool.nop(nofuse=True)
                        nc.gpsimd.indirect_dma_start(
                            attn_sums[l], bass.IndirectOffsetOnAxis(ap=sidx[q][:, k:k + 1], axis=0),
                            sums[q][:, k, :], None, compute_op=ALU.add).then_inc(scattered[q], 16)

                    for q in range(2):
                        for k in range(TPH):
                            gather(base, q, k)
                    with pool.Fori(0, groups_e - 1) as i:
                        for q in range(2):
                            for k in range(TPH):
                                scatter(i + base, q, k)
                                gather(i + (base + 1), q, k)
                    for q in range(2):
                        for k in range(TPH):
                            scatter(base + groups_e - 1, q, k)
                    for q in range(2):
                        pool.wait_ge(scattered[q], (base + groups_e) * TPH * 16)

                @block.tensor
                def _(pe):
                    with pe.Fori(0, groups_e) as i:
                        for q in range(2):
                            pe.wait_ge(gathered[q], (i + (base + 1)) * (2 * TPH * 16))
                            pe.wait_ge(pair_t_copied[q], i + base)
                            for k in range(TPH):
                                last = nc.tensor.transpose(ps_t[q][:, k * P:(k + 1) * P], pair[q][:, k, :], ident)
                            last.then_inc(pair_t[q], 1)
                            pe.wait_ge(pair_t_copied[q], i + (base + 1))
                            pe.wait_ge(edge_loaded[q], (i + (base + 1)) * 48)
                            pe.wait_ge(msg_ready[q], i + base)
                            for k in range(TPH):
                                nc.tensor.matmul(ps_kvqe[q][:, k, 0:3 * D], pairT[q][:, k * P:(k + 1) * P],
                                                 layer(l, "kvq"), start=True, stop=True)
                                last = nc.tensor.matmul(ps_kvqe[q][:, k, 3 * D:4 * D], ea[q][:, k * P:(k + 1) * P],
                                                        layer(l, "e")[0:D, :], start=True, stop=True)
                            last.then_inc(kvqe_ready[q], 1)
                            pe.wait_ge(same_ready[q], i + (base + 1))
                            pe.wait_ge(msg_ready[q], i + (base + 1))
                            pe.wait_ge(sums_copied[q], i + base)
                            for k in range(TPH):
                                last = nc.tensor.matmul(ps_s[q][:, k * MSG:(k + 1) * MSG], same[q][:, k, :],
                                                        msg[q][:, k, :], start=True, stop=True)
                            last.then_inc(sums_ready[q], 1)

                @block.scalar
                def _(act):
                    with act.Fori(0, groups_e) as i:
                        for q in range(2):
                            act.wait_ge(pair_t[q], i + (base + 1))
                            act.wait_ge(kvqe_ready[q], i + base)
                            nc.scalar.activation(pairT[q][:], ps_t[q][:], ACT.Copy).then_inc(pair_t_copied[q], 1)
                            act.wait_ge(kvqe_ready[q], i + (base + 1))
                            act.wait_ge(kqe_ready[q], i + base)
                            nc.scalar.activation(qe[q][:], ps_kvqe[q][:, :, 2 * D:4 * D], ACT.Copy
                                                 ).then_inc(qe_copied, 1)
                            act.wait_ge(clipped, nth(i, q))
                            act.wait_ge(sums_ready[q], i + base)
                            nc.scalar.activation(msg[q][:, :, D:MSG],
                                                 dotc[q][:].rearrange("p (k h) -> p k h", h=HEADS),
                                                 ACT.Exp, scale=DH ** -0.5).then_inc(exp_ready[q], 1)
                            act.wait_ge(sums_ready[q], i + (base + 1))
                            act.wait_ge(scattered[q], (i + base) * (TPH * 16))
                            nc.scalar.activation(sums[q][:], ps_s[q][:, 0:TPH * MSG].rearrange(
                                "p (k c) -> p k c", c=MSG), ACT.Copy).then_inc(sums_copied[q], 1)

                @block.vector
                def _(dve):
                    with dve.Fori(0, groups_e) as i:
                        for q in range(2):
                            dve.wait_ge(edge_loaded[q], (i + (base + 1)) * 48)
                            dve.wait_ge(sums_ready[q], i + base)
                            nc.vector.tensor_tensor(same[q][:], drow[q][:],
                                                    dcol[q][:].unsqueeze(2).broadcast_to([P, TPH, P]),
                                                    ALU.is_equal).then_inc(same_ready[q], 1)
                            if l == 0:
                                dve.wait_ge(same_ready[q], i + 1)
                                nc.vector.tensor_tensor(earlier[q][:], same[q][:],
                                                        const("earlier").unsqueeze(1).broadcast_to([P, TPH, P]),
                                                        ALU.mult).then_inc(writer_step, 1)
                                nc.vector.tensor_scalar(offset[q][:], dcol[q][:], const("spare"), None,
                                                        ALU.subtract).then_inc(writer_step, 1)
                                dve.wait_ge(writer_step, i * 8 + (4 * q + 2))
                                nc.vector.tensor_reduce(count[q][:], earlier[q][:], AX.X, ALU.add
                                                        ).then_inc(writer_step, 1)
                                dve.wait_ge(writer_step, i * 8 + (4 * q + 3))
                                nc.vector.scalar_tensor_tensor(masked[q][:], count[q][:], 0.0, offset[q][:],
                                                               ALU.is_equal, ALU.mult).then_inc(writer_step, 1)
                                dve.wait_ge(writer_step, i * 8 + (4 * q + 4))
                                nc.vector.tensor_scalar(scatter_all[:, bass.ds(i * TPG + q * TPH, TPH)], masked[q][:],
                                                        const("spare"), None, ALU.add)
                                dve.wait_ge(scattered[q], i * (TPH * 16))
                                nc.vector.tensor_scalar(sidx[q][:], masked[q][:], const("spare"), None, ALU.add
                                                        ).then_inc(scatter_idx_ready[q], 1)
                            else:
                                dve.wait_ge(scattered[q], (i + base) * (TPH * 16))
                                nc.vector.tensor_copy(sidx[q][:], scatter_all[:, bass.ds(i * TPG + q * TPH, TPH)]
                                                      ).then_inc(scatter_idx_ready[q], 1)
                            dve.wait_ge(qe_copied, nth(i, q))
                            nc.vector.tensor_tensor(kq[q][:].rearrange("p (k c) -> p k c", c=D),
                                                    ps_kvqe[q][:, :, 0:D], qe[q][:, :, 0:D], ALU.mult
                                                    ).then_inc(kq_ready, 1)
                            dve.wait_ge(kq_ready, nth(i, q))
                            nc.vector.tensor_tensor(kqe[q][:].rearrange("p (k c) -> p k c", c=D),
                                                    kq[q][:].rearrange("p (k c) -> p k c", c=D),
                                                    qe[q][:, :, D:2 * D], ALU.mult).then_inc(kqe_ready[q], 1)
                            dve.wait_ge(kqe_ready[q], i + (base + 1))
                            nc.vector.tensor_reduce(dot[q][:], kqe[q][:].rearrange("p (a c) -> p a c", c=DH), AX.X,
                                                    ALU.add).then_inc(dot_ready, 1)
                            dve.wait_ge(dot_ready, nth(i, q))
                            dve.wait_ge(exp_ready[q], i + base)
                            nc.vector.tensor_scalar(dotc[q][:], dot[q][:], CLIP, -CLIP, ALU.min, ALU.max
                                                    ).then_inc(clipped, 1)
                            dve.wait_ge(exp_ready[q], i + (base + 1))
                            nc.vector.tensor_tensor(
                                msg[q][:, :, 0:D].rearrange("p k (h c) -> p k h c", c=DH),
                                ps_kvqe[q][:, :, D:2 * D].rearrange("p k (h c) -> p k h c", c=DH),
                                msg[q][:, :, D:MSG].unsqueeze(3).broadcast_to([P, TPH, HEADS, DH]),
                                ALU.mult).then_inc(msg_ready[q], 1)

        node_loaded, z_ready, rz_ready, attn_ready = sems("node_loaded"), sem("z_ready"), sem("rz_ready"), sems("attn_ready")
        h_t, a_t, h_t_copied, a_t_copied = sems("h_t"), sem("a_t"), sem("h_t_copied"), sem("a_t_copied")
        c_ready = [sem(f"c{k}_ready") for k in range(3)]
        sq_ready = [sem(f"sq{k}_ready") for k in range(3)]
        var_ready = [sem(f"var{k}_ready") for k in range(3)]
        std_ready = [sem(f"std{k}_ready") for k in range(3)]
        rstd_ready = [sem(f"rstd{k}_ready") for k in range(3)]
        norm_ready = [sem(f"norm{k}_ready") for k in range(3)]
        h_ready = [sem(f"h{k}_ready") for k in range(2)]
        hid_ready, hid_lo_copied, hid_hi_copied = sem("hid_ready"), sem("hid_lo_copied"), sem("hid_hi_copied")
        x_t, x_t_copied = sems("x_t"), sem("x_t_copied")
        rows_t, rows_copied, rows_stored = sem("rows_t"), sems("rows_copied"), sems("rows_stored")

        def nodes(l):
            last_layer = l == LAYERS - 1
            source = (x_g, h_mid_g)[l]
            target = (h_mid_g, x_mid_g)[l]
            base = [l * (pairs + odd), l * pairs]
            with ExitStack() as ctx:
                def buf(name, shape):
                    return [sb(f"{name}_n{l}{q}", shape, ctx=ctx) for q in range(2)]

                acc = buf("acc", [P, TPG, MSG])
                hrow = buf("hrow", [P, TPG * D])
                xrow = buf("xrow", [P, TPG * D])
                z = buf("z", [P, TPG, HEADS])
                rz = buf("rz", [P, TPG, HEADS])
                attn = buf("attn", [P, TPG, D])
                hT, aT, xT = buf("hT", [P, HROWS]), buf("aT", [P, HROWS]), buf("xT", [P, HROWS])
                sq, std, rstd = buf("sq", [P, HROWS]), buf("std", [P, HROWS]), buf("rstd", [P, HROWS])
                norm = buf("norm", [P, HROWS])
                h1T, h2T = buf("h1T", [P, HROWS]), buf("h2T", [P, HROWS])
                hid_lo, hid_hi = buf("hid_lo", [P, HROWS]), buf("hid_hi", [P, HROWS])
                rows = buf("rows", [P, TPG * D])
                ps = [[ctx.enter_context(nc.psum_tensor(f"ps_n{l}{q}{b}", [P, HROWS], F32)) for b in range(4)]
                      for q in range(2)]
                loads = 3 if last_layer else 2
                block = ctx.enter_context(nc.Block())

                def over_groups(eng, stages):
                    with eng.Fori(0, pairs) as i:
                        for stage in stages:
                            for q in range(2):
                                stage(i * 2 + q, i + base[q], q)
                    if odd:
                        for stage in stages:
                            stage(2 * pairs, pairs + base[0], 0)

                def nth(g, k=0):
                    return g + (1 + (l * groups_n if k < 2 else 0))

                @block.sync
                def _(sp):
                    def load(g, n, q):
                        sp.wait_ge(attn_ready[q], n)
                        sp.dma_start(acc[q][:], attn_sums_g[l][bass.ds(g, 1)].rearrange("a p c -> p (a c)")
                                     ).then_inc(node_loaded[q], 16)
                        sp.wait_ge(h_t[q], n)
                        sp.dma_start(hrow[q][:], source[bass.ds(g, 1)].rearrange("a p c -> p (a c)")
                                     ).then_inc(node_loaded[q], 16)
                        if last_layer:
                            sp.wait_ge(x_t[q], n - base[q])
                            sp.dma_start(xrow[q][:], x_g[bass.ds(g, 1)].rearrange("a p c -> p (a c)")
                                         ).then_inc(node_loaded[q], 16)

                    over_groups(sp, [load])

                def loaded(n, q):
                    return (n + 1 - base[q]) * (16 * loads) + base[q] * 32

                @block.gpsimd
                def _(pool):
                    def store(g, n, q):
                        pool.wait_ge(rows_copied[q], n + 1)
                        pool.nop(nofuse=True)
                        pool.dma_start(target[bass.ds(g, 1)].rearrange("a p c -> p (a c)"), rows[q][:]
                                       ).then_inc(rows_stored[q], 16)

                    over_groups(pool, [store])
                    pool.wait_ge(rows_stored[0], 16 * (base[0] + pairs + odd))
                    pool.wait_ge(rows_stored[1], 16 * (base[1] + pairs))

                @block.tensor
                def _(pe):
                    def turn(dst, src):
                        for m in range(TPH):
                            last = nc.tensor.transpose(dst[:, m * P:(m + 1) * P], src[:, m * P:(m + 1) * P], ident)
                        return last

                    def turns(g, n, q):
                        pe.wait_ge(node_loaded[q], loaded(n, q))
                        pe.wait_ge(rows_copied[q], n)
                        turn(ps[q][0], hrow[q][:]).then_inc(h_t[q], 1)

                    def turns_attn(g, n, q):
                        pe.wait_ge(attn_ready[q], n + 1)
                        turn(ps[q][1], attn[q][:].rearrange("p k c -> p (k c)")).then_inc(a_t, 1)

                    def center1(g, n, q):
                        pe.wait_ge(h_t_copied, nth(g))
                        nc.tensor.matmul(ps[q][2][:], center, hT[q][:], start=True, stop=False)
                        pe.wait_ge(a_t_copied, nth(g))
                        nc.tensor.matmul(ps[q][2][:], centered[:, l, 0, :], aT[q][:], start=False, stop=True
                                         ).then_inc(c_ready[0], 1)

                    def variance(k):
                        def stage(g, n, q):
                            pe.wait_ge(sq_ready[k], nth(g, k))
                            nc.tensor.matmul(ps[q][3][:], average, sq[q][:], start=True, stop=True
                                             ).then_inc(var_ready[k], 1)
                        return stage

                    def hidden(g, n, q):
                        pe.wait_ge(h_ready[0], nth(g))
                        nc.tensor.matmul(ps[q][0][:], layer(l, "w1_lo"), h1T[q][:], start=True, stop=True)
                        nc.tensor.matmul(ps[q][1][:], layer(l, "w1_hi"), h1T[q][:], start=True, stop=True
                                         ).then_inc(hid_ready, 1)

                    def center2(g, n, q):
                        nc.tensor.matmul(ps[q][2][:], center, h1T[q][:], start=True, stop=False)
                        pe.wait_ge(hid_lo_copied, nth(g))
                        nc.tensor.matmul(ps[q][2][:], centered[:, l, 1, :], hid_lo[q][:], start=False, stop=False)
                        pe.wait_ge(hid_hi_copied, nth(g))
                        nc.tensor.matmul(ps[q][2][:], centered[:, l, 2, :], hid_hi[q][:], start=False, stop=True
                                         ).then_inc(c_ready[1], 1)

                    def turns_x(g, n, q):
                        turn(ps[q][1], xrow[q][:]).then_inc(x_t[q], 1)

                    def center3(g, n, q):
                        pe.wait_ge(x_t_copied, g + 1)
                        pe.wait_ge(h_ready[1], nth(g))
                        nc.tensor.matmul(ps[q][2][:], center, xT[q][:], start=True, stop=False)
                        nc.tensor.matmul(ps[q][2][:], center, h2T[q][:], start=False, stop=True
                                         ).then_inc(c_ready[2], 1)

                    def turns_out(g, n, q):
                        if last_layer:
                            pe.wait_ge(norm_ready[2], g + 1)
                            turn(ps[q][0], norm[q][:]).then_inc(rows_t, 1)
                        else:
                            pe.wait_ge(h_ready[1], nth(g))
                            turn(ps[q][0], h2T[q][:]).then_inc(rows_t, 1)

                    stages = [turns, turns_attn, center1, variance(0), hidden, center2]
                    if last_layer:
                        stages += [turns_x, variance(1), center3, variance(2), turns_out]
                    else:
                        stages += [variance(1), turns_out]
                    over_groups(pe, stages)

                @block.scalar
                def _(act):
                    def copy_h(g, n, q):
                        act.wait_ge(h_t[q], n + 1)
                        nc.scalar.activation(hT[q][:], ps[q][0][:], ACT.Copy).then_inc(h_t_copied, 1)

                    def square(k):
                        def stage(g, n, q):
                            act.wait_ge(c_ready[k], nth(g, k))
                            if k < 2:
                                ins = nc.scalar.activation(sq[q][:], ps[q][2][:], ACT.Square,
                                                           bias=centered_b[:, l, k:k + 1])
                            else:
                                ins = nc.scalar.activation(sq[q][:], ps[q][2][:], ACT.Square)
                            ins.then_inc(sq_ready[k], 1)
                        return stage

                    def deviation(k):
                        def stage(g, n, q):
                            act.wait_ge(var_ready[k], nth(g, k))
                            nc.scalar.activation(std[q][:], ps[q][3][:], ACT.Sqrt, bias=eps_col[:, 0:1]
                                                 ).then_inc(std_ready[k], 1)
                        return stage

                    def relu_lo(g, n, q):
                        act.wait_ge(hid_ready, nth(g))
                        nc.scalar.activation(hid_lo[q][:], ps[q][0][:], ACT.Relu, bias=layer_bias(l, "b1")
                                             ).then_inc(hid_lo_copied, 1)

                    def copy_x(g, n, q):
                        act.wait_ge(x_t[q], n + 1 - base[q])
                        nc.scalar.activation(xT[q][:], ps[q][1][:], ACT.Copy).then_inc(x_t_copied, 1)

                    def copy_rows(g, n, q):
                        act.wait_ge(rows_t, nth(g))
                        act.wait_ge(rows_stored[q], n * 16)
                        nc.scalar.activation(rows[q][:], ps[q][0][:], ACT.Copy).then_inc(rows_copied[q], 1)

                    stages = [copy_h, square(0), deviation(0), relu_lo, square(1)]
                    if last_layer:
                        stages += [copy_x, deviation(1), square(2), deviation(2), copy_rows]
                    else:
                        stages += [deviation(1), copy_rows]
                    over_groups(act, stages)

                @block.vector
                def _(dve):
                    def attention_rows(g, n, q):
                        dve.wait_ge(node_loaded[q], loaded(n, q))
                        nc.vector.tensor_scalar(z[q][:], acc[q][:, :, D:MSG], EPS_Z, None, ALU.add
                                                ).then_inc(z_ready, 1)
                        dve.wait_ge(z_ready, nth(g))
                        nc.vector.reciprocal(rz[q][:], z[q][:]).then_inc(rz_ready, 1)
                        dve.wait_ge(rz_ready, nth(g))
                        nc.vector.tensor_tensor(attn[q][:].rearrange("p k (h c) -> p k h c", c=DH),
                                                acc[q][:, :, 0:D].rearrange("p k (h c) -> p k h c", c=DH),
                                                rz[q][:].unsqueeze(3).broadcast_to([P, TPG, HEADS, DH]),
                                                ALU.mult).then_inc(attn_ready[q], 1)

                    def copy_a(g, n, q):
                        dve.wait_ge(a_t, nth(g))
                        nc.vector.tensor_copy(aT[q][:], ps[q][1][:]).then_inc(a_t_copied, 1)

                    def normed(k):
                        def stage(g, n, q):
                            dve.wait_ge(std_ready[k], nth(g, k))
                            nc.vector.reciprocal(rstd[q][:], std[q][:]).then_inc(rstd_ready[k], 1)
                            dve.wait_ge(rstd_ready[k], nth(g, k))
                            if k == 2:
                                nc.vector.tensor_tensor(norm[q][:], ps[q][2][:], rstd[q][:], ALU.mult
                                                        ).then_inc(norm_ready[k], 1)
                                return
                            nc.vector.scalar_tensor_tensor(norm[q][:], ps[q][2][:], centered_b[:, l, k:k + 1],
                                                           rstd[q][:], ALU.add, ALU.mult).then_inc(norm_ready[k], 1)
                            dve.wait_ge(norm_ready[k], nth(g, k))
                            nc.vector.tensor_scalar((h1T, h2T)[k][q][:], norm[q][:],
                                                    layer_bias(l, ("g1", "g2")[k]), layer_bias(l, ("be1", "be2")[k]),
                                                    ALU.mult, ALU.add).then_inc(h_ready[k], 1)
                        return stage

                    def relu_hi(g, n, q):
                        dve.wait_ge(hid_ready, nth(g))
                        nc.vector.tensor_scalar(hid_hi[q][:], ps[q][1][:], layer_bias(l, "b1"), 0.0, ALU.add, ALU.max
                                                ).then_inc(hid_hi_copied, 1)

                    stages = [attention_rows, copy_a, normed(0), relu_hi, normed(1)]
                    if last_layer:
                        stages += [normed(2)]
                    over_groups(dve, stages)

        for l in range(LAYERS):
            attention(l)
            nodes(l)

        ea_loaded = sems("ea_loaded")
        s_t, s_t_copied, eh_ready = sems("s_t"), sems("s_t_copied"), sems("eh_ready")
        eh_copied, eh_stats, eh_stored = sems("eh_copied"), sems("eh_stats"), sems("eh_stored")
        affine_step = sem("affine_step")
        loads_before = LAYERS * groups_e * 16
        gathers_before = LAYERS * groups_e * 2 * TPH * 16

        def bn_affine(dve, act, stats, affine, step, g, be):
            if dve is not None:
                nc.vector.bn_aggr(affine[:, 0:2], stats[:]).then_inc(affine_step, 1)
                dve.wait_ge(affine_step, step + 2)
                nc.vector.reciprocal(affine[:, 3:4], affine[:, 2:3]).then_inc(affine_step, 1)
                dve.wait_ge(affine_step, step + 3)
                nc.vector.tensor_tensor(affine[:, 4:5], affine[:, 3:4], mlp_bias(g), ALU.mult).then_inc(affine_step, 1)
                dve.wait_ge(affine_step, step + 4)
                nc.vector.tensor_tensor(affine[:, 6:7], affine[:, 0:1], affine[:, 4:5], ALU.mult
                                        ).then_inc(affine_step, 1)
                dve.wait_ge(affine_step, step + 5)
                nc.vector.tensor_tensor(affine[:, 5:6], mlp_bias(be), affine[:, 6:7], ALU.subtract
                                        ).then_inc(affine_step, 1)
            if act is not None:
                act.wait_ge(affine_step, step + 1)
                nc.scalar.activation(affine[:, 2:3], affine[:, 1:2], ACT.Sqrt, bias=eps_col[:, 0:1]
                                     ).then_inc(affine_step, 1)

        assert EPS_BN == EPS_LN

        with ExitStack() as ctx:
            def buf(name, shape, dt=F32):
                return [sb(f"{name}_s{q}", shape, dt, ctx) for q in range(2)]

            idx = buf("idx", [P, TPH], I32)
            src = buf("src", [P, TPH, D])
            u = buf("u", [P, HROWS])
            eh = buf("eh", [P, HROWS])
            stats = sb("stats", [P, 2 * groups_e, 6], ctx=ctx)
            ps_t = [ctx.enter_context(nc.psum_tensor(f"ps_st{q}", [P, HROWS], F32)) for q in range(2)]
            ps_h = [ctx.enter_context(nc.psum_tensor(f"ps_sh{q}", [P, HROWS], F32)) for q in range(2)]
            block = ctx.enter_context(nc.Block())

            @block.sync
            def _(sp):
                with sp.Fori(0, groups_e) as i:
                    for q in range(2):
                        sp.wait_ge(gathered[q], i * (TPH * 16) + gathers_before)
                        sp.dma_start(idx[q][:], gather_idx[bass.ds(i * 2 + q, 1), :, 0:TPH].rearrange(
                            "a p c -> p (a c)")).then_inc(idx_loaded[q], 16)
                        sp.wait_ge(eh_ready[q], i)
                        sp.dma_start(u[q][D:2 * D, :], ea_t_h[bass.ds(i * 2 + q, 1)].rearrange("a p c -> p (a c)")
                                     ).then_inc(ea_loaded[q], 16)

            @block.gpsimd
            def _(pool):
                with pool.Fori(0, groups_e) as i:
                    for q in range(2):
                        pool.wait_ge(idx_loaded[q], i * 16 + (loads_before + 16))
                        pool.wait_ge(s_t[q], i)
                        pool.nop(nofuse=True)
                        for k in range(TPH):
                            nc.gpsimd.indirect_dma_start(
                                src[q][:, k, :], None, x_mid, bass.IndirectOffsetOnAxis(ap=idx[q][:, k:k + 1], axis=0)
                            ).then_inc(gathered[q], 16)

            @block.tensor
            def _(pe):
                with pe.Fori(0, groups_e) as i:
                    for q in range(2):
                        pe.wait_ge(gathered[q], i * (TPH * 16) + (gathers_before + TPH * 16))
                        pe.wait_ge(s_t_copied[q], i)
                        pe.nop(nofuse=True)
                        for k in range(TPH):
                            last = nc.tensor.transpose(ps_t[q][0:D, k * P:(k + 1) * P], src[q][:, k, :], ident)
                        last.then_inc(s_t[q], 1)
                        pe.wait_ge(s_t_copied[q], i + 1)
                        pe.wait_ge(ea_loaded[q], i * 16 + 16)
                        pe.wait_ge(eh_copied[q], i)
                        nc.tensor.matmul(ps_h[q][:], mlp("w1a"), u[q][:], start=True, stop=True
                                         ).then_inc(eh_ready[q], 1)

            @block.scalar
            def _(act):
                with act.Fori(0, groups_e) as i:
                    for q in range(2):
                        act.wait_ge(s_t[q], i + 1)
                        act.wait_ge(eh_ready[q], i)
                        nc.scalar.activation(u[q][0:D, :], ps_t[q][0:D, :], ACT.Copy).then_inc(s_t_copied[q], 1)
                        act.wait_ge(eh_ready[q], i + 1)
                        act.wait_ge(eh_stats[q], i)
                        act.wait_ge(eh_stored[q], i * 16)
                        nc.scalar.activation(eh[q][:], ps_h[q][:], ACT.Identity, bias=mlp_bias("b1a")
                                             ).then_inc(eh_copied[q], 1)
                        act.wait_ge(eh_copied[q], i + 1)
                        act.dma_start(edge_hid[bass.ds(i * 2 + q, 1)].rearrange("a p c -> p (a c)"), eh[q][:]
                                      ).then_inc(eh_stored[q], 16)
                for q in range(2):
                    act.wait_ge(eh_stored[q], 16 * groups_e)
                bn_affine(None, act, stats, edge_affine, 0, "g1a", "be1a")

            @block.vector
            def _(dve):
                with dve.Fori(0, groups_e) as i:
                    for q in range(2):
                        dve.wait_ge(eh_copied[q], i + 1)
                        nc.vector.bn_stats(stats[:, bass.ds(i * 2 + q, 1), :].rearrange("p a c -> p (a c)"), eh[q][:]
                                           ).then_inc(eh_stats[q], 1)
                for q in range(2):
                    valid = min(HROWS, n_edges - (2 * (groups_e - 1) + q) * HROWS)
                    assert valid > 0
                    dve.wait_ge(eh_stats[q], groups_e)
                    nc.vector.bn_stats(stats[:, 2 * (groups_e - 1) + q, :], eh[q][:, 0:valid]
                                       ).then_inc(eh_stats[q], 1)
                for q in range(2):
                    dve.wait_ge(eh_stats[q], groups_e + 1)
                bn_affine(dve, None, stats, edge_affine, 0, "g1a", "be1a")

        dst_loaded, eh_loaded, same2, relu_ready = sems("dst_loaded"), sems("eh_loaded"), sems("same2"), sems("relu")
        out_ready, out_copied = sems("out_ready"), sems("out_copied")
        add_ready, add_copied, sidx2 = sems("add_ready"), sems("add_copied"), sems("sidx2")
        added = [sems(f"added{t}_") for t in range(TABLES)]
        PER = TPH // TABLES

        with ExitStack() as ctx:
            def buf(name, shape, dt=F32):
                return [sb(f"{name}_m{q}", shape, dt, ctx) for q in range(2)]

            drow = buf("drow", [P, TPH, P], I32)
            dcol = buf("dcol", [P, TPH], I32)
            same = buf("same", [P, TPH, P])
            sidx = buf("sidx", [P, TPH], I32)
            eh = buf("eh", [P, HROWS])
            act_eh = buf("act_eh", [P, HROWS])
            eo = buf("eo", [P, TPH, HID])
            sums = buf("sums", [P, TPH, HID])
            ps_o = [ctx.enter_context(nc.psum_tensor(f"ps_mo{q}", [P, TPH, HID], F32)) for q in range(2)]
            ps_s = [ctx.enter_context(nc.psum_tensor(f"ps_ms{q}", [P, TPH, HID], F32)) for q in range(2)]
            block = ctx.enter_context(nc.Block())

            @block.sync
            def _(sp):
                with sp.Fori(0, groups_e) as i:
                    for q in range(2):
                        sp.wait_ge(relu_ready[q], i)
                        sp.dma_start(eh[q][:], edge_hid[bass.ds(i * 2 + q, 1)].rearrange("a p c -> p (a c)")
                                     ).then_inc(eh_loaded[q], 16)
                        sp.wait_ge(same2[q], i)
                        sp.dma_start(dcol[q][:], dst_col[bass.ds(i * 2 + q, 1)].rearrange("a p c -> p (a c)")
                                     ).then_inc(dst_loaded[q], 16)
                        sp.dma_start(drow[q][:], dst_row[bass.ds(i * 2 + q, 1), :].rearrange("a c -> (a c)")
                                     .partition_broadcast(P)).then_inc(dst_loaded[q], 16)

            @block.gpsimd
            def _(pool):
                with pool.Fori(0, groups_e) as i:
                    for q in range(2):
                        for k in range(TPH):
                            t = k % TABLES
                            if k == 0:
                                pool.wait_ge(add_copied[q], i + 1)
                                pool.wait_ge(sidx2[q], i + 1)
                            if k < TABLES:
                                pool.wait_ge(added[t][1 - q], (i + q) * (PER * 16))
                            else:
                                pool.wait_ge(added[t][q], i * (PER * 16) + k // TABLES * 16)
                            pool.nop(nofuse=True)
                            nc.gpsimd.indirect_dma_start(
                                mlp_sums[t], bass.IndirectOffsetOnAxis(ap=sidx[q][:, k:k + 1], axis=0),
                                sums[q][:, k, :], None, compute_op=ALU.add).then_inc(added[t][q], 16)
                for t in range(TABLES):
                    for q in range(2):
                        pool.wait_ge(added[t][q], groups_e * PER * 16)

            @block.tensor
            def _(pe):
                with pe.Fori(0, groups_e) as i:
                    for q in range(2):
                        pe.wait_ge(relu_ready[q], i + 1)
                        pe.wait_ge(out_copied[q], i)
                        for k in range(TPH):
                            last = nc.tensor.matmul(ps_o[q][:, k, :], act_eh[q][:, k * P:(k + 1) * P], mlp("w2a"),
                                                    start=True, stop=True)
                        last.then_inc(out_ready[q], 1)
                        pe.wait_ge(same2[q], i + 1)
                        pe.wait_ge(out_copied[q], i + 1)
                        pe.wait_ge(add_copied[q], i)
                        for k in range(TPH):
                            last = nc.tensor.matmul(ps_s[q][:, k, :], same[q][:, k, :], eo[q][:, k, :],
                                                    start=True, stop=True)
                        last.then_inc(add_ready[q], 1)

            @block.scalar
            def _(act):
                with act.Fori(0, groups_e) as i:
                    for q in range(2):
                        act.wait_ge(eh_loaded[q], i * 16 + 16)
                        act.wait_ge(out_ready[q], i)
                        nc.scalar.activation(act_eh[q][:], eh[q][:], ACT.Relu, bias=edge_affine[:, 5:6],
                                             scale=edge_affine[:, 4:5]).then_inc(relu_ready[q], 1)
                        act.wait_ge(add_ready[q], i + 1)
                        for t in range(TABLES):
                            act.wait_ge(added[t][q], i * (PER * 16))
                        nc.scalar.activation(sums[q][:], ps_s[q][:], ACT.Copy).then_inc(add_copied[q], 1)

            @block.vector
            def _(dve):
                with dve.Fori(0, groups_e) as i:
                    for q in range(2):
                        dve.wait_ge(dst_loaded[q], i * 32 + 32)
                        dve.wait_ge(add_ready[q], i)
                        nc.vector.tensor_tensor(same[q][:], drow[q][:],
                                                dcol[q][:].unsqueeze(2).broadcast_to([P, TPH, P]),
                                                ALU.is_equal).then_inc(same2[q], 1)
                        for t in range(TABLES):
                            dve.wait_ge(added[t][q], i * (PER * 16))
                        nc.vector.tensor_copy(sidx[q][:], scatter_all[:, bass.ds(i * TPG + q * TPH, TPH)]
                                              ).then_inc(sidx2[q], 1)
                        dve.wait_ge(out_ready[q], i + 1)
                        nc.vector.tensor_tensor(eo[q][:], ps_o[q][:],
                                                b2a_rows[:].unsqueeze(1).broadcast_to([P, TPH, HID]),
                                                ALU.add).then_inc(out_copied[q], 1)

        nh_loaded, nh_summed, nx_t, na_t = sems("nh_loaded"), sems("nh_summed"), sems("nx_t"), sems("na_t")
        na_lo, na_hi = sem("na_lo"), sem("na_hi")
        nh_ready, nh_hi, nh_stats, nh_stored = (sems("nh_ready"), sems("nh_hi"),
                                                       sems("nh_stats"), sems("nh_stored"))

        def over_groups(eng, stages):
            with eng.Fori(0, pairs) as i:
                for stage in stages:
                    for q in range(2):
                        stage(i * 2 + q, i, q)
            if odd:
                for stage in stages:
                    stage(2 * pairs, pairs, 0)

        with ExitStack() as ctx:
            def buf(name, shape, dt=F32):
                return [sb(f"{name}_h{q}", shape, dt, ctx) for q in range(2)]

            xrow = buf("xrow", [P, TPG * D])
            part = [buf(f"part{t}", [P, TPG * HID]) for t in range(TABLES)]
            agg = buf("agg", [P, TPG, HID])
            xT = buf("xT", [P, HROWS])
            aggT = buf("aggT", [P, 2, HROWS])
            nh = buf("nh", [P, 2, HROWS])
            stats = sb("nstats", [P, 2 * groups_n, 6], ctx=ctx)
            ps = [[ctx.enter_context(nc.psum_tensor(f"ps_h{q}{b}", [P, HROWS], F32)) for b in range(4)]
                  for q in range(2)]
            block = ctx.enter_context(nc.Block())

            @block.sync
            def _(sp):
                def load(g, n, q):
                    sp.wait_ge(nx_t[q], n)
                    sp.dma_start(xrow[q][:], x_mid_g[bass.ds(g, 1)].rearrange("a p c -> p (a c)")
                                 ).then_inc(nh_loaded[q], 16)
                    sp.wait_ge(nh_summed[q], n)
                    for t in range(TABLES):
                        sp.dma_start(part[t][q][:], mlp_sums_g[t][bass.ds(g, 1)].rearrange("a p c -> p (a c)")
                                     ).then_inc(nh_loaded[q], 16)
                over_groups(sp, [load])

            @block.gpsimd
            def _(pool):
                def total(g, n, q):
                    pool.wait_ge(nh_loaded[q], (n + 1) * (16 * (1 + TABLES)))
                    pool.wait_ge(na_t[q], n)
                    nc.gpsimd.tensor_tensor(agg[q][:].rearrange("p k c -> p (k c)"), part[0][q][:], part[1][q][:],
                                            ALU.add).then_inc(nh_summed[q], 1)
                over_groups(pool, [total])

            @block.tensor
            def _(pe):
                def turns_x(g, n, q):
                    pe.wait_ge(nh_loaded[q], (n + 1) * (16 * (1 + TABLES)))
                    pe.wait_ge(nh_hi[q], n)
                    for m in range(TPH):
                        last = nc.tensor.transpose(ps[q][0][:, m * P:(m + 1) * P], xrow[q][:, m * P:(m + 1) * P],
                                                   ident)
                    last.then_inc(nx_t[q], 1)

                def turns_agg(g, n, q):
                    pe.wait_ge(nh_summed[q], n + 1)
                    for j in range(TPG):
                        m = j // 2
                        last = nc.tensor.transpose(ps[q][1 + j % 2][:, m * P:(m + 1) * P], agg[q][:, j, :], ident)
                    last.then_inc(na_t[q], 1)

                def hidden(g, n, q):
                    pe.wait_ge(na_lo, g + 1)
                    pe.wait_ge(na_hi, g + 1)
                    for side, (dst, w) in enumerate(((ps[q][3], "w1b_x_lo"), (ps[q][0], "w1b_x_hi"))):
                        nc.tensor.matmul(dst[:], mlp(w), xT[q][:], start=True, stop=False)
                        last = nc.tensor.matmul(dst[:], mlp("w1b_agg"), aggT[q][:, side, :], start=False, stop=True)
                    last.then_inc(nh_ready[q], 1)

                over_groups(pe, [turns_x, turns_agg, hidden])

            @block.scalar
            def _(act):
                def copy_lo(g, n, q):
                    act.wait_ge(na_t[q], n + 1)
                    act.wait_ge(nh_ready[q], n)
                    nc.scalar.activation(aggT[q][:, 0, :], ps[q][1][:], ACT.Copy).then_inc(na_lo, 1)

                def bias_lo(g, n, q):
                    act.wait_ge(nh_ready[q], n + 1)
                    act.wait_ge(nh_stats[q], n)
                    act.wait_ge(nh_stored[q], n * 16)
                    nc.scalar.activation(nh[q][:, 0, :], ps[q][3][:], ACT.Identity, bias=mlp_bias("b1b"))

                def bias_hi(g, n, q):
                    nc.scalar.activation(nh[q][:, 1, :], ps[q][0][:], ACT.Identity, bias=mlp_bias("b1b")
                                         ).then_inc(nh_hi[q], 1)

                def store(g, n, q):
                    act.wait_ge(nh_hi[q], n + 1)
                    act.dma_start(node_hid[bass.ds(g, 1)].rearrange("a p c -> p (a c)"),
                                  nh[q][:].rearrange("p s c -> p (s c)")).then_inc(nh_stored[q], 16)

                over_groups(act, [copy_lo, bias_lo, bias_hi, store])
                act.wait_ge(nh_stored[0], 16 * (pairs + odd))
                act.wait_ge(nh_stored[1], 16 * pairs)
                bn_affine(None, act, stats, node_affine, 6, "g1b", "be1b")

            @block.vector
            def _(dve):
                def copy_x(g, n, q):
                    dve.wait_ge(nx_t[q], n + 1)
                    dve.wait_ge(nh_ready[q], n)
                    nc.vector.tensor_copy(xT[q][:], ps[q][0][:])

                def copy_hi(g, n, q):
                    dve.wait_ge(na_t[q], n + 1)
                    nc.vector.tensor_copy(aggT[q][:, 1, :], ps[q][2][:]).then_inc(na_hi, 1)

                def statistics(g, n, q):
                    dve.wait_ge(nh_hi[q], n + 1)
                    dve.nop(nofuse=True)
                    for side in range(2):
                        last = nc.vector.bn_stats(
                            stats[:, bass.ds(g * 2 + side, 1), :].rearrange("p a c -> p (a c)"), nh[q][:, side, :])
                    last.then_inc(nh_stats[q], 1)

                over_groups(dve, [copy_x, copy_hi, statistics])
                q = (groups_n - 1) % 2
                n = pairs + odd if q == 0 else pairs
                left = n_nodes - (groups_n - 1) * ROWS
                assert left > 0 and left % TPG == 0
                dve.wait_ge(nh_stats[q], n)
                for side in range(2):
                    last = nc.vector.bn_stats(stats[:, 2 * (groups_n - 1) + side, :], nh[q][:, side, :].rearrange(
                        "p (m c) -> p m c", c=P)[:, :, 0:left // TPG])
                last.then_inc(nh_stats[q], 1)
                dve.wait_ge(nh_stats[q], n + 1)
                dve.wait_ge(nh_stats[1 - q], pairs if q == 0 else pairs + odd)
                bn_affine(dve, None, stats, node_affine, 6, "g1b", "be1b")

        f_loaded, f_relu, f_ready, f_bias = sems("f_loaded"), sems("f_relu"), sems("f_ready"), sems("f_bias")
        f_sum, f_total, f_mean, f_center, f_sq = (sems("f_sum"), sem("f_total"), sem("f_mean"), sem("f_center"),
                                                  sem("f_sq"))
        f_var, f_std, f_rstd, f_out, f_stored = (sem("f_var"), sem("f_std"), sem("f_rstd"), sem("f_out"),
                                                 sems("f_stored"))
        with ExitStack() as ctx:
            def buf(name, shape, dt=F32):
                return [sb(f"{name}_f{q}", shape, dt, ctx) for q in range(2)]

            xrow = buf("xrow", [P, TPG, D])
            nh = buf("nh", [P, 2, HROWS])
            act_nh = buf("act_nh", [P, 2, HROWS])
            xb = buf("xb", [P, TPG, D])
            y = buf("y", [P, TPG, D])
            total = buf("total", [P, TPG])
            mean = buf("mean", [P, TPG])
            cen = buf("cen", [P, TPG, D])
            sq = buf("sq", [P, TPG, D])
            var, std, rstd = buf("var", [P, TPG]), buf("std", [P, TPG]), buf("rstd", [P, TPG])
            res = buf("res", [P, TPG, D])
            ps = [ctx.enter_context(nc.psum_tensor(f"ps_f{q}", [P, TPG, D], F32)) for q in range(2)]
            block = ctx.enter_context(nc.Block())

            @block.sync
            def _(sp):
                def load(g, n, q):
                    sp.wait_ge(f_relu[q], n)
                    sp.dma_start(nh[q][:].rearrange("p s c -> p (s c)"),
                                 node_hid[bass.ds(g, 1)].rearrange("a p c -> p (a c)")).then_inc(f_loaded[q], 16)
                    sp.wait_ge(f_bias[q], n)
                    sp.dma_start(xrow[q][:].rearrange("p k c -> p (k c)"),
                                 x_mid_g[bass.ds(g, 1)].rearrange("a p c -> p (a c)")).then_inc(f_loaded[q], 16)
                over_groups(sp, [load])

            @block.gpsimd
            def _(pool):
                def bias(g, n, q):
                    pool.wait_ge(f_loaded[q], (n + 1) * 32)
                    pool.wait_ge(f_sum[q], n)
                    nc.gpsimd.tensor_tensor(xb[q][:], xrow[q][:], b2b_rows[:].unsqueeze(1).broadcast_to([P, TPG, D]),
                                            ALU.add).then_inc(f_bias[q], 1)

                def store(g, n, q):
                    pool.wait_ge(f_out, g + 1)
                    pool.nop(nofuse=True)
                    pool.dma_start(out_g[bass.ds(g, 1)].rearrange("a p c -> p (a c)"),
                                   res[q][:].rearrange("p k c -> p (k c)")).then_inc(f_stored[q], 16)
                over_groups(pool, [bias, store])
                pool.wait_ge(f_stored[0], 16 * (pairs + odd))
                pool.wait_ge(f_stored[1], 16 * pairs)

            @block.tensor
            def _(pe):
                def product(g, n, q):
                    pe.wait_ge(f_relu[q], n + 1)
                    pe.wait_ge(f_sum[q], n)
                    for j in range(TPG):
                        m = j // 2
                        last = nc.tensor.matmul(ps[q][:, j, :], act_nh[q][:, j % 2, m * P:(m + 1) * P], mlp("w2b"),
                                                start=True, stop=True)
                    last.then_inc(f_ready[q], 1)
                over_groups(pe, [product])

            @block.scalar
            def _(act):
                def relu(g, n, q):
                    act.wait_ge(f_loaded[q], (n + 1) * 32)
                    act.wait_ge(f_ready[q], n)
                    nc.scalar.activation(act_nh[q][:], nh[q][:], ACT.Relu, bias=node_affine[:, 5:6],
                                         scale=node_affine[:, 4:5]).then_inc(f_relu[q], 1)

                def square(g, n, q):
                    act.wait_ge(f_center, g + 1)
                    nc.scalar.activation(sq[q][:], cen[q][:], ACT.Square).then_inc(f_sq, 1)

                def deviation(g, n, q):
                    act.wait_ge(f_var, g + 1)
                    nc.scalar.activation(std[q][:], var[q][:], ACT.Sqrt, bias=eps_col[:, 0:1], scale=1.0 / D
                                         ).then_inc(f_std, 1)
                over_groups(act, [relu, square, deviation])

            @block.vector
            def _(dve):
                def center_rows(g, n, q):
                    dve.wait_ge(f_ready[q], n + 1)
                    dve.wait_ge(f_bias[q], n + 1)
                    nc.vector.tensor_tensor(y[q][:], ps[q][:], xb[q][:], ALU.add).then_inc(f_sum[q], 1)
                    dve.wait_ge(f_sum[q], n + 1)
                    nc.vector.tensor_reduce(total[q][:], y[q][:], AX.X, ALU.add).then_inc(f_total, 1)
                    dve.wait_ge(f_total, g + 1)
                    nc.vector.tensor_scalar(mean[q][:], total[q][:], 1.0 / D, None, ALU.mult).then_inc(f_mean, 1)
                    dve.wait_ge(f_mean, g + 1)
                    nc.vector.tensor_tensor(cen[q][:], y[q][:], mean[q][:].unsqueeze(2).broadcast_to([P, TPG, D]),
                                            ALU.subtract).then_inc(f_center, 1)

                def variance(g, n, q):
                    dve.wait_ge(f_sq, g + 1)
                    nc.vector.tensor_reduce(var[q][:], sq[q][:], AX.X, ALU.add).then_inc(f_var, 1)

                def scale(g, n, q):
                    dve.wait_ge(f_std, g + 1)
                    nc.vector.reciprocal(rstd[q][:], std[q][:]).then_inc(f_rstd, 1)
                    dve.wait_ge(f_rstd, g + 1)
                    dve.wait_ge(f_stored[q], n * 16)
                    nc.vector.tensor_tensor(res[q][:], cen[q][:], rstd[q][:].unsqueeze(2).broadcast_to([P, TPG, D]),
                                            ALU.mult).then_inc(f_out, 1)
                over_groups(dve, [center_rows, variance, scale])


def _round(n, k):
    return (n + k - 1) // k * k


def host_arrays(inp):
    f = {k: np.asarray(v) for k, v in inp.items()}
    n, e = f["x"].shape[0], f["src"].shape[0]
    n_pad, e_pad = _round(n, ROWS), _round(e, ROWS)
    if n_pad == n:
        n_pad += ROWS
    halves = e_pad // HROWS
    x = np.zeros((n_pad, D), np.float32)
    x[:n] = f["x"]
    ea_t = np.zeros((D, e_pad), np.float32)
    ea_t[:, :e] = f["edge_attr_64"].T
    src = np.full(e_pad, n_pad - 1, np.int32)
    dst = np.full(e_pad, n_pad - 1, np.int32)
    src[:e], dst[:e] = f["src"], f["dst"]
    src_c = src.reshape(halves, TPH, P).transpose(0, 2, 1)
    dst_c = dst.reshape(halves, TPH, P).transpose(0, 2, 1)

    consts = np.zeros((P, N_CONSTS), np.float32)
    eye, pair = np.eye(P, dtype=np.float32), np.kron(np.eye(2), np.ones((D, D))).astype(np.float32) / D
    consts[:, 0:P], consts[:, P:2 * P], consts[:, 2 * P:3 * P] = eye, eye - pair, pair
    consts[:, 3 * P:4 * P] = np.tril(np.ones((P, P)), -1)
    consts[:, 4 * P] = n_pad + np.arange(P)

    layer_w = np.zeros((P, LAYERS, N_LAYER_W), np.float32)
    layer_b = np.zeros((P, LAYERS, len(LAYER_B)), np.float32)
    for l in range(LAYERS):
        w = {k: f[f"L0_gnn_{k}"][l] for k in ("WK", "WV", "WQ", "WE", "WO", "W1", "W2", "bO", "ln1_g", "ln1_b", "b1",
                                              "b2", "ln2_g", "ln2_b")}
        lw = layer_w[:, l]
        lw[:D, 0:D], lw[:D, D:2 * D], lw[D:, 2 * D:3 * D], lw[:D, 3 * D:4 * D] = w["WK"], w["WV"], w["WQ"], w["WE"]
        for r in range(2):
            lw[r * D:(r + 1) * D, 256 + r * D:256 + (r + 1) * D] = w["WO"].T
            lw[r * D:(r + 1) * D, 384 + r * P:384 + (r + 1) * P] = w["W1"]
            lw[r * D:(r + 1) * D, 640 + r * P:640 + (r + 1) * P] = w["W2"].T
        for k, name in enumerate(("bO", "ln1_g", "ln1_b", "b1", "b2", "ln2_g", "ln2_b")):
            layer_b[:, l, k] = w[name] if w[name].size == P else np.concatenate([w[name], w[name]])

    g = {k: f[f"L1_gnn_{k}"] for k in ("W1a", "b1a", "g1a", "be1a", "W2a", "b2a", "W1b", "b1b", "g1b", "be1b", "W2b",
                                       "b2b")}
    mlp_w = np.zeros((P, N_MLP_W), np.float32)
    mlp_w[:, 0:P], mlp_w[:, P:2 * P] = g["W1a"], g["W2a"]
    mlp_w[:D, 2 * P:3 * P], mlp_w[D:, 3 * P:4 * P] = g["W1b"][:D], g["W1b"][:D]
    mlp_w[:, 4 * P:5 * P], mlp_w[:, 5 * P:] = g["W1b"][D:], g["W2b"]
    mlp_b = np.stack([g[k] for k in MLP_B], axis=1)
    mlp_rows = np.zeros((2, HID), np.float32)
    mlp_rows[0], mlp_rows[1, :D] = g["b2a"], g["b2b"]
    return dict(x=x, ea_t=ea_t, gather_idx=np.ascontiguousarray(np.concatenate([src_c, dst_c], axis=2)),
                dst_row=dst.reshape(halves, HROWS), dst_col=np.ascontiguousarray(dst_c), consts=consts,
                layer_w=layer_w, layer_b=layer_b, mlp_w=mlp_w, mlp_b=np.ascontiguousarray(mlp_b), mlp_rows=mlp_rows)


def kernel(**inputs):
    import concourse.bacc as bacc
    from concourse.bass_utils import run_bass_kernel_spmd

    n, e = inputs["x"].shape[0], inputs["src"].shape[0]
    arrays = host_arrays(inputs)
    nc = bacc.Bacc("TRN2", target_bir_lowering=False, num_devices=1)
    args = {k: nc.dram_tensor(f"in_{k}", a.shape, mybir.dt.from_np(a.dtype), kind="ExternalInput").ap()
            for k, a in arrays.items()}
    out = nc.dram_tensor("out_nodes", arrays["x"].shape, F32, kind="ExternalOutput").ap()
    build(nc, n, e, *args.values(), out)
    r = run_bass_kernel_spmd(nc, [{f"in_{k}": a for k, a in arrays.items()}], core_ids=[0])
    return r.results[0]["out_nodes"][:n]
```

```python
from contextlib import ExitStack

import numpy as np

import concourse.bass as bass
from concourse import mybir

P = 128
D = 64
HEADS = 4
DH = D // HEADS
HID = 2 * D
LAYERS = 2
MSG = D + HEADS
TPG = 8
TPH = TPG // 2
ROWS = TPG * P
HROWS = TPH * P
TILES = 2
TABLES = 2
SPARE = TILES * P
WIDTH = 4
ACT_SET = "natural_log_exp_and_others"
EPS_LN = 1e-5
EPS_BN = 1e-5
EPS_Z = 1e-6
CLIP = 5.0 * DH ** 0.5

ALU = mybir.AluOpType
ACT = mybir.ActivationFunctionType
AX = mybir.AxisListType
F32 = mybir.dt.float32
I32 = mybir.dt.int32

CONSTS = dict(ident=(0, P), center=(P, P), average=(2 * P, P),
              earlier=(3 * P, TILES * TILES * P), spare=((3 + TILES * TILES) * P, TPH))
N_CONSTS = (3 + TILES * TILES) * P + TPH
LAYER_W = dict(kvq=(0, 3 * D), e=(3 * D, D), wo_t=(256, P), w1_lo=(384, P), w1_hi=(512, P),
               w2_t_lo=(640, P), w2_t_hi=(768, P))
N_LAYER_W = 896
LAYER_B = ("bo", "g1", "be1", "b1", "b2", "g2", "be2")
MLP_W = dict(w1a=(0, P), w2a=(P, P), w1b_x_lo=(2 * P, P), w1b_x_hi=(3 * P, P), w1b_agg=(4 * P, P), w2b=(5 * P, D))
N_MLP_W = 5 * P + D
MLP_B = ("b1a", "g1a", "be1a", "b1b", "g1b", "be1b")


def row_of(ap, p=P):
    return ap.partition_broadcast(p)


def build(nc, n_nodes, n_edges, x, x_t, ea_t, gather_idx, dst_row, dst_col, consts, layer_w, layer_b, mlp_w, mlp_b,
          mlp_rows, out):
    groups_n = x.shape[0] // ROWS
    groups_e = ea_t.shape[1] // ROWS
    n_pad = groups_n * ROWS
    table_rows = n_pad + SPARE
    assert groups_e <= groups_n

    def dram(name, shape):
        return nc.dram_tensor(name, shape, F32, kind="Internal").ap()

    h_mid, h_mid_t = dram("h_mid", [n_pad, D]), dram("h_mid_t", [groups_n, P, HROWS])
    x_mid, x_mid_t = dram("x_mid", [n_pad, D]), dram("x_mid_t", [groups_n, P, HROWS])
    attn_sums = [dram(f"attn_sums{l}", [table_rows, MSG]) for l in range(LAYERS)]
    mlp_sums = [dram(f"mlp_sums{t}", [table_rows, HID]) for t in range(TABLES)]
    edge_hid = dram("edge_hid", [2 * groups_e, P, HROWS])
    node_hid = dram("node_hid", [groups_n, P, ROWS])

    def by_group(table):
        return table[0:n_pad, :].rearrange("(g p j) d -> g p (j d)", p=P, j=TPG)

    def spare_rows(table):
        return table[n_pad:table_rows, :].rearrange("(p j) d -> p (j d)", p=P)

    def pick(ap, i):
        return ap[bass.ds(i, 1)].rearrange("a p c -> p (a c)")

    h_mid_g, x_mid_g, out_g = by_group(h_mid), by_group(x_mid), by_group(out)
    attn_sums_g = [by_group(t) for t in attn_sums]
    mlp_sums_g = [by_group(t) for t in mlp_sums]
    ea_t_h = ea_t.rearrange("d (h c) -> h d c", c=HROWS)

    def over_groups(eng, stages, count=groups_n, width=WIDTH):
        with eng.Fori(0, count // width) as i:
            for stage in stages:
                for q in range(width):
                    stage(i * width + q, i, q)
        for stage in stages:
            for q in range(count % width):
                stage(count - count % width + q, count // width, q)

    def turns_of(q, count=groups_n, width=WIDTH):
        return count // width + (q < count % width)

    class Stage:

        def __init__(self, tag):
            self.tag = tag

        def __enter__(self):
            self.ctx = ExitStack()
            self.handles = []
            return self

        def sem(self, name):
            self.handles.append(nc.alloc_semaphore(f"{self.tag}_{name}"))
            return self.handles[-1]

        def sems(self, name, width=2):
            return [self.sem(f"{name}{q}") for q in range(width)]

        def sb(self, name, shape, dt=F32):
            return self.ctx.enter_context(nc.sbuf_tensor(f"{self.tag}_{name}", shape, dt))

        def bufs(self, name, shape, dt=F32, width=2):
            return [self.sb(f"{name}{q}", shape, dt) for q in range(width)]

        def banks(self, name, shape, width=2):
            return [self.ctx.enter_context(nc.psum_tensor(f"{self.tag}_{name}{q}", shape, F32)) for q in range(width)]

        def block(self):
            return self.ctx.enter_context(nc.Block())

        def __exit__(self, *failed):
            self.ctx.__exit__(*failed)
            if failed[0] is None:
                nc.clear_and_free_semaphores(self.handles)
                nc.all_engine_barrier()

    with ExitStack() as top:
        def sb(name, shape, dt=F32):
            return top.enter_context(nc.sbuf_tensor(name, shape, dt))

        cst = sb("cst", [P, N_CONSTS])
        lw = sb("lw", [P, LAYERS, N_LAYER_W])
        lb = sb("lb", [P, LAYERS, len(LAYER_B)])
        mw = sb("mw", [P, N_MLP_W])
        mb = sb("mb", [P, len(MLP_B)])
        b2a_rows = sb("b2a_rows", [P, HID])
        b2b_rows = sb("b2b_rows", [P, D])
        eps_col = sb("eps_col", [P, 1])
        centered = sb("centered", [P, LAYERS, 3, P])
        centered_b = sb("centered_b", [P, LAYERS, 2])
        scatter_all = sb("scatter_all", [P, groups_e * TPG], I32)
        zeros = sb("zeros", [P, TPG * HID])
        edge_affine = sb("edge_affine", [P, 8])
        node_affine = sb("node_affine", [P, 8])

        def const(name):
            a, n = CONSTS[name]
            return cst[:, a:a + n]

        def layer(l, name):
            a, n = LAYER_W[name]
            return lw[:, l, a:a + n]

        def layer_bias(l, name):
            k = LAYER_B.index(name)
            return lb[:, l, k:k + 1]

        def mlp(name):
            a, n = MLP_W[name]
            return mw[:, a:a + n]

        def mlp_bias(name):
            k = MLP_B.index(name)
            return mb[:, k:k + 1]

        ident = const("ident")
        center = const("center")
        average = const("average")

        with Stage("setup") as st:
            setup_loaded, zeros_set, table_zero = st.sem("setup_loaded"), st.sem("zeros_set"), st.sem("table_zero")
            weights_centered, weights_copied = st.sem("weights_centered"), st.sem("weights_copied")
            n_setup = 7
            ps_w = st.banks("ps_w", [P, 512])
            block = st.block()

            @block.sync
            def _(sp):
                for dst, src in ((cst[:], consts), (lw[:], layer_w), (lb[:], layer_b), (mw[:], mlp_w), (mb[:], mlp_b),
                                 (b2a_rows[:], row_of(mlp_rows[0, :])),
                                 (b2b_rows[:], row_of(mlp_rows[1, 0:D]))):
                    sp.dma_start(dst, src).then_inc(setup_loaded, 16)
                sp.wait_ge(zeros_set, 1)
                with sp.Fori(0, groups_n) as i:
                    sp.dma_start(pick(attn_sums_g[0], i), zeros[:, 0:TPG * MSG]).then_inc(table_zero, 16)
                for table in (*attn_sums, *mlp_sums):
                    spare = spare_rows(table)
                    sp.dma_start(spare, zeros[:, 0:spare.shape[1]]).then_inc(table_zero, 16)
                sp.wait_ge(table_zero, 16 * (groups_n + LAYERS + TABLES))

            @block.scalar
            def _(act):
                nc.scalar.preload_act_table_set(ACT_SET)

            @block.vector
            def _(dve):
                nc.vector.memset(eps_col[:], EPS_LN)
                nc.vector.memset(zeros[:], 0.0).then_inc(zeros_set, 1)
                dve.wait_ge(weights_centered, 1)
                for l in range(LAYERS):
                    nc.vector.tensor_copy(centered[:, l, :, :], ps_w[l][:, 0:3 * P].rearrange("p (k c) -> p k c", c=P))
                    nc.vector.tensor_copy(centered_b[:, l, :], ps_w[l][:, 3 * P:3 * P + 2]).then_inc(weights_copied, 1)
                dve.wait_ge(weights_copied, LAYERS)

            @block.tensor
            def _(pe):
                pe.wait_ge(setup_loaded, 16 * n_setup)
                for l in range(LAYERS):
                    for k, name in enumerate(("wo_t", "w2_t_lo", "w2_t_hi")):
                        nc.tensor.matmul(ps_w[l][:, k * P:(k + 1) * P], layer(l, name), center, start=True, stop=True)
                    for k, name in enumerate(("bo", "b2")):
                        last = nc.tensor.matmul(ps_w[l][:, 3 * P + k:3 * P + k + 1], center, layer_bias(l, name),
                                                start=True, stop=True)
                last.then_inc(weights_centered, 1)

        def attention(l):
            nodes = (x, h_mid)[l]
            with Stage(f"attention{l}") as st:
                idx_loaded, gathered = st.sems("idx_loaded"), st.sems("gathered")
                edge_loaded = st.sems("edge_loaded")
                pair_t, pair_t_copied, kvqe_ready = st.sems("pair_t"), st.sems("pair_t_copied"), st.sems("kvqe_ready")
                same_ready, scatter_idx_ready = st.sems("same_ready"), st.sems("scatter_idx_ready")
                kqe_ready, exp_ready, msg_ready = st.sems("kqe_ready"), st.sems("exp_ready"), st.sems("msg_ready")
                sums_ready, sums_copied, scattered = st.sems("sums_ready"), st.sems("sums_copied"), st.sems("scattered")
                writer_step, qe_copied, kq_ready = st.sem("writer_step"), st.sem("qe_copied"), st.sem("kq_ready")
                dot_ready, clipped, tables_zero = st.sem("dot_ready"), st.sem("clipped"), st.sem("tables_zero")

                idx = st.bufs("idx", [P, 2 * TPH], I32)
                pair = st.bufs("pair", [P, TPH, 2 * D])
                pairT = st.bufs("pairT", [P, HROWS])
                ea = st.bufs("ea", [D, HROWS])
                drow = st.bufs("drow", [P, HROWS], I32)
                dcol = st.bufs("dcol", [P, TPH], I32)
                same = st.bufs("same", [P, TPH, TILES * P])
                earlier = st.bufs("earlier", [P, TPH, TILES * P])
                count = st.bufs("count", [P, TPH])
                offset = st.bufs("offset", [P, TPH])
                masked = st.bufs("masked", [P, TPH])
                sidx = st.bufs("sidx", [P, TPH], I32)
                qe = st.bufs("qe", [P, TPH, 2 * D])
                kq = st.bufs("kq", [P, TPH, D])
                kqe = st.bufs("kqe", [P, TPH, D])
                dot = st.bufs("dot", [P, TPH * HEADS])
                dotc = st.bufs("dotc", [P, TPH, HEADS])
                msg = st.bufs("msg", [P, TPH, MSG])
                sums = st.bufs("sums", [P, TPH, MSG])
                ps_t = st.banks("ps_t", [P, HROWS])
                ps_kvqe = st.banks("ps_kvqe", [P, TPH, 4 * D])
                ps_s = st.banks("ps_s", [P, 512])

                def nth(i, q):
                    return i * 2 + (q + 1)

                block = st.block()

                @block.sync
                def _(sp):
                    with sp.Fori(0, groups_e) as i:
                        for q in range(2):
                            sp.wait_ge(gathered[q], i * (2 * TPH * 16))
                            sp.dma_start(idx[q][:], pick(gather_idx, i * 2 + q)).then_inc(idx_loaded[q], 16)
                            sp.wait_ge(kvqe_ready[q], i)
                            sp.dma_start(ea[q][:], pick(ea_t_h, i * 2 + q)).then_inc(edge_loaded[q], 16)
                            if l == 0:
                                sp.wait_ge(writer_step, i * 6)
                            sp.wait_ge(same_ready[q], i)
                            sp.dma_start(dcol[q][:], pick(dst_col, i * 2 + q)).then_inc(edge_loaded[q], 16)
                            sp.dma_start(drow[q][:], row_of(dst_row[bass.ds(i * 2 + q, 1), :].rearrange("a c -> (a c)"))
                                         ).then_inc(edge_loaded[q], 16)
                        if l == 0:
                            for table in (attn_sums_g[1], *mlp_sums_g):
                                sp.dma_start(pick(table, i), zeros[:, 0:table.shape[2]]).then_inc(tables_zero, 16)
                    if l == 0:
                        for g in range(groups_e, groups_n):
                            for table in (attn_sums_g[1], *mlp_sums_g):
                                sp.dma_start(table[g], zeros[:, 0:table.shape[2]]).then_inc(tables_zero, 16)
                        sp.wait_ge(tables_zero, 16 * groups_n * (1 + TABLES))

                @block.gpsimd
                def _(pool):
                    def gather(i, q, k):
                        if k == 0:
                            pool.wait_ge(idx_loaded[q], i * 16 + 16)
                            pool.wait_ge(pair_t[q], i)
                            pool.nop(nofuse=True)
                        for side in range(2):
                            nc.gpsimd.indirect_dma_start(
                                pair[q][:, k, side * D:(side + 1) * D], None, nodes,
                                bass.IndirectOffsetOnAxis(ap=idx[q][:, side * TPH + k:side * TPH + k + 1], axis=0)
                            ).then_inc(gathered[q], 16)

                    def scatter(i, q, k):
                        if k == 0:
                            pool.wait_ge(sums_copied[q], i + 1)
                            pool.wait_ge(scatter_idx_ready[q], i + 1)
                            pool.wait_ge(scattered[1 - q], (i + q) * (TPH * 16))
                            pool.nop(nofuse=True)
                        elif k % TILES == 0:
                            pool.wait_ge(scattered[q], i * (TPH * 16) + 16 * k)
                            pool.nop(nofuse=True)
                        nc.gpsimd.indirect_dma_start(
                            attn_sums[l], bass.IndirectOffsetOnAxis(ap=sidx[q][:, k:k + 1], axis=0),
                            sums[q][:, k, :], None, compute_op=ALU.add).then_inc(scattered[q], 16)

                    for q in range(2):
                        for k in range(TPH):
                            gather(0, q, k)
                    with pool.Fori(0, groups_e - 1) as i:
                        for q in range(2):
                            for k in range(TPH):
                                scatter(i, q, k)
                                gather(i + 1, q, k)
                    for q in range(2):
                        for k in range(TPH):
                            scatter(groups_e - 1, q, k)
                    for q in range(2):
                        pool.wait_ge(scattered[q], groups_e * TPH * 16)

                @block.tensor
                def _(pe):
                    with pe.Fori(0, groups_e) as i:
                        for q in range(2):
                            pe.wait_ge(gathered[q], i * (2 * TPH * 16) + 2 * TPH * 16)
                            pe.wait_ge(pair_t_copied[q], i)
                            for k in range(TPH):
                                last = nc.tensor.transpose(ps_t[q][:, k * P:(k + 1) * P], pair[q][:, k, :], ident)
                            last.then_inc(pair_t[q], 1)
                            pe.wait_ge(pair_t_copied[q], i + 1)
                            pe.wait_ge(edge_loaded[q], i * 48 + 48)
                            pe.wait_ge(msg_ready[q], i)
                            for k in range(TPH):
                                nc.tensor.matmul(ps_kvqe[q][:, k, 0:3 * D], pairT[q][:, k * P:(k + 1) * P],
                                                 layer(l, "kvq"), start=True, stop=True)
                                last = nc.tensor.matmul(ps_kvqe[q][:, k, 3 * D:4 * D], ea[q][:, k * P:(k + 1) * P],
                                                        layer(l, "e")[0:D, :], start=True, stop=True)
                            last.then_inc(kvqe_ready[q], 1)
                            pe.wait_ge(same_ready[q], i + 1)
                            pe.wait_ge(msg_ready[q], i + 1)
                            pe.wait_ge(sums_copied[q], i)
                            for k in range(TPH):
                                for t in range(TILES):
                                    last = nc.tensor.matmul(
                                        ps_s[q][:, k * MSG:(k + 1) * MSG],
                                        same[q][:, k // TILES * TILES + t, k % TILES * P:(k % TILES + 1) * P],
                                        msg[q][:, k // TILES * TILES + t, :], start=(t == 0), stop=(t == TILES - 1))
                            last.then_inc(sums_ready[q], 1)

                @block.scalar
                def _(act):
                    nc.scalar.preload_act_table_set(ACT_SET)
                    with act.Fori(0, groups_e) as i:
                        for q in range(2):
                            act.wait_ge(pair_t[q], i + 1)
                            act.wait_ge(kvqe_ready[q], i)
                            nc.scalar.activation(pairT[q][:], ps_t[q][:], ACT.Copy).then_inc(pair_t_copied[q], 1)
                            act.wait_ge(kvqe_ready[q], i + 1)
                            act.wait_ge(kqe_ready[q], i)
                            nc.scalar.activation(qe[q][:], ps_kvqe[q][:, :, 2 * D:4 * D], ACT.Copy
                                                 ).then_inc(qe_copied, 1)
                            act.wait_ge(clipped, nth(i, q))
                            act.wait_ge(sums_ready[q], i)
                            nc.scalar.activation(msg[q][:, :, D:MSG], dotc[q][:], ACT.Exp, scale=DH ** -0.5
                                                 ).then_inc(exp_ready[q], 1)
                            act.wait_ge(sums_ready[q], i + 1)
                            act.wait_ge(scattered[q], i * (TPH * 16))
                            nc.scalar.activation(sums[q][:], ps_s[q][:, 0:TPH * MSG].rearrange(
                                "p (k c) -> p k c", c=MSG), ACT.Copy).then_inc(sums_copied[q], 1)

                @block.vector
                def _(dve):
                    with dve.Fori(0, groups_e) as i:
                        for q in range(2):
                            dve.wait_ge(edge_loaded[q], i * 48 + 48)
                            dve.wait_ge(sums_ready[q], i)
                            same_destinations(same[q], drow[q], dcol[q]).then_inc(same_ready[q], 1)
                            if l == 0:
                                dve.wait_ge(same_ready[q], i + 1)
                                nc.vector.tensor_tensor(
                                    earlier[q][:].rearrange("p (a t) c -> p a (t c)", t=TILES),
                                    same[q][:].rearrange("p (a t) c -> p a (t c)", t=TILES),
                                    const("earlier").unsqueeze(1).broadcast_to([P, TPH // TILES, TILES * TILES * P]),
                                    ALU.mult)
                                nc.vector.tensor_tensor(offset[q][:], dcol[q][:], const("spare"), ALU.subtract
                                                        ).then_inc(writer_step, 1)
                                dve.wait_ge(writer_step, i * 6 + (3 * q + 1))
                                nc.vector.tensor_reduce(count[q][:], earlier[q][:], AX.X, ALU.add
                                                        ).then_inc(writer_step, 1)
                                dve.wait_ge(writer_step, i * 6 + (3 * q + 2))
                                nc.vector.scalar_tensor_tensor(masked[q][:], count[q][:], 0.0, offset[q][:],
                                                               ALU.is_equal, ALU.mult).then_inc(writer_step, 1)
                                dve.wait_ge(writer_step, i * 6 + (3 * q + 3))
                                nc.vector.tensor_tensor(scatter_all[:, bass.ds(i * TPG + q * TPH, TPH)], masked[q][:],
                                                        const("spare"), ALU.add)
                            dve.wait_ge(qe_copied, nth(i, q))
                            nc.vector.tensor_tensor(kq[q][:], ps_kvqe[q][:, :, 0:D], qe[q][:, :, 0:D], ALU.mult
                                                    ).then_inc(kq_ready, 1)
                            dve.wait_ge(kq_ready, nth(i, q))
                            nc.vector.tensor_tensor(kqe[q][:], kq[q][:], qe[q][:, :, D:2 * D], ALU.mult
                                                    ).then_inc(kqe_ready[q], 1)
                            dve.wait_ge(kqe_ready[q], i + 1)
                            nc.vector.tensor_reduce(dot[q][:], kqe[q][:].rearrange("p k (h c) -> p (k h) c", c=DH),
                                                    AX.X, ALU.add).then_inc(dot_ready, 1)
                            dve.wait_ge(dot_ready, nth(i, q))
                            dve.wait_ge(exp_ready[q], i)
                            nc.vector.tensor_scalar(dotc[q][:].rearrange("p k h -> p (k h)"), dot[q][:], CLIP, -CLIP,
                                                    ALU.min, ALU.max).then_inc(clipped, 1)
                            dve.wait_ge(exp_ready[q], i + 1)
                            nc.vector.tensor_tensor(
                                msg[q][:, :, 0:D].rearrange("p k (h c) -> p k h c", c=DH),
                                ps_kvqe[q][:, :, D:2 * D].rearrange("p k (h c) -> p k h c", c=DH),
                                msg[q][:, :, D:MSG].unsqueeze(3).broadcast_to([P, TPH, HEADS, DH]),
                                ALU.mult).then_inc(msg_ready[q], 1)
                            dve.wait_ge(scattered[q], i * (TPH * 16))
                            if l == 0:
                                nc.vector.tensor_tensor(sidx[q][:], masked[q][:], const("spare"), ALU.add
                                                        ).then_inc(scatter_idx_ready[q], 1)
                            else:
                                nc.vector.tensor_copy(sidx[q][:], scatter_all[:, bass.ds(i * TPG + q * TPH, TPH)]
                                                      ).then_inc(scatter_idx_ready[q], 1)

        def same_destinations(same, drow, dcol):
            return nc.vector.tensor_tensor(
                same[:].rearrange("p (a t) c -> p a t c", t=TILES),
                drow[:].rearrange("p (a c) -> p a c", c=TILES * P).unsqueeze(2).broadcast_to(
                    [P, TPH // TILES, TILES, TILES * P]),
                dcol[:].rearrange("p (a t) -> p a t", t=TILES).unsqueeze(3).broadcast_to(
                    [P, TPH // TILES, TILES, TILES * P]),
                ALU.is_equal)

        def nodes(l):
            last_layer = l == LAYERS - 1
            norms = 3 if last_layer else 2
            source_t = (x_t, h_mid_t)[l]
            target, target_t = ((h_mid_g, h_mid_t), (x_mid_g, x_mid_t))[l]
            loads = 3 if last_layer else 2
            with Stage(f"nodes{l}") as st:
                node_loaded, attn_ready = st.sems("node_loaded", WIDTH), st.sems("attn_ready", WIDTH)
                center1_ready, xb_ready = st.sems("center1_ready", WIDTH), st.sems("xb_ready", WIDTH)
                rows_copied, rows_stored = st.sems("rows_copied", WIDTH), st.sems("rows_stored", WIDTH)
                t_stored = st.sems("t_stored", WIDTH)
                z_ready, rz_ready, a_t, a_t_copied = (st.sem("z_ready"), st.sem("rz_ready"), st.sem("a_t"),
                                                      st.sem("a_t_copied"))
                center2_ready, center3_ready = st.sem("center2_ready"), st.sem("center3_ready")
                sq_ready, var_ready, log_ready, rstd_ready, norm_ready = (
                    [st.sem(f"{name}{k}_ready") for k in range(norms)] for name in ("sq", "var", "log", "rstd", "norm"))
                h_ready = [st.sem(f"h{k}_ready") for k in range(2)]
                hid_ready, hid_lo_copied, hid_hi_copied = st.sem("hid_ready"), st.sem("hid_lo"), st.sem("hid_hi")
                rows_t = st.sem("rows_t")

                def bufs(name, shape=(P, HROWS)):
                    return st.bufs(name, list(shape), width=WIDTH)

                acc, z, rz = bufs("acc", (P, TPG, MSG)), bufs("z", (P, TPG, HEADS)), bufs("rz", (P, TPG, HEADS))
                attn = bufs("attn", (P, TPG, D))
                hT, aT, sq, log, rstd, norm = (bufs(f"{name}") for name in ("hT", "aT", "sq", "log", "rstd", "norm"))
                h1T, h2T, hid_lo, hid_hi, rows = (bufs(name) for name in ("h1T", "h2T", "hid_lo", "hid_hi", "rows"))
                xT, xb = (bufs("xT"), bufs("xb")) if last_layer else (None, None)
                outT = bufs("outT") if last_layer else h2T
                bank0, bank1 = st.banks("bank0_", [P, HROWS], WIDTH), st.banks("bank1_", [P, HROWS], WIDTH)
                block = st.block()

                @block.sync
                def _(sp):
                    def load(g, n, q):
                        sp.wait_ge(attn_ready[q], n)
                        sp.dma_start(acc[q][:].rearrange("p k c -> p (k c)"), pick(attn_sums_g[l], g)
                                     ).then_inc(node_loaded[q], 16)
                        sp.wait_ge(center1_ready[q], n)
                        sp.dma_start(hT[q][:], pick(source_t, g)).then_inc(node_loaded[q], 16)
                        if last_layer:
                            sp.wait_ge(xb_ready[q], n)
                            sp.dma_start(xT[q][:], pick(x_t, g)).then_inc(node_loaded[q], 16)

                    over_groups(sp, [load])

                if last_layer:
                    @block.gpsimd
                    def _(pool):
                        def add_bias(g, n, q):
                            pool.wait_ge(node_loaded[q], n * (16 * loads) + 16 * loads)
                            pool.wait_ge(rows_copied[q], n)
                            pool.nop(nofuse=True)
                            nc.gpsimd.tensor_scalar(xb[q][:], xT[q][:], layer_bias(l, "be2"), None, ALU.add
                                                    ).then_inc(xb_ready[q], 1)

                        over_groups(pool, [add_bias])

                @block.tensor
                def _(pe):
                    def turn(dst, src):
                        for m in range(TPH):
                            last = nc.tensor.transpose(dst[:, m * P:(m + 1) * P], src[:, m * P:(m + 1) * P], ident)
                        return last

                    def turn_attention(g, n, q):
                        pe.wait_ge(attn_ready[q], n + 1)
                        pe.wait_ge(rows_copied[q], n)
                        turn(bank0[q], attn[q][:].rearrange("p k c -> p (k c)")).then_inc(a_t, 1)

                    def center1(g, n, q):
                        pe.wait_ge(node_loaded[q], n * (16 * loads) + 16 * loads)
                        pe.wait_ge(a_t_copied, g + 1)
                        nc.tensor.matmul(bank1[q][:], center, hT[q][:], start=True, stop=False)
                        nc.tensor.matmul(bank1[q][:], centered[:, l, 0, :], aT[q][:], start=False, stop=True
                                         ).then_inc(center1_ready[q], 1)

                    def variance(k):
                        def stage(g, n, q):
                            pe.wait_ge(sq_ready[k], g + 1)
                            nc.tensor.matmul((bank0, bank1)[k > 0][q][:], average, sq[q][:], start=True, stop=True
                                             ).then_inc(var_ready[k], 1)
                        return stage

                    def hidden(g, n, q):
                        pe.wait_ge(h_ready[0], g + 1)
                        nc.tensor.matmul(bank0[q][:], layer(l, "w1_lo"), h1T[q][:], start=True, stop=True)
                        nc.tensor.matmul(bank1[q][:], layer(l, "w1_hi"), h1T[q][:], start=True, stop=True
                                         ).then_inc(hid_ready, 1)

                    def center2(g, n, q):
                        pe.wait_ge(hid_lo_copied, g + 1)
                        nc.tensor.matmul(bank0[q][:], center, h1T[q][:], start=True, stop=False)
                        nc.tensor.matmul(bank0[q][:], centered[:, l, 1, :], hid_lo[q][:], start=False, stop=False)
                        pe.wait_ge(hid_hi_copied, g + 1)
                        nc.tensor.matmul(bank0[q][:], centered[:, l, 2, :], hid_hi[q][:], start=False, stop=True
                                         ).then_inc(center2_ready, 1)

                    def center3(g, n, q):
                        pe.wait_ge(h_ready[1], g + 1)
                        nc.tensor.matmul(bank0[q][:], center, h2T[q][:], start=True, stop=True
                                         ).then_inc(center3_ready, 1)

                    def turn_out(g, n, q):
                        pe.wait_ge(norm_ready[2] if last_layer else h_ready[1], g + 1)
                        turn(bank0[q], outT[q]).then_inc(rows_t, 1)

                    stages = [turn_attention, center1, variance(0), hidden, center2, variance(1)]
                    if last_layer:
                        stages += [center3, variance(2)]
                    over_groups(pe, stages + [turn_out])

                @block.scalar
                def _(act):
                    nc.scalar.preload_act_table_set(ACT_SET)

                    def square(k):
                        bank = (bank1, bank0, bank0)[k]

                        def stage(g, n, q):
                            if k == 0:
                                act.wait_ge(center1_ready[q], n + 1)
                            else:
                                act.wait_ge((center2_ready, center3_ready)[k - 1], g + 1)
                            if k < 2:
                                ins = nc.scalar.activation(sq[q][:], bank[q][:], ACT.Square,
                                                           bias=centered_b[:, l, k:k + 1])
                            else:
                                ins = nc.scalar.activation(sq[q][:], bank[q][:], ACT.Square)
                            ins.then_inc(sq_ready[k], 1)
                        return stage

                    def logarithm(k):
                        def stage(g, n, q):
                            act.wait_ge(var_ready[k], g + 1)
                            nc.scalar.activation(log[q][:], (bank0, bank1)[k > 0][q][:], ACT.Ln, bias=eps_col[:, 0:1]
                                                 ).then_inc(log_ready[k], 1)
                        return stage

                    def inverse_root(k):
                        def stage(g, n, q):
                            act.wait_ge(log_ready[k], g + 1)
                            nc.scalar.activation(rstd[q][:], log[q][:], ACT.Exp, scale=-0.5
                                                 ).then_inc(rstd_ready[k], 1)
                        return stage

                    def relu_lo(g, n, q):
                        act.wait_ge(hid_ready, g + 1)
                        nc.scalar.activation(hid_lo[q][:], bank0[q][:], ACT.Relu, bias=layer_bias(l, "b1")
                                             ).then_inc(hid_lo_copied, 1)

                    def store_t(g, n, q):
                        act.wait_ge(norm_ready[2] if last_layer else h_ready[1], g + 1)
                        act.dma_start(pick(target_t, g), outT[q][:]).then_inc(t_stored[q], 16)

                    def copy_rows(g, n, q):
                        act.wait_ge(rows_t, g + 1)
                        act.wait_ge(rows_stored[q], n * 16)
                        nc.scalar.activation(rows[q][:], bank0[q][:], ACT.Copy).then_inc(rows_copied[q], 1)

                    def store_rows(g, n, q):
                        act.wait_ge(rows_copied[q], n + 1)
                        act.dma_start(pick(target, g), rows[q][:]).then_inc(rows_stored[q], 16)

                    def norm_stages(k):
                        return [square(k), logarithm(k), inverse_root(k)]

                    stages = [*norm_stages(0), relu_lo, *norm_stages(1)]
                    if last_layer:
                        stages += norm_stages(2)
                    over_groups(act, stages + [store_t, copy_rows, store_rows])
                    for q in range(WIDTH):
                        act.wait_ge(rows_stored[q], 16 * turns_of(q))
                        act.wait_ge(t_stored[q], 16 * turns_of(q))

                @block.vector
                def _(dve):
                    def attention_rows(g, n, q):
                        dve.wait_ge(node_loaded[q], n * (16 * loads) + 16 * loads)
                        nc.vector.tensor_scalar(z[q][:], acc[q][:, :, D:MSG], EPS_Z, None, ALU.add
                                                ).then_inc(z_ready, 1)
                        dve.wait_ge(z_ready, g + 1)
                        nc.vector.reciprocal(rz[q][:], z[q][:]).then_inc(rz_ready, 1)
                        dve.wait_ge(rz_ready, g + 1)
                        nc.vector.tensor_tensor(attn[q][:].rearrange("p k (h c) -> p k h c", c=DH),
                                                acc[q][:, :, 0:D].rearrange("p k (h c) -> p k h c", c=DH),
                                                rz[q][:].unsqueeze(3).broadcast_to([P, TPG, HEADS, DH]),
                                                ALU.mult).then_inc(attn_ready[q], 1)

                    def copy_a(g, n, q):
                        dve.wait_ge(a_t, g + 1)
                        nc.vector.tensor_copy(aT[q][:], bank0[q][:]).then_inc(a_t_copied, 1)

                    def normed(k):
                        def stage(g, n, q):
                            dve.wait_ge(rstd_ready[k], g + 1)
                            if k == 2 or (k == 1 and not last_layer):
                                dve.wait_ge(t_stored[q], n * 16)
                            if k == 2:
                                nc.vector.tensor_tensor(outT[q][:], bank0[q][:], rstd[q][:], ALU.mult
                                                        ).then_inc(norm_ready[k], 1)
                                return
                            nc.vector.scalar_tensor_tensor(norm[q][:], (bank1, bank0)[k][q][:],
                                                           centered_b[:, l, k:k + 1], rstd[q][:], ALU.add, ALU.mult
                                                           ).then_inc(norm_ready[k], 1)
                            dve.wait_ge(norm_ready[k], g + 1)
                            if k == 1 and last_layer:
                                dve.wait_ge(xb_ready[q], n + 1)
                                nc.vector.scalar_tensor_tensor(h2T[q][:], norm[q][:], layer_bias(l, "g2"), xb[q][:],
                                                               ALU.mult, ALU.add).then_inc(h_ready[k], 1)
                                return
                            nc.vector.tensor_scalar((h1T, h2T)[k][q][:], norm[q][:],
                                                    layer_bias(l, ("g1", "g2")[k]), layer_bias(l, ("be1", "be2")[k]),
                                                    ALU.mult, ALU.add).then_inc(h_ready[k], 1)
                        return stage

                    def relu_hi(g, n, q):
                        dve.wait_ge(hid_ready, g + 1)
                        nc.vector.tensor_scalar(hid_hi[q][:], bank1[q][:], layer_bias(l, "b1"), 0.0, ALU.add, ALU.max
                                                ).then_inc(hid_hi_copied, 1)

                    over_groups(dve, [attention_rows, copy_a, normed(0), relu_hi] + [normed(k) for k in
                                                                                     range(1, norms)])

        for l in range(LAYERS):
            attention(l)
            nodes(l)

        def bn_affine(dve, act, stats, affine, step, g, be):
            if dve is not None:
                nc.vector.bn_aggr(affine[:, 0:2], stats[:]).then_inc(step, 1)
                dve.wait_ge(step, 3)
                nc.vector.tensor_tensor(affine[:, 4:5], affine[:, 3:4], mlp_bias(g), ALU.mult).then_inc(step, 1)
                dve.wait_ge(step, 4)
                nc.vector.tensor_tensor(affine[:, 6:7], affine[:, 0:1], affine[:, 4:5], ALU.mult).then_inc(step, 1)
                dve.wait_ge(step, 5)
                nc.vector.tensor_tensor(affine[:, 5:6], mlp_bias(be), affine[:, 6:7], ALU.subtract).then_inc(step, 1)
            if act is not None:
                act.wait_ge(step, 1)
                nc.scalar.activation(affine[:, 2:3], affine[:, 1:2], ACT.Ln, bias=eps_col[:, 0:1]).then_inc(step, 1)
                act.wait_ge(step, 2)
                nc.scalar.activation(affine[:, 3:4], affine[:, 2:3], ACT.Exp, scale=-0.5).then_inc(step, 1)

        assert EPS_BN == EPS_LN

        with Stage("edge_hidden") as st:
            halves = 2 * groups_e
            idx_loaded, gathered, ea_loaded = (st.sems("idx_loaded", WIDTH), st.sems("gathered", WIDTH),
                                               st.sems("ea_loaded", WIDTH))
            src_t, src_t_copied, hid_ready = (st.sems("src_t", WIDTH), st.sems("src_t_copied", WIDTH),
                                              st.sems("hid_ready", WIDTH))
            hid_copied, hid_stats, hid_stored = (st.sems("hid_copied", WIDTH), st.sems("hid_stats", WIDTH),
                                                 st.sems("hid_stored", WIDTH))
            affine_step = st.sem("affine_step")

            idx = st.bufs("idx", [P, TPH], I32, WIDTH)
            src = st.bufs("src", [P, TPH, D], width=WIDTH)
            u = st.bufs("u", [P, HROWS], width=WIDTH)
            hid = st.bufs("hid", [P, HROWS], width=WIDTH)
            stats = st.sb("stats", [P, halves, 6])
            ps_t, ps_h = st.banks("ps_t", [P, HROWS], WIDTH), st.banks("ps_h", [P, HROWS], WIDTH)
            block = st.block()

            @block.sync
            def _(sp):
                def load(h, n, q):
                    sp.wait_ge(gathered[q], n * (TPH * 16))
                    sp.dma_start(idx[q][:], gather_idx[bass.ds(h, 1), :, 0:TPH].rearrange("a p c -> p (a c)")
                                 ).then_inc(idx_loaded[q], 16)
                    sp.wait_ge(hid_ready[q], n)
                    sp.dma_start(u[q][D:2 * D, :], pick(ea_t_h, h)).then_inc(ea_loaded[q], 16)
                over_groups(sp, [load], halves)

            @block.gpsimd
            def _(pool):
                def gather(h, n, q):
                    pool.wait_ge(idx_loaded[q], n * 16 + 16)
                    pool.wait_ge(src_t[q], n)
                    pool.nop(nofuse=True)
                    for k in range(TPH):
                        nc.gpsimd.indirect_dma_start(
                            src[q][:, k, :], None, x_mid, bass.IndirectOffsetOnAxis(ap=idx[q][:, k:k + 1], axis=0)
                        ).then_inc(gathered[q], 16)
                over_groups(pool, [gather], halves)

            @block.tensor
            def _(pe):
                def turn(h, n, q):
                    pe.wait_ge(gathered[q], n * (TPH * 16) + TPH * 16)
                    pe.wait_ge(src_t_copied[q], n)
                    pe.nop(nofuse=True)
                    for k in range(TPH):
                        last = nc.tensor.transpose(ps_t[q][0:D, k * P:(k + 1) * P], src[q][:, k, :], ident)
                    last.then_inc(src_t[q], 1)
                    pe.wait_ge(src_t_copied[q], n + 1)
                    pe.wait_ge(ea_loaded[q], n * 16 + 16)
                    pe.wait_ge(hid_copied[q], n)
                    nc.tensor.matmul(ps_h[q][:], mlp("w1a"), u[q][:], start=True, stop=True).then_inc(hid_ready[q], 1)
                over_groups(pe, [turn], halves)

            @block.scalar
            def _(act):
                nc.scalar.preload_act_table_set(ACT_SET)

                def bias(h, n, q):
                    act.wait_ge(hid_ready[q], n + 1)
                    act.wait_ge(hid_stats[q], n)
                    act.wait_ge(hid_stored[q], n * 16)
                    nc.scalar.activation(hid[q][:], ps_h[q][:], ACT.Identity, bias=mlp_bias("b1a")
                                         ).then_inc(hid_copied[q], 1)
                    act.wait_ge(hid_copied[q], n + 1)
                    act.dma_start(pick(edge_hid, h), hid[q][:]).then_inc(hid_stored[q], 16)
                over_groups(act, [bias], halves)
                for q in range(WIDTH):
                    act.wait_ge(hid_stored[q], 16 * turns_of(q, halves))
                bn_affine(None, act, stats, edge_affine, affine_step, "g1a", "be1a")

            @block.vector
            def _(dve):
                def statistics(h, n, q):
                    dve.wait_ge(src_t[q], n + 1)
                    dve.wait_ge(hid_ready[q], n)
                    nc.vector.tensor_copy(u[q][0:D, :], ps_t[q][0:D, :]).then_inc(src_t_copied[q], 1)
                    dve.wait_ge(hid_copied[q], n + 1)
                    nc.vector.bn_stats(stats[:, bass.ds(h, 1), :].rearrange("p a c -> p (a c)"), hid[q][:]
                                       ).then_inc(hid_stats[q], 1)
                over_groups(dve, [statistics], halves)
                for h in (halves - 2, halves - 1):
                    valid = min(HROWS, n_edges - h * HROWS)
                    assert valid > 0
                    q = h % WIDTH
                    dve.wait_ge(hid_stats[q], turns_of(q, halves))
                    nc.vector.bn_stats(stats[:, h, :], hid[q][:, 0:valid]).then_inc(hid_stats[q], 1)
                for q in range(WIDTH):
                    again = q in ((halves - 2) % WIDTH, (halves - 1) % WIDTH)
                    dve.wait_ge(hid_stats[q], turns_of(q, halves) + again)
                bn_affine(dve, None, stats, edge_affine, affine_step, "g1a", "be1a")

        with Stage("edge_sums") as st:
            dst_loaded, hid_loaded, same_ready = st.sems("dst_loaded"), st.sems("hid_loaded"), st.sems("same_ready")
            relu_ready, out_ready, out_copied = st.sems("relu_ready"), st.sems("out_ready"), st.sems("out_copied")
            sums_ready, sums_copied = st.sems("sums_ready"), st.sems("sums_copied")
            scatter_idx_ready = st.sems("scatter_idx_ready")
            added = [st.sems(f"added{t}_") for t in range(TABLES)]
            assert TPH == TABLES * TILES

            drow = st.bufs("drow", [P, HROWS], I32)
            dcol = st.bufs("dcol", [P, TPH], I32)
            same = st.bufs("same", [P, TPH, TILES * P])
            sidx = st.bufs("sidx", [P, TPH], I32)
            hid = st.bufs("hid", [P, HROWS])
            act_hid = st.bufs("act_hid", [P, HROWS])
            eo = st.bufs("eo", [P, TPH, HID])
            sums = st.bufs("sums", [P, TPH, HID])
            ps_o, ps_s = st.banks("ps_o", [P, TPH, HID]), st.banks("ps_s", [P, TPH, HID])
            block = st.block()

            @block.sync
            def _(sp):
                with sp.Fori(0, groups_e) as i:
                    for q in range(2):
                        sp.wait_ge(relu_ready[q], i)
                        sp.dma_start(hid[q][:], pick(edge_hid, i * 2 + q)).then_inc(hid_loaded[q], 16)
                        sp.wait_ge(same_ready[q], i)
                        sp.dma_start(dcol[q][:], pick(dst_col, i * 2 + q)).then_inc(dst_loaded[q], 16)
                        sp.dma_start(drow[q][:], row_of(dst_row[bass.ds(i * 2 + q, 1), :].rearrange("a c -> (a c)"))
                                     ).then_inc(dst_loaded[q], 16)

            @block.gpsimd
            def _(pool):
                with pool.Fori(0, groups_e) as i:
                    for q in range(2):
                        for t in range(TABLES):
                            if t == 0:
                                pool.wait_ge(sums_copied[q], i + 1)
                                pool.wait_ge(scatter_idx_ready[q], i + 1)
                            pool.wait_ge(added[t][1 - q], (i + q) * (TILES * 16))
                            pool.nop(nofuse=True)
                            for k in range(t * TILES, (t + 1) * TILES):
                                nc.gpsimd.indirect_dma_start(
                                    mlp_sums[t], bass.IndirectOffsetOnAxis(ap=sidx[q][:, k:k + 1], axis=0),
                                    sums[q][:, k, :], None, compute_op=ALU.add).then_inc(added[t][q], 16)
                for t in range(TABLES):
                    for q in range(2):
                        pool.wait_ge(added[t][q], groups_e * TILES * 16)

            @block.tensor
            def _(pe):
                with pe.Fori(0, groups_e) as i:
                    for q in range(2):
                        pe.wait_ge(relu_ready[q], i + 1)
                        pe.wait_ge(out_copied[q], i)
                        for k in range(TPH):
                            last = nc.tensor.matmul(ps_o[q][:, k, :], act_hid[q][:, k * P:(k + 1) * P], mlp("w2a"),
                                                    start=True, stop=True)
                        last.then_inc(out_ready[q], 1)
                        pe.wait_ge(same_ready[q], i + 1)
                        pe.wait_ge(out_copied[q], i + 1)
                        pe.wait_ge(sums_copied[q], i)
                        for k in range(TPH):
                            for t in range(TILES):
                                last = nc.tensor.matmul(
                                    ps_s[q][:, k, :],
                                    same[q][:, k // TILES * TILES + t, k % TILES * P:(k % TILES + 1) * P],
                                    eo[q][:, k // TILES * TILES + t, :], start=(t == 0), stop=(t == TILES - 1))
                        last.then_inc(sums_ready[q], 1)

            @block.scalar
            def _(act):
                nc.scalar.preload_act_table_set(ACT_SET)
                with act.Fori(0, groups_e) as i:
                    for q in range(2):
                        act.wait_ge(hid_loaded[q], i * 16 + 16)
                        act.wait_ge(out_ready[q], i)
                        nc.scalar.activation(act_hid[q][:], hid[q][:], ACT.Relu, bias=edge_affine[:, 5:6],
                                             scale=edge_affine[:, 4:5]).then_inc(relu_ready[q], 1)
                        act.wait_ge(sums_ready[q], i + 1)
                        for t in range(TABLES):
                            act.wait_ge(added[t][q], i * (TILES * 16))
                        nc.scalar.activation(sums[q][:], ps_s[q][:], ACT.Copy).then_inc(sums_copied[q], 1)

            @block.vector
            def _(dve):
                with dve.Fori(0, groups_e) as i:
                    for q in range(2):
                        dve.wait_ge(dst_loaded[q], i * 32 + 32)
                        dve.wait_ge(sums_ready[q], i)
                        same_destinations(same[q], drow[q], dcol[q]).then_inc(same_ready[q], 1)
                        dve.wait_ge(out_ready[q], i + 1)
                        nc.vector.tensor_tensor(eo[q][:], ps_o[q][:],
                                                b2a_rows[:].unsqueeze(1).broadcast_to([P, TPH, HID]),
                                                ALU.add).then_inc(out_copied[q], 1)
                        for t in range(TABLES):
                            dve.wait_ge(added[t][q], i * (TILES * 16))
                        nc.vector.tensor_copy(sidx[q][:], scatter_all[:, bass.ds(i * TPG + q * TPH, TPH)]
                                              ).then_inc(scatter_idx_ready[q], 1)

        with Stage("node_hidden") as st:
            loaded, summed, agg_t = st.sems("loaded", WIDTH), st.sems("summed", WIDTH), st.sems("agg_t", WIDTH)
            hid_ready, stats_ready, stored = (st.sems("hid_ready", WIDTH), st.sems("stats_ready", WIDTH),
                                              st.sems("stored", WIDTH))
            even_copied, odd_copied, even_ready, odd_ready = (st.sem("even_copied"), st.sem("odd_copied"),
                                                              st.sem("even_ready"), st.sem("odd_ready"))
            affine_step = st.sem("affine_step")
            loads = 1 + TABLES

            xT = st.bufs("xT", [P, HROWS], width=WIDTH)
            part = [st.bufs(f"part{t}_", [P, TPG * HID], width=WIDTH) for t in range(TABLES)]
            agg = st.bufs("agg", [P, TPG, HID], width=WIDTH)
            aggT = st.bufs("aggT", [P, 2, HROWS], width=WIDTH)
            hid = st.bufs("hid", [P, 2, HROWS], width=WIDTH)
            stats = st.sb("stats", [P, 2 * groups_n, 6])
            even, odd = st.banks("even", [P, HROWS], WIDTH), st.banks("odd", [P, HROWS], WIDTH)
            assert TABLES == 2
            block = st.block()

            @block.sync
            def _(sp):
                def load(g, n, q):
                    sp.wait_ge(summed[q], n)
                    for t in range(TABLES):
                        sp.dma_start(part[t][q][:], pick(mlp_sums_g[t], g)).then_inc(loaded[q], 16)
                    sp.wait_ge(hid_ready[q], n)
                    sp.dma_start(xT[q][:], pick(x_mid_t, g)).then_inc(loaded[q], 16)
                over_groups(sp, [load])

            @block.gpsimd
            def _(pool):
                def total(g, n, q):
                    pool.wait_ge(loaded[q], n * (16 * loads) + 16 * loads)
                    pool.wait_ge(agg_t[q], n)
                    nc.gpsimd.tensor_tensor(agg[q][:].rearrange("p k c -> p (k c)"), part[0][q][:], part[1][q][:],
                                            ALU.add).then_inc(summed[q], 1)
                over_groups(pool, [total])

            @block.tensor
            def _(pe):
                def turn(g, n, q):
                    pe.wait_ge(summed[q], n + 1)
                    pe.wait_ge(stats_ready[q], n)
                    for j in range(TPG):
                        m = j // 2
                        last = nc.tensor.transpose((even, odd)[j % 2][q][:, m * P:(m + 1) * P], agg[q][:, j, :], ident)
                    last.then_inc(agg_t[q], 1)

                def hidden(g, n, q):
                    pe.wait_ge(loaded[q], n * (16 * loads) + 16 * loads)
                    pe.wait_ge(even_copied, g + 1)
                    nc.tensor.matmul(even[q][:], mlp("w1b_x_lo"), xT[q][:], start=True, stop=False)
                    nc.tensor.matmul(even[q][:], mlp("w1b_agg"), aggT[q][:, 0, :], start=False, stop=True)
                    pe.wait_ge(odd_copied, g + 1)
                    nc.tensor.matmul(odd[q][:], mlp("w1b_x_hi"), xT[q][:], start=True, stop=False)
                    nc.tensor.matmul(odd[q][:], mlp("w1b_agg"), aggT[q][:, 1, :], start=False, stop=True
                                     ).then_inc(hid_ready[q], 1)

                over_groups(pe, [turn, hidden])

            @block.scalar
            def _(act):
                nc.scalar.preload_act_table_set(ACT_SET)

                def copy_even(g, n, q):
                    act.wait_ge(agg_t[q], n + 1)
                    nc.scalar.activation(aggT[q][:, 0, :], even[q][:], ACT.Copy).then_inc(even_copied, 1)

                def bias_even(g, n, q):
                    act.wait_ge(hid_ready[q], n + 1)
                    act.wait_ge(stats_ready[q], n)
                    act.wait_ge(stored[q], n * 16)
                    nc.scalar.activation(hid[q][:, 0, :], even[q][:], ACT.Identity, bias=mlp_bias("b1b")
                                         ).then_inc(even_ready, 1)

                def store(g, n, q):
                    act.wait_ge(even_ready, g + 1)
                    act.wait_ge(odd_ready, g + 1)
                    act.dma_start(pick(node_hid, g), hid[q][:].rearrange("p s c -> p (s c)")).then_inc(stored[q], 16)

                over_groups(act, [copy_even, bias_even, store])
                for q in range(WIDTH):
                    act.wait_ge(stored[q], 16 * turns_of(q))
                bn_affine(None, act, stats, node_affine, affine_step, "g1b", "be1b")

            @block.vector
            def _(dve):
                def copy_odd(g, n, q):
                    dve.wait_ge(agg_t[q], n + 1)
                    nc.vector.tensor_copy(aggT[q][:, 1, :], odd[q][:]).then_inc(odd_copied, 1)

                def bias_odd(g, n, q):
                    dve.wait_ge(hid_ready[q], n + 1)
                    dve.wait_ge(stored[q], n * 16)
                    nc.vector.tensor_scalar(hid[q][:, 1, :], odd[q][:], mlp_bias("b1b"), None, ALU.add
                                            ).then_inc(odd_ready, 1)

                def statistics(g, n, q):
                    dve.wait_ge(even_ready, g + 1)
                    dve.wait_ge(odd_ready, g + 1)
                    dve.nop(nofuse=True)
                    for side in range(2):
                        last = nc.vector.bn_stats(
                            stats[:, bass.ds(g * 2 + side, 1), :].rearrange("p a c -> p (a c)"), hid[q][:, side, :])
                    last.then_inc(stats_ready[q], 1)

                over_groups(dve, [copy_odd, bias_odd, statistics])
                q_last = (groups_n - 1) % WIDTH
                left = n_nodes - (groups_n - 1) * ROWS
                assert left > 0 and left % TPG == 0
                for q in range(WIDTH):
                    dve.wait_ge(stats_ready[q], turns_of(q))
                for side in range(2):
                    last = nc.vector.bn_stats(stats[:, 2 * (groups_n - 1) + side, :],
                                              hid[q_last][:, side, :].rearrange("p (m c) -> p m c", c=P)
                                              [:, :, 0:left // TPG])
                last.then_inc(stats_ready[q_last], 1)
                dve.wait_ge(stats_ready[q_last], turns_of(q_last) + 1)
                bn_affine(dve, None, stats, node_affine, affine_step, "g1b", "be1b")

        with Stage("output") as st:
            loaded, relu_ready, out_ready = (st.sems("loaded", WIDTH), st.sems("relu_ready", WIDTH),
                                             st.sems("out_ready", WIDTH))
            bias_ready, y_ready, stored = (st.sems("bias_ready", WIDTH), st.sems("y_ready", WIDTH),
                                           st.sems("stored", WIDTH))
            total_ready, mean_ready, cen_ready, sq_ready, var_ready, log_ready, rstd_ready, res_ready = (
                st.sem(name) for name in ("total_ready", "mean_ready", "cen_ready", "sq_ready", "var_ready",
                                          "log_ready", "rstd_ready", "res_ready"))

            def bufs(name, *shape):
                return st.bufs(name, [P, *shape], width=WIDTH)

            xrow, xb, y, cen, sq, res = (bufs(name, TPG, D) for name in ("xrow", "xb", "y", "cen", "sq", "res"))
            hid, act_hid = bufs("hid", 2, HROWS), bufs("act_hid", 2, HROWS)
            total, mean, var, log, rstd = (bufs(name, TPG) for name in ("total", "mean", "var", "log", "rstd"))
            ps = st.banks("ps_y", [P, TPG, D], WIDTH)
            block = st.block()

            @block.sync
            def _(sp):
                def load(g, n, q):
                    sp.wait_ge(relu_ready[q], n)
                    sp.dma_start(hid[q][:].rearrange("p s c -> p (s c)"), pick(node_hid, g)).then_inc(loaded[q], 16)
                    sp.wait_ge(bias_ready[q], n)
                    sp.dma_start(xrow[q][:].rearrange("p k c -> p (k c)"), pick(x_mid_g, g)).then_inc(loaded[q], 16)
                over_groups(sp, [load])

            @block.gpsimd
            def _(pool):
                def bias(g, n, q):
                    pool.wait_ge(loaded[q], n * 32 + 32)
                    pool.wait_ge(y_ready[q], n)
                    nc.gpsimd.tensor_tensor(xb[q][:], xrow[q][:], b2b_rows[:].unsqueeze(1).broadcast_to([P, TPG, D]),
                                            ALU.add).then_inc(bias_ready[q], 1)
                over_groups(pool, [bias])

            @block.tensor
            def _(pe):
                def product(g, n, q):
                    pe.wait_ge(relu_ready[q], n + 1)
                    pe.wait_ge(y_ready[q], n)
                    for j in range(TPG):
                        m = j // 2
                        last = nc.tensor.matmul(ps[q][:, j, :], act_hid[q][:, j % 2, m * P:(m + 1) * P], mlp("w2b"),
                                                start=True, stop=True)
                    last.then_inc(out_ready[q], 1)
                over_groups(pe, [product])

            @block.scalar
            def _(act):
                nc.scalar.preload_act_table_set(ACT_SET)

                def relu(g, n, q):
                    act.wait_ge(loaded[q], n * 32 + 32)
                    act.wait_ge(out_ready[q], n)
                    nc.scalar.activation(act_hid[q][:], hid[q][:], ACT.Relu, bias=node_affine[:, 5:6],
                                         scale=node_affine[:, 4:5]).then_inc(relu_ready[q], 1)

                def square(g, n, q):
                    act.wait_ge(cen_ready, g + 1)
                    nc.scalar.activation(sq[q][:], cen[q][:], ACT.Square).then_inc(sq_ready, 1)

                def inverse_root(g, n, q):
                    act.wait_ge(var_ready, g + 1)
                    nc.scalar.activation(log[q][:], var[q][:], ACT.Ln, bias=eps_col[:, 0:1], scale=1.0 / D
                                         ).then_inc(log_ready, 1)
                    act.wait_ge(log_ready, g + 1)
                    nc.scalar.activation(rstd[q][:], log[q][:], ACT.Exp, scale=-0.5).then_inc(rstd_ready, 1)

                def store(g, n, q):
                    act.wait_ge(res_ready, g + 1)
                    act.dma_start(pick(out_g, g), res[q][:].rearrange("p k c -> p (k c)")).then_inc(stored[q], 16)
                over_groups(act, [relu, square, inverse_root, store])
                for q in range(WIDTH):
                    act.wait_ge(stored[q], 16 * turns_of(q))

            @block.vector
            def _(dve):
                def center_rows(g, n, q):
                    dve.wait_ge(out_ready[q], n + 1)
                    dve.wait_ge(bias_ready[q], n + 1)
                    nc.vector.tensor_tensor(y[q][:], ps[q][:], xb[q][:], ALU.add).then_inc(y_ready[q], 1)
                    dve.wait_ge(y_ready[q], n + 1)
                    nc.vector.tensor_reduce(total[q][:], y[q][:], AX.X, ALU.add).then_inc(total_ready, 1)
                    dve.wait_ge(total_ready, g + 1)
                    nc.vector.tensor_scalar(mean[q][:], total[q][:], 1.0 / D, None, ALU.mult).then_inc(mean_ready, 1)
                    dve.wait_ge(mean_ready, g + 1)
                    nc.vector.tensor_tensor(cen[q][:], y[q][:], mean[q][:].unsqueeze(2).broadcast_to([P, TPG, D]),
                                            ALU.subtract).then_inc(cen_ready, 1)

                def variance(g, n, q):
                    dve.wait_ge(sq_ready, g + 1)
                    nc.vector.tensor_reduce(var[q][:], sq[q][:], AX.X, ALU.add).then_inc(var_ready, 1)

                def scale(g, n, q):
                    dve.wait_ge(rstd_ready, g + 1)
                    dve.wait_ge(stored[q], n * 16)
                    nc.vector.tensor_tensor(res[q][:], cen[q][:], rstd[q][:].unsqueeze(2).broadcast_to([P, TPG, D]),
                                            ALU.mult).then_inc(res_ready, 1)
                over_groups(dve, [center_rows, variance, scale])


def _round(n, k):
    return (n + k - 1) // k * k


def host_arrays(inp):
    f = {k: np.asarray(v) for k, v in inp.items()}
    n, e = f["x"].shape[0], f["src"].shape[0]
    n_pad, e_pad = _round(n, ROWS), _round(e, ROWS)
    if n_pad == n:
        n_pad += ROWS
    halves = e_pad // HROWS
    x = np.zeros((n_pad, D), np.float32)
    x[:n] = f["x"]
    x_t = np.ascontiguousarray(x.reshape(-1, P, TPH, 2, D).transpose(0, 3, 4, 2, 1)).reshape(-1, P, HROWS)
    ea_t = np.zeros((D, e_pad), np.float32)
    ea_t[:, :e] = f["edge_attr_64"].T
    src = np.full(e_pad, n_pad - 1, np.int32)
    dst = np.full(e_pad, n_pad - 1, np.int32)
    src[:e], dst[:e] = f["src"], f["dst"]
    src_c = src.reshape(halves, TPH, P).transpose(0, 2, 1)
    dst_c = dst.reshape(halves, TPH, P).transpose(0, 2, 1)

    consts = np.zeros((P, N_CONSTS), np.float32)
    eye, pair = np.eye(P, dtype=np.float32), np.kron(np.eye(2), np.ones((D, D))).astype(np.float32) / D
    consts[:, 0:P], consts[:, P:2 * P], consts[:, 2 * P:3 * P] = eye, eye - pair, pair
    edge = np.arange(TILES * P)
    earlier = (edge[None, :] < edge[:, None]).astype(np.float32)
    consts[:, 3 * P:(3 + TILES * TILES) * P] = earlier.reshape(TILES, P, -1).transpose(1, 0, 2).reshape(P, -1)
    consts[:, (3 + TILES * TILES) * P:] = n_pad + np.arange(TPH) % TILES * P + np.arange(P)[:, None]

    layer_w = np.zeros((P, LAYERS, N_LAYER_W), np.float32)
    layer_b = np.zeros((P, LAYERS, len(LAYER_B)), np.float32)
    for l in range(LAYERS):
        w = {k: f[f"L0_gnn_{k}"][l] for k in ("WK", "WV", "WQ", "WE", "WO", "W1", "W2", "bO", "ln1_g", "ln1_b", "b1",
                                              "b2", "ln2_g", "ln2_b")}
        lw = layer_w[:, l]
        lw[:D, 0:D], lw[:D, D:2 * D], lw[D:, 2 * D:3 * D], lw[:D, 3 * D:4 * D] = w["WK"], w["WV"], w["WQ"], w["WE"]
        for r in range(2):
            lw[r * D:(r + 1) * D, 256 + r * D:256 + (r + 1) * D] = w["WO"].T
            lw[r * D:(r + 1) * D, 384 + r * P:384 + (r + 1) * P] = w["W1"]
            lw[r * D:(r + 1) * D, 640 + r * P:640 + (r + 1) * P] = w["W2"].T
        for k, name in enumerate(("bO", "ln1_g", "ln1_b", "b1", "b2", "ln2_g", "ln2_b")):
            layer_b[:, l, k] = w[name] if w[name].size == P else np.concatenate([w[name], w[name]])

    g = {k: f[f"L1_gnn_{k}"] for k in ("W1a", "b1a", "g1a", "be1a", "W2a", "b2a", "W1b", "b1b", "g1b", "be1b", "W2b",
                                       "b2b")}
    mlp_w = np.zeros((P, N_MLP_W), np.float32)
    mlp_w[:, 0:P], mlp_w[:, P:2 * P] = g["W1a"], g["W2a"]
    mlp_w[:D, 2 * P:3 * P], mlp_w[D:, 3 * P:4 * P] = g["W1b"][:D], g["W1b"][:D]
    mlp_w[:, 4 * P:5 * P], mlp_w[:, 5 * P:] = g["W1b"][D:], g["W2b"]
    mlp_b = np.stack([g[k] for k in MLP_B], axis=1)
    mlp_rows = np.zeros((2, HID), np.float32)
    mlp_rows[0], mlp_rows[1, :D] = g["b2a"], g["b2b"]
    return dict(x=x, x_t=x_t, ea_t=ea_t, gather_idx=np.ascontiguousarray(np.concatenate([src_c, dst_c], axis=2)),
                dst_row=dst.reshape(halves, HROWS), dst_col=np.ascontiguousarray(dst_c), consts=consts,
                layer_w=layer_w, layer_b=layer_b, mlp_w=mlp_w, mlp_b=np.ascontiguousarray(mlp_b), mlp_rows=mlp_rows)


def kernel(**inputs):
    import concourse.bacc as bacc
    from concourse.bass_utils import run_bass_kernel_spmd

    n, e = inputs["x"].shape[0], inputs["src"].shape[0]
    arrays = host_arrays(inputs)
    nc = bacc.Bacc("TRN2", target_bir_lowering=False, num_devices=1)
    args = {k: nc.dram_tensor(f"in_{k}", a.shape, mybir.dt.from_np(a.dtype), kind="ExternalInput").ap()
            for k, a in arrays.items()}
    out = nc.dram_tensor("out_nodes", arrays["x"].shape, F32, kind="ExternalOutput").ap()
    build(nc, n, e, *args.values(), out)
    r = run_bass_kernel_spmd(nc, [{f"in_{k}": a for k, a in arrays.items()}], core_ids=[0])
    return r.results[0]["out_nodes"][:n]
```

```python
from contextlib import ExitStack

import numpy as np

import concourse.bass as bass
from concourse import mybir

P = 128
D = 64
HEADS = 4
DH = D // HEADS
HID = 2 * D
LAYERS = 2
MSG = D + HEADS
TPG = 8
TPH = TPG // 2
ROWS = TPG * P
HROWS = TPH * P
PARTS = 3
TABLES = 2
SPARE = HROWS
WIDTH = 4
WIDE = 7
SCATTER_LAG = 3
ACT_SET = "natural_log_exp_and_others"
EPS_LN = 1e-5
EPS_BN = 1e-5
EPS_Z = 1e-6
CLIP = 5.0 * DH ** 0.5

ALU = mybir.AluOpType
ACT = mybir.ActivationFunctionType
AX = mybir.AxisListType
F32 = mybir.dt.float32
BF16 = mybir.dt.bfloat16
I32 = mybir.dt.int32

CONSTS = dict(ident=(0, P), center=(P, P), average=(2 * P, P),
              earlier=(3 * P, TPH * HROWS), spare=(3 * P + TPH * HROWS, TPH))
N_CONSTS = 3 * P + TPH * HROWS + TPH
LAYER_W = dict(kvq=(0, 3 * D), e=(3 * D, D), wo_t=(256, P), w1_lo=(384, P), w1_hi=(512, P),
               w2_t_lo=(640, P), w2_t_hi=(768, P))
N_LAYER_W = 896
LAYER_B = ("bo", "g1", "be1", "b1", "b2", "g2", "be2")
MLP_W = dict(w1a=(0, P), w2a=(P, P), w1b_x_lo=(2 * P, P), w1b_x_hi=(3 * P, P), w1b_agg=(4 * P, P), w2b=(5 * P, D))
N_MLP_W = 5 * P + D
MLP_B = ("b1a", "g1a", "be1a", "b1b", "g1b", "be1b")


def row_of(ap, p=P):
    return ap.partition_broadcast(p)


def build(nc, n_nodes, n_edges, x, x_t, ea_t, gather_idx, dst_row, dst_col, consts, layer_w, layer_b, mlp_w, mlp_b,
          mlp_rows, out):
    groups_n = x.shape[0] // ROWS
    groups_e = ea_t.shape[1] // ROWS
    n_pad = groups_n * ROWS
    table_rows = n_pad + SPARE
    halves = 2 * groups_e
    assert groups_e <= groups_n and WIDTH <= halves

    def dram(name, shape):
        return nc.dram_tensor(name, shape, F32, kind="Internal").ap()

    h_mid, h_mid_t = dram("h_mid", [n_pad, D]), dram("h_mid_t", [groups_n, P, HROWS])
    x_mid, x_mid_t = dram("x_mid", [n_pad, D]), dram("x_mid_t", [groups_n, P, HROWS])
    attn_sums = [dram(f"attn_sums{l}", [table_rows, MSG]) for l in range(LAYERS)]
    mlp_sums = [dram(f"mlp_sums{t}", [table_rows, HID]) for t in range(TABLES)]
    edge_hid = dram("edge_hid", [2 * groups_e, P, HROWS])
    node_hid = dram("node_hid", [groups_n, P, ROWS])

    def by_group(table):
        return table[0:n_pad, :].rearrange("(g p j) d -> g p (j d)", p=P, j=TPG)

    def spare_rows(table):
        return table[n_pad:table_rows, :].rearrange("(p j) d -> p (j d)", p=P)

    def pick(ap, i):
        return ap[bass.ds(i, 1)].rearrange("a p c -> p (a c)")

    h_mid_g, x_mid_g, out_g = by_group(h_mid), by_group(x_mid), by_group(out)
    attn_sums_g = [by_group(t) for t in attn_sums]
    mlp_sums_g = [by_group(t) for t in mlp_sums]
    ea_t_h = ea_t.rearrange("d (h c) -> h d c", c=HROWS)

    def over_groups(eng, stages, count=groups_n, width=WIDTH):
        def run(stage, first, n, size):
            pair = stage if isinstance(stage, tuple) else (stage,)
            for q in range(size + len(pair) - 1):
                for lag, part in enumerate(pair):
                    if 0 <= q - lag < size:
                        part(first + (q - lag), n, q - lag)

        def size_of(turn):
            return max(0, min(width, count - turn * width))

        def groups(first, n, size, next_size):
            for stage in stages:
                if isinstance(stage, tuple) and stage[0] == "ahead":
                    run(stage[1], first + width, n + 1, next_size)
                else:
                    run(stage, first, n, size)

        for stage in stages:
            if isinstance(stage, tuple) and stage[0] == "ahead":
                run(stage[1], 0, 0, size_of(0))
        loops = count // width - 1
        with eng.Fori(0, loops) as i:
            groups(i * width, i, width, width)
        for turn in range(loops, (count + width - 1) // width):
            groups(turn * width, turn, size_of(turn), size_of(turn + 1))

    def staggered(eng, stages, count, width=WIDTH):
        first, steps = width, count + max(lag for lag, _ in stages)
        loops = (count - first) // width

        def step(t):
            for lag, stage in stages:
                if 0 <= t - lag < count:
                    stage(t - lag, (t - lag) // width, (t - lag) % width)
        for t in range(first):
            step(t)
        with eng.Fori(0, loops) as i:
            for q in range(width):
                for lag, stage in stages:
                    stage(i * width + (first + q - lag), i + (first + q - lag) // width, (q - lag) % width)
        for t in range(first + loops * width, steps):
            step(t)

    def turns_of(q, count=groups_n, width=WIDTH):
        return count // width + (q < count % width)

    class Stage:

        def __init__(self, tag):
            self.tag = tag

        def __enter__(self):
            self.ctx = ExitStack()
            self.handles = []
            return self

        def sem(self, name):
            self.handles.append(nc.alloc_semaphore(f"{self.tag}_{name}"))
            return self.handles[-1]

        def sems(self, name, width=2):
            return [self.sem(f"{name}{q}") for q in range(width)]

        def sb(self, name, shape, dt=F32):
            return self.ctx.enter_context(nc.sbuf_tensor(f"{self.tag}_{name}", shape, dt))

        def bufs(self, name, shape, dt=F32, width=2):
            return [self.sb(f"{name}{q}", shape, dt) for q in range(width)]

        def banks(self, name, shape, width=2):
            return [self.ctx.enter_context(nc.psum_tensor(f"{self.tag}_{name}{q}", shape, F32)) for q in range(width)]

        def block(self):
            return self.ctx.enter_context(nc.Block())

        def __exit__(self, *failed):
            self.ctx.__exit__(*failed)
            if failed[0] is None:
                nc.clear_and_free_semaphores(self.handles)
                nc.all_engine_barrier()

    with ExitStack() as top:
        def sb(name, shape, dt=F32):
            return top.enter_context(nc.sbuf_tensor(name, shape, dt))

        cst = sb("cst", [P, N_CONSTS])
        lw = sb("lw", [P, LAYERS, N_LAYER_W])
        lb = sb("lb", [P, LAYERS, len(LAYER_B)])
        mw = sb("mw", [P, N_MLP_W])
        mb = sb("mb", [P, len(MLP_B)])
        b2a_rows = sb("b2a_rows", [P, HID])
        b2b_rows = sb("b2b_rows", [P, D])
        eps_col = sb("eps_col", [P, 1])
        centered = sb("centered", [P, LAYERS, 3, P])
        centered_b = sb("centered_b", [P, LAYERS, 2])
        scatter_all = sb("scatter_all", [P, groups_e * TPG], I32)
        zeros = sb("zeros", [P, TPG * HID])
        edge_affine = sb("edge_affine", [P, 8])
        node_affine = sb("node_affine", [P, 8])

        def const(name):
            a, n = CONSTS[name]
            return cst[:, a:a + n]

        def layer(l, name):
            a, n = LAYER_W[name]
            return lw[:, l, a:a + n]

        def layer_bias(l, name):
            k = LAYER_B.index(name)
            return lb[:, l, k:k + 1]

        def mlp(name):
            a, n = MLP_W[name]
            return mw[:, a:a + n]

        def mlp_bias(name):
            k = MLP_B.index(name)
            return mb[:, k:k + 1]

        ident = const("ident")
        center = const("center")
        average = const("average")

        with Stage("setup") as st:
            setup_loaded, zeros_set, spare_zero = st.sem("setup_loaded"), st.sem("zeros_set"), st.sem("spare_zero")
            weights_centered, weights_copied = st.sem("weights_centered"), st.sem("weights_copied")
            n_setup = 7
            ps_w = st.banks("ps_w", [P, 512])
            block = st.block()

            @block.sync
            def _(sp):
                for dst, src in ((cst[:], consts), (lw[:], layer_w), (lb[:], layer_b), (mw[:], mlp_w), (mb[:], mlp_b),
                                 (b2a_rows[:], row_of(mlp_rows[0, :])),
                                 (b2b_rows[:], row_of(mlp_rows[1, 0:D]))):
                    sp.dma_start(dst, src).then_inc(setup_loaded, 16)
                sp.wait_ge(zeros_set, 1)
                for table in (*attn_sums, *mlp_sums):
                    spare = spare_rows(table)
                    sp.dma_start(spare, zeros[:, 0:spare.shape[1]]).then_inc(spare_zero, 16)
                sp.wait_ge(spare_zero, 16 * (LAYERS + TABLES))

            @block.scalar
            def _(act):
                nc.scalar.preload_act_table_set(ACT_SET)

            @block.vector
            def _(dve):
                nc.vector.memset(eps_col[:], EPS_LN)
                nc.vector.memset(zeros[:], 0.0).then_inc(zeros_set, 1)
                dve.wait_ge(weights_centered, 1)
                for l in range(LAYERS):
                    nc.vector.tensor_copy(centered[:, l, :, :], ps_w[l][:, 0:3 * P].rearrange("p (k c) -> p k c", c=P))
                    nc.vector.tensor_copy(centered_b[:, l, :], ps_w[l][:, 3 * P:3 * P + 2]).then_inc(weights_copied, 1)
                dve.wait_ge(weights_copied, LAYERS)

            @block.tensor
            def _(pe):
                pe.wait_ge(setup_loaded, 16 * n_setup)
                for l in range(LAYERS):
                    for k, name in enumerate(("wo_t", "w2_t_lo", "w2_t_hi")):
                        nc.tensor.matmul(ps_w[l][:, k * P:(k + 1) * P], layer(l, name), center, start=True, stop=True)
                    for k, name in enumerate(("bo", "b2")):
                        last = nc.tensor.matmul(ps_w[l][:, 3 * P + k:3 * P + k + 1], center, layer_bias(l, name),
                                                start=True, stop=True)
                last.then_inc(weights_centered, 1)

        def attention(l):
            nodes = (x, h_mid)[l]
            with Stage(f"attention{l}") as st:
                idx_loaded, gathered, edge_loaded = (st.sems("idx_loaded", WIDTH), st.sems("gathered", WIDTH),
                                                     st.sems("edge_loaded", WIDTH))
                pair_t, kvqe_ready, kqe_ready = (st.sems("pair_t", WIDTH), st.sems("kvqe_ready", WIDTH),
                                                 st.sems("kqe_ready", WIDTH))
                same_ready, writer_step, scatter_idx_ready = (st.sems("same_ready", WIDTH),
                                                              st.sems("writer_step", WIDTH),
                                                              st.sems("scatter_idx_ready", WIDTH))
                exp_ready, sums_ready, scattered = (st.sems("exp_ready", WIDTH), st.sems("sums_ready", WIDTH),
                                                    st.sems("scattered", WIDTH))
                pair_t_copied, qe_copied, kq_ready, dot_ready, clipped = (
                    st.sem(name) for name in ("pair_t_copied", "qe_copied", "kq_ready", "dot_ready", "clipped"))
                msg_ready, part0_ready, rest_ready, part1_ready, parts_ready = (
                    st.sem(name) for name in ("msg_ready", "part0_ready", "rest_ready", "part1_ready", "parts_ready"))
                sums_copied, table_zero, later_zero = st.sem("sums_copied"), st.sem("table_zero"), st.sem("later_zero")

                def bufs(name, shape, dt=F32):
                    return st.bufs(name, shape, dt, WIDTH)

                idx = bufs("idx", [P, 2 * TPH], I32)
                pair = bufs("pair", [P, TPH, 2 * D])
                pairT = bufs("pairT", [P, HROWS])
                ea = bufs("ea", [D, HROWS])
                drow = bufs("drow", [P, HROWS], I32)
                dcol = bufs("dcol", [P, TPH], I32)
                same = bufs("same", [P, TPH, HROWS], BF16)
                earlier = bufs("earlier", [P, TPH, HROWS], BF16) if l == 0 else None
                count, offset, masked = (bufs(name, [P, TPH]) for name in ("count", "offset", "masked"))
                sidx = bufs("sidx", [P, TPH], I32)
                qe = bufs("qe", [P, TPH, 2 * D])
                kq, kqe = bufs("kq", [P, TPH, D]), bufs("kqe", [P, TPH, D])
                dot, dotc = bufs("dot", [P, TPH * HEADS]), bufs("dotc", [P, TPH, HEADS])
                msg, sums = bufs("msg", [P, TPH, MSG]), bufs("sums", [P, TPH, MSG])
                rest, parts = bufs("rest", [P, TPH, MSG]), bufs("parts", [P, TPH, PARTS, MSG], BF16)
                ps_t = st.banks("ps_t", [P, HROWS])
                ps_kvqe = st.banks("ps_kvqe", [P, TPH, 4 * D])
                ps_s = st.banks("ps_s", [P, 512])
                block = st.block()

                @block.sync
                def _(sp):
                    def load(h, n, q):
                        sp.wait_ge(gathered[q], n * (2 * TPH * 16))
                        sp.dma_start(idx[q][:], pick(gather_idx, h)).then_inc(idx_loaded[q], 16)
                        sp.wait_ge(kvqe_ready[q], n)
                        sp.dma_start(ea[q][:], pick(ea_t_h, h)).then_inc(edge_loaded[q], 16)
                        if l == 0:
                            sp.wait_ge(writer_step[q], n * 3)
                        sp.wait_ge(same_ready[q], n)
                        sp.nop(nofuse=True)
                        sp.dma_start(dcol[q][:], pick(dst_col, h)).then_inc(edge_loaded[q], 16)
                        sp.dma_start(drow[q][:], row_of(dst_row[bass.ds(h, 1), :].rearrange("a c -> (a c)"))
                                     ).then_inc(edge_loaded[q], 16)

                    def zero(g):
                        for table in (attn_sums_g[1], *mlp_sums_g):
                            sp.dma_start(pick(table, g), zeros[:, 0:table.shape[2]]).then_inc(later_zero, 16)

                    for h in range(WIDTH):
                        load(h, 0, h)
                    if l == 0:
                        with sp.Fori(0, groups_n) as g:
                            sp.dma_start(pick(attn_sums_g[0], g), zeros[:, 0:TPG * MSG]).then_inc(table_zero, 16)
                    with sp.Fori(0, halves // WIDTH - 1) as i:
                        for q in range(WIDTH):
                            load(i * WIDTH + (WIDTH + q), i + 1, q)
                            if l == 0 and q % 2 == 1:
                                zero(i * (WIDTH // 2) + q // 2)
                    for h in range(halves // WIDTH * WIDTH, halves):
                        load(h, h // WIDTH, h % WIDTH)
                    if l == 0:
                        for g in range((halves // WIDTH - 1) * (WIDTH // 2), groups_n):
                            zero(g)
                        sp.wait_ge(later_zero, 16 * groups_n * (1 + TABLES))

                @block.gpsimd
                def _(pool):
                    def gather(h, n, q):
                        pool.wait_ge(idx_loaded[q], n * 16 + 16)
                        pool.wait_ge(pair_t[q], n)
                        pool.nop(nofuse=True)
                        for k in range(TPH):
                            for side in range(2):
                                nc.gpsimd.indirect_dma_start(
                                    pair[q][:, k, side * D:(side + 1) * D], None, nodes,
                                    bass.IndirectOffsetOnAxis(ap=idx[q][:, side * TPH + k:side * TPH + k + 1], axis=0)
                                ).then_inc(gathered[q], 16)

                    def scatter(h, n, q):
                        if l == 0 and isinstance(h, int) and h == 0:
                            pool.wait_ge(table_zero, groups_n * 16)
                        pool.wait_ge(sums_copied, h + 1)
                        pool.wait_ge(scatter_idx_ready[q], n + 1)
                        pool.wait_ge(scattered[(q - 1) % WIDTH], (n + (q >= 1)) * (TPH * 16))
                        pool.nop(nofuse=True)
                        for k in range(TPH):
                            nc.gpsimd.indirect_dma_start(
                                attn_sums[l], bass.IndirectOffsetOnAxis(ap=sidx[q][:, k:k + 1], axis=0),
                                sums[q][:, k, :], None, compute_op=ALU.add).then_inc(scattered[q], 16)

                    staggered(pool, [(0, gather), (SCATTER_LAG, scatter)], halves)
                    for q in range(WIDTH):
                        pool.wait_ge(scattered[q], turns_of(q, halves) * (TPH * 16))

                @block.tensor
                def _(pe):
                    def turn(h, n, q):
                        pe.wait_ge(gathered[q], n * (2 * TPH * 16) + 2 * TPH * 16)
                        bank = q % 2
                        for k in range(TPH):
                            last = nc.tensor.transpose(ps_t[bank][:, k * P:(k + 1) * P], pair[q][:, k, :], ident)
                        last.then_inc(pair_t[q], 1)

                    def kvqe(h, n, q):
                        pe.wait_ge(pair_t_copied, h + 1)
                        pe.wait_ge(edge_loaded[q], n * 48 + 48)
                        for k in range(TPH):
                            nc.tensor.matmul(ps_kvqe[q % 2][:, k, 0:3 * D], pairT[q][:, k * P:(k + 1) * P],
                                             layer(l, "kvq"), start=True, stop=True)
                            last = nc.tensor.matmul(ps_kvqe[q % 2][:, k, 3 * D:4 * D], ea[q][:, k * P:(k + 1) * P],
                                                    layer(l, "e")[0:D, :], start=True, stop=True)
                        last.then_inc(kvqe_ready[q], 1)

                    def sum_up(h, n, q):
                        pe.wait_ge(same_ready[q], n + 1)
                        pe.wait_ge(parts_ready, h + 1)
                        if not isinstance(h, int) or h >= 2:
                            pe.wait_ge(sums_copied, h - 1)
                        for k in range(TPH):
                            for t in range(TPH):
                                for part in range(PARTS):
                                    last = nc.tensor.matmul(
                                        ps_s[q % 2][:, k * MSG:(k + 1) * MSG], same[q][:, t, k * P:(k + 1) * P],
                                        parts[q][:, t, part, :], start=(t == 0 and part == 0),
                                        stop=(t == TPH - 1 and part == PARTS - 1))
                        last.then_inc(sums_ready[q], 1)

                    staggered(pe, [(0, turn), (0, kvqe), (1, sum_up)], halves)

                @block.scalar
                def _(act):
                    nc.scalar.preload_act_table_set(ACT_SET)

                    def copy_pair(h, n, q):
                        act.wait_ge(pair_t[q], n + 1)
                        act.wait_ge(kvqe_ready[q], n)
                        nc.scalar.activation(pairT[q][:], ps_t[q % 2][:], ACT.Copy).then_inc(pair_t_copied, 1)

                    def copy_qe(h, n, q):
                        act.wait_ge(kvqe_ready[q], n + 1)
                        act.wait_ge(kqe_ready[q], n)
                        nc.scalar.activation(qe[q][:], ps_kvqe[q % 2][:, :, 2 * D:4 * D], ACT.Copy
                                             ).then_inc(qe_copied, 1)

                    def score(h, n, q):
                        act.wait_ge(clipped, h + 1)
                        act.wait_ge(sums_ready[q], n)
                        nc.scalar.activation(msg[q][:, :, D:MSG], dotc[q][:], ACT.Exp, scale=DH ** -0.5
                                             ).then_inc(exp_ready[q], 1)

                    def split(h, n, q):
                        act.wait_ge(msg_ready, h + 1)
                        nc.scalar.activation(parts[q][:, :, 0, :], msg[q][:], ACT.Copy).then_inc(part0_ready, 1)
                        act.wait_ge(rest_ready, h + 1)
                        nc.scalar.activation(parts[q][:, :, 1, :], rest[q][:], ACT.Copy).then_inc(part1_ready, 1)

                    def copy_sums(h, n, q):
                        act.wait_ge(sums_ready[q], n + 1)
                        act.wait_ge(scattered[q], n * (TPH * 16))
                        nc.scalar.activation(sums[q][:], ps_s[q % 2][:, 0:TPH * MSG].rearrange(
                            "p (k c) -> p k c", c=MSG), ACT.Copy).then_inc(sums_copied, 1)

                    staggered(act, [(0, copy_pair), (0, copy_qe), (0, score), (0, split), (1, copy_sums)],
                              halves)

                @block.vector
                def _(dve):
                    def compare(h, n, q):
                        dve.wait_ge(edge_loaded[q], n * 48 + 48)
                        dve.wait_ge(sums_ready[q], n)
                        same_destinations(same[q], drow[q], dcol[q]).then_inc(same_ready[q], 1)

                    def writer(h, n, q):
                        dve.wait_ge(same_ready[q], n + 1)
                        nc.vector.tensor_tensor(earlier[q][:].rearrange("p t c -> p (t c)"),
                                                same[q][:].rearrange("p t c -> p (t c)"), const("earlier"), ALU.mult)
                        nc.vector.tensor_tensor(offset[q][:], dcol[q][:], const("spare"), ALU.subtract
                                                ).then_inc(writer_step[q], 1)
                        dve.wait_ge(writer_step[q], n * 3 + 1)
                        nc.vector.tensor_reduce(count[q][:], earlier[q][:], AX.X, ALU.add).then_inc(writer_step[q], 1)
                        dve.wait_ge(writer_step[q], n * 3 + 2)
                        nc.vector.scalar_tensor_tensor(masked[q][:], count[q][:], 0.0, offset[q][:],
                                                       ALU.is_equal, ALU.mult).then_inc(writer_step[q], 1)
                        dve.wait_ge(writer_step[q], n * 3 + 3)
                        nc.vector.tensor_tensor(scatter_all[:, bass.ds(h * TPH, TPH)], masked[q][:], const("spare"),
                                                ALU.add)

                    def scores(h, n, q):
                        dve.wait_ge(qe_copied, h + 1)
                        nc.vector.tensor_tensor(kq[q][:], ps_kvqe[q % 2][:, :, 0:D], qe[q][:, :, 0:D], ALU.mult
                                                ).then_inc(kq_ready, 1)
                        dve.wait_ge(kq_ready, h + 1)
                        nc.vector.tensor_tensor(kqe[q][:], kq[q][:], qe[q][:, :, D:2 * D], ALU.mult
                                                ).then_inc(kqe_ready[q], 1)
                        dve.wait_ge(kqe_ready[q], n + 1)
                        nc.vector.tensor_reduce(dot[q][:], kqe[q][:].rearrange("p k (h c) -> p (k h) c", c=DH),
                                                AX.X, ALU.add).then_inc(dot_ready, 1)
                        dve.wait_ge(dot_ready, h + 1)
                        dve.wait_ge(exp_ready[q], n)
                        nc.vector.tensor_scalar(dotc[q][:].rearrange("p k h -> p (k h)"), dot[q][:], CLIP, -CLIP,
                                                ALU.min, ALU.max).then_inc(clipped, 1)

                    def messages(h, n, q):
                        dve.wait_ge(exp_ready[q], n + 1)
                        nc.vector.tensor_tensor(
                            msg[q][:, :, 0:D].rearrange("p k (h c) -> p k h c", c=DH),
                            ps_kvqe[q % 2][:, :, D:2 * D].rearrange("p k (h c) -> p k h c", c=DH),
                            msg[q][:, :, D:MSG].unsqueeze(3).broadcast_to([P, TPH, HEADS, DH]),
                            ALU.mult).then_inc(msg_ready, 1)
                        dve.wait_ge(part0_ready, h + 1)
                        nc.vector.tensor_tensor(rest[q][:], msg[q][:], parts[q][:, :, 0, :], ALU.subtract
                                                ).then_inc(rest_ready, 1)
                        dve.wait_ge(part1_ready, h + 1)
                        nc.vector.tensor_tensor(parts[q][:, :, 2, :], rest[q][:], parts[q][:, :, 1, :], ALU.subtract
                                                ).then_inc(parts_ready, 1)

                    def destinations(h, n, q):
                        dve.wait_ge(scattered[q], n * (TPH * 16))
                        if l == 0:
                            nc.vector.tensor_tensor(sidx[q][:], masked[q][:], const("spare"), ALU.add
                                                    ).then_inc(scatter_idx_ready[q], 1)
                        else:
                            nc.vector.tensor_copy(sidx[q][:], scatter_all[:, bass.ds(h * TPH, TPH)]
                                                  ).then_inc(scatter_idx_ready[q], 1)

                    staggered(dve, [(0, compare), *([(0, writer)] if l == 0 else []), (0, scores), (0, messages),
                                    (0, destinations)], halves)

        def same_destinations(same, drow, dcol):
            return nc.vector.tensor_tensor(same[:], drow[:].unsqueeze(1).broadcast_to([P, TPH, HROWS]),
                                           dcol[:].unsqueeze(2).broadcast_to([P, TPH, HROWS]), ALU.is_equal)

        def nodes(l):
            last_layer = l == LAYERS - 1
            norms = 3 if last_layer else 2
            source_t = (x_t, h_mid_t)[l]
            target, target_t = ((h_mid_g, h_mid_t), (x_mid_g, x_mid_t))[l]
            with Stage(f"nodes{l}") as st:
                node_loaded, attn_ready = st.sems("node_loaded", WIDE), st.sems("attn_ready", WIDE)
                center1_ready, xb_ready = st.sems("center1_ready", WIDE), st.sems("xb_ready", WIDE)
                rows_copied, rows_stored = st.sems("rows_copied", WIDE), st.sems("rows_stored", WIDE)
                t_stored, x_loaded = st.sems("t_stored", WIDE), st.sems("x_loaded", WIDE)
                z_ready, rz_ready, a_t, a_t_copied, rows_t = (
                    st.sem(name) for name in ("z_ready", "rz_ready", "a_t", "a_t_copied", "rows_t"))
                lo_ready, lo_copied, hi_ready, hi_copied = (
                    st.sem(name) for name in ("lo_ready", "lo_copied", "hi_ready", "hi_copied"))
                center2_ready, center3_ready = st.sem("center2_ready"), st.sem("center3_ready")
                sq_ready, cen_ready, var_ready, log_ready, rstd_ready, norm_ready, h_ready = (
                    [st.sem(f"{name}{k}_ready") for k in range(norms)]
                    for name in ("sq", "cen", "var", "log", "rstd", "norm", "h"))

                def bufs(name, shape=(P, HROWS)):
                    return st.bufs(name, list(shape), width=WIDE)

                acc, z, rz = bufs("acc", (P, TPG, MSG)), bufs("z", (P, TPG, HEADS)), bufs("rz", (P, TPG, HEADS))
                attn = bufs("attn", (P, TPG, D))
                hT, rstd, cen, h1T, h2T, rows = (bufs(name) for name in ("hT", "rstd", "cen", "h1T", "h2T", "rows"))
                hid_lo, hid_hi = bufs("hid_lo"), bufs("hid_hi")
                aT = hid_lo
                xb = bufs("xb") if last_layer else None
                outT = h1T if last_layer else h2T
                bank = st.banks("bank", [P, HROWS], WIDE)
                block = st.block()

                @block.sync
                def _(sp):
                    def load(g, n, q):
                        sp.wait_ge(attn_ready[q], n)
                        sp.dma_start(acc[q][:].rearrange("p k c -> p (k c)"), pick(attn_sums_g[l], g)
                                     ).then_inc(node_loaded[q], 16)
                        sp.wait_ge(center1_ready[q], n)
                        sp.dma_start(hT[q][:], pick(source_t, g)).then_inc(node_loaded[q], 16)

                    def load_x(g, n, q):
                        sp.wait_ge(rows_copied[q], n)
                        sp.dma_start(xb[q][:], pick(x_t, g)).then_inc(x_loaded[q], 16)

                    over_groups(sp, [("ahead", load), load_x] if last_layer else [load], width=WIDE)

                if last_layer:
                    @block.gpsimd
                    def _(pool):
                        def add_bias(g, n, q):
                            pool.wait_ge(x_loaded[q], n * 16 + 16)
                            pool.nop(nofuse=True)
                            nc.gpsimd.tensor_scalar(xb[q][:], xb[q][:], layer_bias(l, "be2"), None, ALU.add
                                                    ).then_inc(xb_ready[q], 1)

                        over_groups(pool, [add_bias], width=WIDE)

                @block.tensor
                def _(pe):
                    def turn(dst, src):
                        for m in range(TPH):
                            last = nc.tensor.transpose(dst[:, m * P:(m + 1) * P], src[:, m * P:(m + 1) * P], ident)
                        return last

                    def turn_attention(g, n, q):
                        pe.wait_ge(attn_ready[q], n + 1)
                        pe.wait_ge(rows_copied[q], n)
                        turn(bank[q], attn[q][:].rearrange("p k c -> p (k c)")).then_inc(a_t, 1)

                    def center1(g, n, q):
                        pe.wait_ge(node_loaded[q], n * 32 + 32)
                        pe.wait_ge(a_t_copied, g + 1)
                        nc.tensor.matmul(bank[q][:], center, hT[q][:], start=True, stop=False)
                        nc.tensor.matmul(bank[q][:], centered[:, l, 0, :], aT[q][:], start=False, stop=True
                                         ).then_inc(center1_ready[q], 1)

                    def variance(k):
                        def stage(g, n, q):
                            pe.wait_ge(sq_ready[k], g + 1)
                            nc.tensor.matmul(bank[q][:], average, rstd[q][:], start=True, stop=True
                                             ).then_inc(var_ready[k], 1)
                        return stage

                    def hidden_lo(g, n, q):
                        pe.wait_ge(h_ready[0], g + 1)
                        nc.tensor.matmul(bank[q][:], layer(l, "w1_lo"), h1T[q][:], start=True, stop=True
                                         ).then_inc(lo_ready, 1)

                    def hidden_hi(g, n, q):
                        pe.wait_ge(lo_copied, g + 1)
                        nc.tensor.matmul(bank[q][:], layer(l, "w1_hi"), h1T[q][:], start=True, stop=True
                                         ).then_inc(hi_ready, 1)

                    def center2(g, n, q):
                        pe.wait_ge(hi_copied, g + 1)
                        nc.tensor.matmul(bank[q][:], center, h1T[q][:], start=True, stop=False)
                        nc.tensor.matmul(bank[q][0:D, :], centered[:, l, 1, 0:D], hid_lo[q][:], start=False, stop=True)
                        nc.tensor.matmul(bank[q][D:P, :], centered[:, l, 2, D:P], hid_hi[q][:], start=False, stop=True
                                         ).then_inc(center2_ready, 1)

                    def center3(g, n, q):
                        pe.wait_ge(h_ready[1], g + 1)
                        nc.tensor.matmul(bank[q][:], center, h2T[q][:], start=True, stop=True
                                         ).then_inc(center3_ready, 1)

                    def turn_out(g, n, q):
                        pe.wait_ge(h_ready[norms - 1], g + 1)
                        turn(bank[q], outT[q]).then_inc(rows_t, 1)

                    stages = [turn_attention, center1, variance(0), hidden_lo, hidden_hi, center2, variance(1)]
                    if last_layer:
                        stages += [center3, variance(2)]
                    over_groups(pe, stages + [turn_out], width=WIDE)

                @block.scalar
                def _(act):
                    nc.scalar.preload_act_table_set(ACT_SET)

                    def square(k):
                        def stage(g, n, q):
                            act.wait_ge(cen_ready[k], g + 1)
                            nc.scalar.activation(rstd[q][:], cen[q][:], ACT.Square).then_inc(sq_ready[k], 1)
                        return stage

                    def logarithm(k):
                        def stage(g, n, q):
                            act.wait_ge(var_ready[k], g + 1)
                            nc.scalar.activation(rstd[q][:], bank[q][:], ACT.Ln, bias=eps_col[:, 0:1]
                                                 ).then_inc(log_ready[k], 1)
                        return stage

                    def inverse_root(k):
                        def stage(g, n, q):
                            act.wait_ge(log_ready[k], g + 1)
                            nc.scalar.activation(rstd[q][:], rstd[q][:], ACT.Exp, scale=-0.5
                                                 ).then_inc(rstd_ready[k], 1)
                        return stage

                    def relu_lo(g, n, q):
                        act.wait_ge(lo_ready, g + 1)
                        nc.scalar.activation(hid_lo[q][:], bank[q][:], ACT.Relu, bias=layer_bias(l, "b1")
                                             ).then_inc(lo_copied, 1)

                    def store_t(g, n, q):
                        act.wait_ge(h_ready[norms - 1], g + 1)
                        act.dma_start(pick(target_t, g), outT[q][:]).then_inc(t_stored[q], 16)

                    def copy_rows(g, n, q):
                        act.wait_ge(rows_t, g + 1)
                        act.wait_ge(rows_stored[q], n * 16)
                        nc.scalar.activation(rows[q][:], bank[q][:], ACT.Copy).then_inc(rows_copied[q], 1)

                    def store_rows(g, n, q):
                        act.wait_ge(rows_copied[q], n + 1)
                        act.dma_start(pick(target, g), rows[q][:]).then_inc(rows_stored[q], 16)

                    stages = [square(0), (logarithm(0), inverse_root(0)), relu_lo]
                    for k in range(1, norms):
                        stages += [square(k), (logarithm(k), inverse_root(k))]
                    over_groups(act, stages + [store_t, copy_rows, store_rows], width=WIDE)
                    for q in range(WIDE):
                        act.wait_ge(rows_stored[q], 16 * turns_of(q, width=WIDE))
                        act.wait_ge(t_stored[q], 16 * turns_of(q, width=WIDE))

                @block.vector
                def _(dve):
                    def attention_rows(g, n, q):
                        dve.wait_ge(node_loaded[q], n * 32 + 32)
                        nc.vector.tensor_scalar(z[q][:], acc[q][:, :, D:MSG], EPS_Z, None, ALU.add
                                                ).then_inc(z_ready, 1)
                        dve.wait_ge(z_ready, g + 1)
                        nc.vector.reciprocal(rz[q][:], z[q][:]).then_inc(rz_ready, 1)
                        dve.wait_ge(rz_ready, g + 1)
                        nc.vector.tensor_tensor(attn[q][:].rearrange("p k (h c) -> p k h c", c=DH),
                                                acc[q][:, :, 0:D].rearrange("p k (h c) -> p k h c", c=DH),
                                                rz[q][:].unsqueeze(3).broadcast_to([P, TPG, HEADS, DH]),
                                                ALU.mult).then_inc(attn_ready[q], 1)

                    def copy_a(g, n, q):
                        dve.wait_ge(a_t, g + 1)
                        nc.vector.tensor_copy(aT[q][:], bank[q][:]).then_inc(a_t_copied, 1)

                    def copy_centered(k):
                        def stage(g, n, q):
                            if k == 0:
                                dve.wait_ge(center1_ready[q], n + 1)
                            else:
                                dve.wait_ge((center2_ready, center3_ready)[k - 1], g + 1)
                            if k < 2:
                                ins = nc.vector.tensor_scalar(cen[q][:], bank[q][:], centered_b[:, l, k:k + 1], None,
                                                              ALU.add)
                            else:
                                ins = nc.vector.tensor_copy(cen[q][:], bank[q][:])
                            ins.then_inc(cen_ready[k], 1)
                        return stage

                    def scale(k):
                        def stage(g, n, q):
                            dve.wait_ge(rstd_ready[k], g + 1)
                            if k == 2:
                                nc.vector.tensor_tensor(outT[q][:], cen[q][:], rstd[q][:], ALU.mult
                                                        ).then_inc(h_ready[k], 1)
                                return
                            nc.vector.tensor_tensor(cen[q][:], cen[q][:], rstd[q][:], ALU.mult
                                                    ).then_inc(norm_ready[k], 1)
                        return stage

                    def shift(k):
                        def stage(g, n, q):
                            dve.wait_ge(norm_ready[k], g + 1)
                            if (k == 0 and last_layer) or (k == 1 and not last_layer):
                                dve.wait_ge(t_stored[q], n * 16)
                            if k == 1 and last_layer:
                                dve.wait_ge(xb_ready[q], n + 1)
                                nc.vector.scalar_tensor_tensor(h2T[q][:], cen[q][:], layer_bias(l, "g2"), xb[q][:],
                                                               ALU.mult, ALU.add).then_inc(h_ready[k], 1)
                                return
                            nc.vector.tensor_scalar((h1T, h2T)[k][q][:], cen[q][:],
                                                    layer_bias(l, ("g1", "g2")[k]), layer_bias(l, ("be1", "be2")[k]),
                                                    ALU.mult, ALU.add).then_inc(h_ready[k], 1)
                        return stage

                    def relu_hi(g, n, q):
                        dve.wait_ge(hi_ready, g + 1)
                        nc.vector.tensor_scalar(hid_hi[q][:], bank[q][:], layer_bias(l, "b1"), 0.0, ALU.add, ALU.max
                                                ).then_inc(hi_copied, 1)

                    stages = [copy_a, copy_centered(0), (scale(0), shift(0)), relu_hi, ("ahead", attention_rows),
                              copy_centered(1), (scale(1), shift(1))]
                    if last_layer:
                        stages += [copy_centered(2), scale(2)]
                    over_groups(dve, stages, width=WIDE)

        for l in range(LAYERS):
            attention(l)
            nodes(l)

        def bn_affine(dve, act, stats, affine, step, g, be):
            if dve is not None:
                nc.vector.bn_aggr(affine[:, 0:2], stats[:]).then_inc(step, 1)
                dve.wait_ge(step, 3)
                nc.vector.tensor_tensor(affine[:, 4:5], affine[:, 3:4], mlp_bias(g), ALU.mult).then_inc(step, 1)
                dve.wait_ge(step, 4)
                nc.vector.tensor_tensor(affine[:, 6:7], affine[:, 0:1], affine[:, 4:5], ALU.mult).then_inc(step, 1)
                dve.wait_ge(step, 5)
                nc.vector.tensor_tensor(affine[:, 5:6], mlp_bias(be), affine[:, 6:7], ALU.subtract).then_inc(step, 1)
            if act is not None:
                act.wait_ge(step, 1)
                nc.scalar.activation(affine[:, 2:3], affine[:, 1:2], ACT.Ln, bias=eps_col[:, 0:1]).then_inc(step, 1)
                act.wait_ge(step, 2)
                nc.scalar.activation(affine[:, 3:4], affine[:, 2:3], ACT.Exp, scale=-0.5).then_inc(step, 1)

        assert EPS_BN == EPS_LN

        with Stage("edge_hidden") as st:
            idx_loaded, gathered, ea_loaded = (st.sems("idx_loaded", WIDTH), st.sems("gathered", WIDTH),
                                               st.sems("ea_loaded", WIDTH))
            src_t, src_t_copied, hid_ready = (st.sems("src_t", WIDTH), st.sems("src_t_copied", WIDTH),
                                              st.sems("hid_ready", WIDTH))
            hid_copied, hid_stats, hid_stored = (st.sems("hid_copied", WIDTH), st.sems("hid_stats", WIDTH),
                                                 st.sems("hid_stored", WIDTH))
            affine_step = st.sem("affine_step")

            idx = st.bufs("idx", [P, TPH], I32, WIDTH)
            src = st.bufs("src", [P, TPH, D], width=WIDTH)
            u = st.bufs("u", [P, HROWS], width=WIDTH)
            hid = st.bufs("hid", [P, HROWS], width=WIDTH)
            stats = st.sb("stats", [P, halves, 6])
            ps_t, ps_h = st.banks("ps_t", [P, HROWS], WIDTH), st.banks("ps_h", [P, HROWS], WIDTH)
            block = st.block()

            @block.sync
            def _(sp):
                def load(h, n, q):
                    sp.wait_ge(gathered[q], n * (TPH * 16))
                    sp.dma_start(idx[q][:], gather_idx[bass.ds(h, 1), :, 0:TPH].rearrange("a p c -> p (a c)")
                                 ).then_inc(idx_loaded[q], 16)
                    sp.wait_ge(hid_ready[q], n)
                    sp.dma_start(u[q][D:2 * D, :], pick(ea_t_h, h)).then_inc(ea_loaded[q], 16)
                over_groups(sp, [load], halves)

            @block.gpsimd
            def _(pool):
                def gather(h, n, q):
                    pool.wait_ge(idx_loaded[q], n * 16 + 16)
                    pool.wait_ge(src_t[q], n)
                    pool.nop(nofuse=True)
                    for k in range(TPH):
                        nc.gpsimd.indirect_dma_start(
                            src[q][:, k, :], None, x_mid, bass.IndirectOffsetOnAxis(ap=idx[q][:, k:k + 1], axis=0)
                        ).then_inc(gathered[q], 16)
                over_groups(pool, [gather], halves)

            @block.tensor
            def _(pe):
                def turn(h, n, q):
                    pe.wait_ge(gathered[q], n * (TPH * 16) + TPH * 16)
                    pe.wait_ge(src_t_copied[q], n)
                    pe.nop(nofuse=True)
                    for k in range(TPH):
                        last = nc.tensor.transpose(ps_t[q][0:D, k * P:(k + 1) * P], src[q][:, k, :], ident)
                    last.then_inc(src_t[q], 1)
                    pe.wait_ge(src_t_copied[q], n + 1)
                    pe.wait_ge(ea_loaded[q], n * 16 + 16)
                    pe.wait_ge(hid_copied[q], n)
                    nc.tensor.matmul(ps_h[q][:], mlp("w1a"), u[q][:], start=True, stop=True).then_inc(hid_ready[q], 1)
                over_groups(pe, [turn], halves)

            @block.scalar
            def _(act):
                nc.scalar.preload_act_table_set(ACT_SET)

                def bias(h, n, q):
                    act.wait_ge(hid_ready[q], n + 1)
                    act.wait_ge(hid_stats[q], n)
                    act.wait_ge(hid_stored[q], n * 16)
                    nc.scalar.activation(hid[q][:], ps_h[q][:], ACT.Identity, bias=mlp_bias("b1a")
                                         ).then_inc(hid_copied[q], 1)
                    act.wait_ge(hid_copied[q], n + 1)
                    act.dma_start(pick(edge_hid, h), hid[q][:]).then_inc(hid_stored[q], 16)
                over_groups(act, [bias], halves)
                for q in range(WIDTH):
                    act.wait_ge(hid_stored[q], 16 * turns_of(q, halves))
                bn_affine(None, act, stats, edge_affine, affine_step, "g1a", "be1a")

            @block.vector
            def _(dve):
                def statistics(h, n, q):
                    dve.wait_ge(src_t[q], n + 1)
                    dve.wait_ge(hid_ready[q], n)
                    nc.vector.tensor_copy(u[q][0:D, :], ps_t[q][0:D, :]).then_inc(src_t_copied[q], 1)
                    dve.wait_ge(hid_copied[q], n + 1)
                    nc.vector.bn_stats(stats[:, bass.ds(h, 1), :].rearrange("p a c -> p (a c)"), hid[q][:]
                                       ).then_inc(hid_stats[q], 1)
                over_groups(dve, [statistics], halves)
                for h in (halves - 2, halves - 1):
                    valid = min(HROWS, n_edges - h * HROWS)
                    assert valid > 0
                    q = h % WIDTH
                    dve.wait_ge(hid_stats[q], turns_of(q, halves))
                    nc.vector.bn_stats(stats[:, h, :], hid[q][:, 0:valid]).then_inc(hid_stats[q], 1)
                for q in range(WIDTH):
                    again = q in ((halves - 2) % WIDTH, (halves - 1) % WIDTH)
                    dve.wait_ge(hid_stats[q], turns_of(q, halves) + again)
                bn_affine(dve, None, stats, edge_affine, affine_step, "g1a", "be1a")

        with Stage("edge_sums") as st:
            dst_loaded, hid_loaded, same_ready = (st.sems("dst_loaded", WIDTH), st.sems("hid_loaded", WIDTH),
                                                  st.sems("same_ready", WIDTH))
            relu_ready, out_ready, sums_ready = (st.sems("relu_ready", WIDTH), st.sems("out_ready", WIDTH),
                                                 st.sems("sums_ready", WIDTH))
            out_copied, sums_copied = st.sems("out_copied", WIDTH), st.sems("sums_copied", WIDTH)
            scatter_idx_ready, added = st.sems("scatter_idx_ready", WIDTH), st.sems("added", WIDTH)

            def bufs(name, shape, dt=F32):
                return st.bufs(name, shape, dt, WIDTH)

            drow, dcol, sidx = bufs("drow", [P, HROWS], I32), bufs("dcol", [P, TPH], I32), bufs("sidx", [P, TPH], I32)
            same = bufs("same", [P, TPH, HROWS])
            hid, act_hid = bufs("hid", [P, HROWS]), bufs("act_hid", [P, HROWS])
            eo, sums = bufs("eo", [P, TPH, HID]), bufs("sums", [P, TPH, HID])
            ps_o, ps_s = st.banks("ps_o", [P, TPH, HID], WIDTH), st.banks("ps_s", [P, TPH, HID], WIDTH)
            block = st.block()

            @block.sync
            def _(sp):
                def load(h, n, q):
                    sp.wait_ge(relu_ready[q], n)
                    sp.dma_start(hid[q][:], pick(edge_hid, h)).then_inc(hid_loaded[q], 16)
                    sp.wait_ge(same_ready[q], n)
                    sp.dma_start(dcol[q][:], pick(dst_col, h)).then_inc(dst_loaded[q], 16)
                    sp.dma_start(drow[q][:], row_of(dst_row[bass.ds(h, 1), :].rearrange("a c -> (a c)"))
                                 ).then_inc(dst_loaded[q], 16)
                over_groups(sp, [load], halves)

            @block.gpsimd
            def _(pool):
                def scatter(h, n, q):
                    pool.wait_ge(sums_copied[q], n + 1)
                    pool.wait_ge(scatter_idx_ready[q], n + 1)
                    pool.wait_ge(added[(q - TABLES) % WIDTH], (n + (q >= TABLES)) * (TPH * 16))
                    pool.nop(nofuse=True)
                    for k in range(TPH):
                        nc.gpsimd.indirect_dma_start(
                            mlp_sums[q % TABLES], bass.IndirectOffsetOnAxis(ap=sidx[q][:, k:k + 1], axis=0),
                            sums[q][:, k, :], None, compute_op=ALU.add).then_inc(added[q], 16)
                over_groups(pool, [scatter], halves)
                for q in range(WIDTH):
                    pool.wait_ge(added[q], turns_of(q, halves) * (TPH * 16))

            @block.tensor
            def _(pe):
                def outputs(h, n, q):
                    pe.wait_ge(relu_ready[q], n + 1)
                    pe.wait_ge(out_copied[q], n)
                    for k in range(TPH):
                        last = nc.tensor.matmul(ps_o[q][:, k, :], act_hid[q][:, k * P:(k + 1) * P], mlp("w2a"),
                                                start=True, stop=True)
                    last.then_inc(out_ready[q], 1)

                def sum_up(h, n, q):
                    pe.wait_ge(same_ready[q], n + 1)
                    pe.wait_ge(out_copied[q], n + 1)
                    pe.wait_ge(sums_copied[q], n)
                    for k in range(TPH):
                        for t in range(TPH):
                            last = nc.tensor.matmul(ps_s[q][:, k, :], same[q][:, t, k * P:(k + 1) * P],
                                                    eo[q][:, t, :], start=(t == 0), stop=(t == TPH - 1))
                    last.then_inc(sums_ready[q], 1)
                staggered(pe, [(0, outputs), (1, sum_up)], halves)

            @block.scalar
            def _(act):
                nc.scalar.preload_act_table_set(ACT_SET)

                def relu(h, n, q):
                    act.wait_ge(hid_loaded[q], n * 16 + 16)
                    act.wait_ge(out_ready[q], n)
                    nc.scalar.activation(act_hid[q][:], hid[q][:], ACT.Relu, bias=edge_affine[:, 5:6],
                                         scale=edge_affine[:, 4:5]).then_inc(relu_ready[q], 1)

                def copy_sums(h, n, q):
                    act.wait_ge(sums_ready[q], n + 1)
                    act.wait_ge(added[q], n * (TPH * 16))
                    nc.scalar.activation(sums[q][:], ps_s[q][:], ACT.Copy).then_inc(sums_copied[q], 1)
                staggered(act, [(0, relu), (2, copy_sums)], halves)

            @block.vector
            def _(dve):
                def compare(h, n, q):
                    dve.wait_ge(dst_loaded[q], n * 32 + 32)
                    dve.wait_ge(sums_ready[q], n)
                    same_destinations(same[q], drow[q], dcol[q]).then_inc(same_ready[q], 1)

                def add_bias(h, n, q):
                    dve.wait_ge(out_ready[q], n + 1)
                    nc.vector.tensor_tensor(eo[q][:], ps_o[q][:], b2a_rows[:].unsqueeze(1).broadcast_to([P, TPH, HID]),
                                            ALU.add).then_inc(out_copied[q], 1)

                def destinations(h, n, q):
                    dve.wait_ge(added[q], n * (TPH * 16))
                    nc.vector.tensor_copy(sidx[q][:], scatter_all[:, bass.ds(h * TPH, TPH)]
                                          ).then_inc(scatter_idx_ready[q], 1)
                staggered(dve, [(0, compare), (0, add_bias), (1, destinations)], halves)

        with Stage("node_hidden") as st:
            loaded, summed, agg_t = st.sems("loaded", WIDTH), st.sems("summed", WIDTH), st.sems("agg_t", WIDTH)
            hid_ready, stats_ready, stored = (st.sems("hid_ready", WIDTH), st.sems("stats_ready", WIDTH),
                                              st.sems("stored", WIDTH))
            even_copied, odd_copied, even_ready, odd_ready = (st.sem("even_copied"), st.sem("odd_copied"),
                                                              st.sem("even_ready"), st.sem("odd_ready"))
            affine_step = st.sem("affine_step")
            loads = 1 + TABLES

            xT = st.bufs("xT", [P, HROWS], width=WIDTH)
            part = [st.bufs(f"part{t}_", [P, TPG * HID], width=WIDTH) for t in range(TABLES)]
            agg = st.bufs("agg", [P, TPG, HID], width=WIDTH)
            aggT = st.bufs("aggT", [P, 2, HROWS], width=WIDTH)
            hid = st.bufs("hid", [P, 2, HROWS], width=WIDTH)
            stats = st.sb("stats", [P, 2 * groups_n, 6])
            even, odd = st.banks("even", [P, HROWS], WIDTH), st.banks("odd", [P, HROWS], WIDTH)
            assert TABLES == 2
            block = st.block()

            @block.sync
            def _(sp):
                def load(g, n, q):
                    sp.wait_ge(summed[q], n)
                    for t in range(TABLES):
                        sp.dma_start(part[t][q][:], pick(mlp_sums_g[t], g)).then_inc(loaded[q], 16)
                    sp.wait_ge(hid_ready[q], n)
                    sp.dma_start(xT[q][:], pick(x_mid_t, g)).then_inc(loaded[q], 16)
                over_groups(sp, [load])

            @block.gpsimd
            def _(pool):
                def total(g, n, q):
                    pool.wait_ge(loaded[q], n * (16 * loads) + 16 * loads)
                    pool.wait_ge(agg_t[q], n)
                    nc.gpsimd.tensor_tensor(agg[q][:].rearrange("p k c -> p (k c)"), part[0][q][:], part[1][q][:],
                                            ALU.add).then_inc(summed[q], 1)
                over_groups(pool, [total])

            @block.tensor
            def _(pe):
                def turn(g, n, q):
                    pe.wait_ge(summed[q], n + 1)
                    pe.wait_ge(stats_ready[q], n)
                    for j in range(TPG):
                        m = j // 2
                        last = nc.tensor.transpose((even, odd)[j % 2][q][:, m * P:(m + 1) * P], agg[q][:, j, :], ident)
                    last.then_inc(agg_t[q], 1)

                def hidden(g, n, q):
                    pe.wait_ge(loaded[q], n * (16 * loads) + 16 * loads)
                    pe.wait_ge(even_copied, g + 1)
                    nc.tensor.matmul(even[q][:], mlp("w1b_x_lo"), xT[q][:], start=True, stop=False)
                    nc.tensor.matmul(even[q][:], mlp("w1b_agg"), aggT[q][:, 0, :], start=False, stop=True)
                    pe.wait_ge(odd_copied, g + 1)
                    nc.tensor.matmul(odd[q][:], mlp("w1b_x_hi"), xT[q][:], start=True, stop=False)
                    nc.tensor.matmul(odd[q][:], mlp("w1b_agg"), aggT[q][:, 1, :], start=False, stop=True
                                     ).then_inc(hid_ready[q], 1)

                over_groups(pe, [turn, hidden])

            @block.scalar
            def _(act):
                nc.scalar.preload_act_table_set(ACT_SET)

                def copy_even(g, n, q):
                    act.wait_ge(agg_t[q], n + 1)
                    nc.scalar.activation(aggT[q][:, 0, :], even[q][:], ACT.Copy).then_inc(even_copied, 1)

                def bias_even(g, n, q):
                    act.wait_ge(hid_ready[q], n + 1)
                    act.wait_ge(stats_ready[q], n)
                    act.wait_ge(stored[q], n * 16)
                    nc.scalar.activation(hid[q][:, 0, :], even[q][:], ACT.Identity, bias=mlp_bias("b1b")
                                         ).then_inc(even_ready, 1)

                def store(g, n, q):
                    act.wait_ge(even_ready, g + 1)
                    act.wait_ge(odd_ready, g + 1)
                    act.dma_start(pick(node_hid, g), hid[q][:].rearrange("p s c -> p (s c)")).then_inc(stored[q], 16)

                over_groups(act, [copy_even, bias_even, store])
                for q in range(WIDTH):
                    act.wait_ge(stored[q], 16 * turns_of(q))
                bn_affine(None, act, stats, node_affine, affine_step, "g1b", "be1b")

            @block.vector
            def _(dve):
                def copy_odd(g, n, q):
                    dve.wait_ge(agg_t[q], n + 1)
                    nc.vector.tensor_copy(aggT[q][:, 1, :], odd[q][:]).then_inc(odd_copied, 1)

                def bias_odd(g, n, q):
                    dve.wait_ge(hid_ready[q], n + 1)
                    dve.wait_ge(stored[q], n * 16)
                    nc.vector.tensor_scalar(hid[q][:, 1, :], odd[q][:], mlp_bias("b1b"), None, ALU.add
                                            ).then_inc(odd_ready, 1)

                def statistics(g, n, q):
                    dve.wait_ge(even_ready, g + 1)
                    dve.wait_ge(odd_ready, g + 1)
                    dve.nop(nofuse=True)
                    for side in range(2):
                        last = nc.vector.bn_stats(
                            stats[:, bass.ds(g * 2 + side, 1), :].rearrange("p a c -> p (a c)"), hid[q][:, side, :])
                    last.then_inc(stats_ready[q], 1)

                over_groups(dve, [copy_odd, bias_odd, statistics])
                q_last = (groups_n - 1) % WIDTH
                left = n_nodes - (groups_n - 1) * ROWS
                assert left > 0 and left % TPG == 0
                for q in range(WIDTH):
                    dve.wait_ge(stats_ready[q], turns_of(q))
                for side in range(2):
                    last = nc.vector.bn_stats(stats[:, 2 * (groups_n - 1) + side, :],
                                              hid[q_last][:, side, :].rearrange("p (m c) -> p m c", c=P)
                                              [:, :, 0:left // TPG])
                last.then_inc(stats_ready[q_last], 1)
                dve.wait_ge(stats_ready[q_last], turns_of(q_last) + 1)
                bn_affine(dve, None, stats, node_affine, affine_step, "g1b", "be1b")

        with Stage("output") as st:
            loaded, relu_ready, out_ready = (st.sems("loaded", WIDE), st.sems("relu_ready", WIDE),
                                             st.sems("out_ready", WIDE))
            bias_ready, y_ready, stored = (st.sems("bias_ready", WIDE), st.sems("y_ready", WIDE),
                                           st.sems("stored", WIDE))
            total_ready, mean_ready, cen_ready, sq_ready, var_ready, log_ready, rstd_ready, res_ready = (
                st.sem(name) for name in ("total_ready", "mean_ready", "cen_ready", "sq_ready", "var_ready",
                                          "log_ready", "rstd_ready", "res_ready"))

            def bufs(name, *shape):
                return st.bufs(name, [P, *shape], width=WIDE)

            xrow, xb, y, cen, sq, res = (bufs(name, TPG, D) for name in ("xrow", "xb", "y", "cen", "sq", "res"))
            hid, act_hid = bufs("hid", 2, HROWS), bufs("act_hid", 2, HROWS)
            total, mean, var, log, rstd = (bufs(name, TPG) for name in ("total", "mean", "var", "log", "rstd"))
            ps = st.banks("ps_y", [P, TPG, D], WIDE)
            block = st.block()

            @block.sync
            def _(sp):
                def load(g, n, q):
                    sp.wait_ge(relu_ready[q], n)
                    sp.dma_start(hid[q][:].rearrange("p s c -> p (s c)"), pick(node_hid, g)).then_inc(loaded[q], 16)
                    sp.wait_ge(bias_ready[q], n)
                    sp.dma_start(xrow[q][:].rearrange("p k c -> p (k c)"), pick(x_mid_g, g)).then_inc(loaded[q], 16)
                over_groups(sp, [load], width=WIDE)

            @block.gpsimd
            def _(pool):
                def bias(g, n, q):
                    pool.wait_ge(loaded[q], n * 32 + 32)
                    pool.wait_ge(y_ready[q], n)
                    nc.gpsimd.tensor_tensor(xb[q][:], xrow[q][:], b2b_rows[:].unsqueeze(1).broadcast_to([P, TPG, D]),
                                            ALU.add).then_inc(bias_ready[q], 1)
                over_groups(pool, [bias], width=WIDE)

            @block.tensor
            def _(pe):
                def product(g, n, q):
                    pe.wait_ge(relu_ready[q], n + 1)
                    pe.wait_ge(y_ready[q], n)
                    for j in range(TPG):
                        m = j // 2
                        last = nc.tensor.matmul(ps[q][:, j, :], act_hid[q][:, j % 2, m * P:(m + 1) * P], mlp("w2b"),
                                                start=True, stop=True)
                    last.then_inc(out_ready[q], 1)
                over_groups(pe, [product], width=WIDE)

            @block.scalar
            def _(act):
                nc.scalar.preload_act_table_set(ACT_SET)

                def relu(g, n, q):
                    act.wait_ge(loaded[q], n * 32 + 32)
                    act.wait_ge(out_ready[q], n)
                    nc.scalar.activation(act_hid[q][:], hid[q][:], ACT.Relu, bias=node_affine[:, 5:6],
                                         scale=node_affine[:, 4:5]).then_inc(relu_ready[q], 1)

                def square(g, n, q):
                    act.wait_ge(cen_ready, g + 1)
                    nc.scalar.activation(sq[q][:], cen[q][:], ACT.Square).then_inc(sq_ready, 1)

                def logarithm(g, n, q):
                    act.wait_ge(var_ready, g + 1)
                    nc.scalar.activation(log[q][:], var[q][:], ACT.Ln, bias=eps_col[:, 0:1], scale=1.0 / D
                                         ).then_inc(log_ready, 1)

                def inverse_root(g, n, q):
                    act.wait_ge(log_ready, g + 1)
                    nc.scalar.activation(rstd[q][:], log[q][:], ACT.Exp, scale=-0.5).then_inc(rstd_ready, 1)

                def store(g, n, q):
                    act.wait_ge(res_ready, g + 1)
                    act.dma_start(pick(out_g, g), res[q][:].rearrange("p k c -> p (k c)")).then_inc(stored[q], 16)
                over_groups(act, [("ahead", relu), square, (logarithm, inverse_root), store], width=WIDE)
                for q in range(WIDE):
                    act.wait_ge(stored[q], 16 * turns_of(q, width=WIDE))

            @block.vector
            def _(dve):
                def center_rows(g, n, q):
                    dve.wait_ge(out_ready[q], n + 1)
                    dve.wait_ge(bias_ready[q], n + 1)
                    nc.vector.tensor_tensor(y[q][:], ps[q][:], xb[q][:], ALU.add).then_inc(y_ready[q], 1)
                    dve.wait_ge(y_ready[q], n + 1)
                    nc.vector.tensor_reduce(total[q][:], y[q][:], AX.X, ALU.add).then_inc(total_ready, 1)
                    dve.wait_ge(total_ready, g + 1)
                    nc.vector.tensor_scalar(mean[q][:], total[q][:], 1.0 / D, None, ALU.mult).then_inc(mean_ready, 1)
                    dve.wait_ge(mean_ready, g + 1)
                    nc.vector.tensor_tensor(cen[q][:], y[q][:], mean[q][:].unsqueeze(2).broadcast_to([P, TPG, D]),
                                            ALU.subtract).then_inc(cen_ready, 1)

                def variance(g, n, q):
                    dve.wait_ge(sq_ready, g + 1)
                    nc.vector.tensor_reduce(var[q][:], sq[q][:], AX.X, ALU.add).then_inc(var_ready, 1)

                def scale(g, n, q):
                    dve.wait_ge(rstd_ready, g + 1)
                    dve.wait_ge(stored[q], n * 16)
                    nc.vector.tensor_tensor(res[q][:], cen[q][:], rstd[q][:].unsqueeze(2).broadcast_to([P, TPG, D]),
                                            ALU.mult).then_inc(res_ready, 1)
                over_groups(dve, [center_rows, variance, scale], width=WIDE)


def _round(n, k):
    return (n + k - 1) // k * k


def host_arrays(inp):
    f = {k: np.asarray(v) for k, v in inp.items()}
    n, e = f["x"].shape[0], f["src"].shape[0]
    n_pad, e_pad = _round(n, ROWS), _round(e, ROWS)
    if n_pad == n:
        n_pad += ROWS
    halves = e_pad // HROWS
    x = np.zeros((n_pad, D), np.float32)
    x[:n] = f["x"]
    x_t = np.ascontiguousarray(x.reshape(-1, P, TPH, 2, D).transpose(0, 3, 4, 2, 1)).reshape(-1, P, HROWS)
    ea_t = np.zeros((D, e_pad), np.float32)
    ea_t[:, :e] = f["edge_attr_64"].T
    src = np.full(e_pad, n_pad - 1, np.int32)
    dst = np.full(e_pad, n_pad - 1, np.int32)
    src[:e], dst[:e] = f["src"], f["dst"]
    src_c = src.reshape(halves, TPH, P).transpose(0, 2, 1)
    dst_c = dst.reshape(halves, TPH, P).transpose(0, 2, 1)

    consts = np.zeros((P, N_CONSTS), np.float32)
    eye, pair = np.eye(P, dtype=np.float32), np.kron(np.eye(2), np.ones((D, D))).astype(np.float32) / D
    consts[:, 0:P], consts[:, P:2 * P], consts[:, 2 * P:3 * P] = eye, eye - pair, pair
    edge = np.arange(HROWS)
    earlier = (edge[None, :] < edge[:, None]).astype(np.float32)
    a, width = CONSTS["earlier"]
    consts[:, a:a + width] = earlier.reshape(TPH, P, HROWS).transpose(1, 0, 2).reshape(P, width)
    a, width = CONSTS["spare"]
    consts[:, a:a + width] = n_pad + edge.reshape(TPH, P).T

    layer_w = np.zeros((P, LAYERS, N_LAYER_W), np.float32)
    layer_b = np.zeros((P, LAYERS, len(LAYER_B)), np.float32)
    for l in range(LAYERS):
        w = {k: f[f"L0_gnn_{k}"][l] for k in ("WK", "WV", "WQ", "WE", "WO", "W1", "W2", "bO", "ln1_g", "ln1_b", "b1",
                                              "b2", "ln2_g", "ln2_b")}
        lw = layer_w[:, l]
        lw[:D, 0:D], lw[:D, D:2 * D], lw[D:, 2 * D:3 * D], lw[:D, 3 * D:4 * D] = w["WK"], w["WV"], w["WQ"], w["WE"]
        for r in range(2):
            lw[r * D:(r + 1) * D, 256 + r * D:256 + (r + 1) * D] = w["WO"].T
            lw[r * D:(r + 1) * D, 384 + r * P:384 + (r + 1) * P] = w["W1"]
            lw[r * D:(r + 1) * D, 640 + r * P:640 + (r + 1) * P] = w["W2"].T
        for k, name in enumerate(("bO", "ln1_g", "ln1_b", "b1", "b2", "ln2_g", "ln2_b")):
            layer_b[:, l, k] = w[name] if w[name].size == P else np.concatenate([w[name], w[name]])

    g = {k: f[f"L1_gnn_{k}"] for k in ("W1a", "b1a", "g1a", "be1a", "W2a", "b2a", "W1b", "b1b", "g1b", "be1b", "W2b",
                                       "b2b")}
    mlp_w = np.zeros((P, N_MLP_W), np.float32)
    mlp_w[:, 0:P], mlp_w[:, P:2 * P] = g["W1a"], g["W2a"]
    mlp_w[:D, 2 * P:3 * P], mlp_w[D:, 3 * P:4 * P] = g["W1b"][:D], g["W1b"][:D]
    mlp_w[:, 4 * P:5 * P], mlp_w[:, 5 * P:] = g["W1b"][D:], g["W2b"]
    mlp_b = np.stack([g[k] for k in MLP_B], axis=1)
    mlp_rows = np.zeros((2, HID), np.float32)
    mlp_rows[0], mlp_rows[1, :D] = g["b2a"], g["b2b"]
    return dict(x=x, x_t=x_t, ea_t=ea_t, gather_idx=np.ascontiguousarray(np.concatenate([src_c, dst_c], axis=2)),
                dst_row=dst.reshape(halves, HROWS), dst_col=np.ascontiguousarray(dst_c), consts=consts,
                layer_w=layer_w, layer_b=layer_b, mlp_w=mlp_w, mlp_b=np.ascontiguousarray(mlp_b), mlp_rows=mlp_rows)


def kernel(**inputs):
    import concourse.bacc as bacc
    from concourse.bass_utils import run_bass_kernel_spmd

    n, e = inputs["x"].shape[0], inputs["src"].shape[0]
    arrays = host_arrays(inputs)
    nc = bacc.Bacc("TRN2", target_bir_lowering=False, num_devices=1)
    args = {k: nc.dram_tensor(f"in_{k}", a.shape, mybir.dt.from_np(a.dtype), kind="ExternalInput").ap()
            for k, a in arrays.items()}
    out = nc.dram_tensor("out_nodes", arrays["x"].shape, F32, kind="ExternalOutput").ap()
    build(nc, n, e, *args.values(), out)
    r = run_bass_kernel_spmd(nc, [{f"in_{k}": a for k, a in arrays.items()}], core_ids=[0])
    return r.results[0]["out_nodes"][:n]
```
